# Optimizing a Trainium2 kernel written in Bass

```python
import numpy as np
import jax
import jax.numpy as jnp

def _softmax(x, axis=-1):
    return jax.nn.softmax(x, axis=axis)

def _gelu(x):
    return jax.nn.gelu(x, approximate=True)

def _silu(x):
    return jax.nn.silu(x)

def _sigmoid(x):
    return jax.nn.sigmoid(x)

def _layernorm(x, axis=-1, eps=1e-05):
    m = jnp.mean(x, axis=axis, keepdims=True)
    v = jnp.var(x, axis=axis, keepdims=True)
    return (x - m) / jnp.sqrt(v + eps)

def _scatter_add(tgt, idx, src, axis=0):
    return tgt.at[idx].add(src)

def _segment_sum(src, seg, n):
    return jax.ops.segment_sum(src, seg, n)
kernel_name = 'mk_flamingo_gated_d4_seqx_r8_6dfb48'

def setup_inputs(seed: int=0):
    np.random.seed(seed)
    _w = jnp.asarray

    def _rec_inputs():
        import jax
        import jax.numpy as jnp
        _rk = jax.random.key(seed)
        x = 7.22e-05 + 1 * jax.random.normal(jax.random.fold_in(_rk, 1), (4, 512, 128), jnp.float32)
        _lenS = 512 - jax.random.randint(jax.random.fold_in(_rk, 7), (4,), 0, max(1, 512 // 4) + 1, jnp.int32)
        _lenS2 = 77 - jax.random.randint(jax.random.fold_in(_rk, 8), (4,), 0, max(1, 77 // 4) + 1, jnp.int32)
        _ctx_1024P = jax.random.normal(jax.random.fold_in(_rk, 11), (4, 16, 128), jnp.float32)
        _ctx_1024c = jax.random.dirichlet(jax.random.fold_in(_rk, 511), 0.3 * jnp.ones((16,), jnp.float32), (4, 77))
        _ctx_1024t = jnp.einsum('bsk,bkd->bsd', _ctx_1024c, _ctx_1024P)
        _ctx_1024t = _ctx_1024t * jax.lax.rsqrt(jnp.mean(jnp.square(_ctx_1024t)) + 1e-12) * 0.953939
        ctx_1024 = 2.81802e-05 + 1.00001 * (_ctx_1024t + 0.3 * jax.random.normal(jax.random.fold_in(_rk, 611), (4, 77, 128), jnp.float32))
        _validS = jnp.arange(512)[None, :] < _lenS[:, None]
        _validS2 = jnp.arange(77)[None, :] < _lenS2[:, None]
        _causal = jnp.tril(jnp.ones((512, 512), dtype=bool))
        mask_Bx1xSxS2_if1 = jnp.where(jnp.ones((4, 1, 512, 77), dtype=bool), 1, 0).astype(jnp.int32)
        mask_BxS2_bk0 = jnp.logical_not(jnp.broadcast_to(_validS2[:, :], (4, 77)))
        _g = jax.random.normal(jax.random.fold_in(_rk, 9001), (2, 4), jnp.float32)
        _g = jnp.sign(_g) * jnp.maximum(jnp.abs(_g), 1.0) + (_g == 0) * 1.0
        g_xattn = _g[0]
        g_ffn = _g[1]
        return (x, ctx_1024, mask_Bx1xSxS2_if1, mask_BxS2_bk0, g_xattn, g_ffn)
    x, ctx_1024, mask_Bx1xSxS2_if1, mask_BxS2_bk0, g_xattn, g_ffn = _rec_inputs()

    def _L0_xattn_setup():
        import jax, jax.numpy as jnp
        import numpy as np
        B, NT, NM, C, H, FF = (8, 128, 256, 128, 8, 512)

        def _ln(x, g, b):
            m = x.mean(-1, keepdims=True)
            v = jnp.mean((x - m) ** 2, axis=-1, keepdims=True)
            return (x - m) / jnp.sqrt(v + 1e-05) * g + b
        key = jax.random.key(seed)
        ks = jax.random.split(key, 8)
        w = lambda k, shape, s=0.02: jax.random.normal(k, shape, dtype=jnp.float32) * s
        return {'tgt': jax.random.normal(ks[0], (B, NT, C), dtype=jnp.float32), 'memory': jax.random.normal(ks[1], (B, NM, C), dtype=jnp.float32), 'qkv_w': w(ks[2], (3 * C, C)), 'qkv_b': jnp.zeros((3 * C,), jnp.float32), 'sa_out_w': w(ks[3], (C, C)), 'sa_out_b': jnp.zeros((C,), jnp.float32), 'in_proj_w': w(ks[4], (3 * C, C)), 'in_proj_b': jnp.zeros((3 * C,), jnp.float32), 'mha_out_w': w(ks[5], (C, C)), 'mha_out_b': jnp.zeros((C,), jnp.float32), 'lin1_w': w(ks[6], (FF, C)), 'lin1_b': jnp.zeros((FF,), jnp.float32), 'lin2_w': w(ks[7], (C, FF)), 'lin2_b': jnp.zeros((C,), jnp.float32), 'ln1_g': jnp.ones((C,), jnp.float32), 'ln1_b': jnp.zeros((C,), jnp.float32), 'ln2_g': jnp.ones((C,), jnp.float32), 'ln2_b': jnp.zeros((C,), jnp.float32), 'ln3_g': jnp.ones((C,), jnp.float32), 'ln3_b': jnp.zeros((C,), jnp.float32)}
    _L0_xattn_all = _L0_xattn_setup()
    _L0_xattn_in = {k: v for k, v in _L0_xattn_all.items() if k in ('qkv_w', 'qkv_b', 'sa_out_w', 'sa_out_b', 'in_proj_w', 'in_proj_b', 'mha_out_w', 'mha_out_b', 'lin1_w', 'lin1_b', 'lin2_w', 'lin2_b', 'ln1_g', 'ln1_b', 'ln2_g', 'ln2_b', 'ln3_g', 'ln3_b')}
    del _L0_xattn_all

    def _L0_ffn_setup():
        import jax, jax.numpy as jnp
        import numpy as np
        DIM = 128
        E = 16
        TOPK = 2
        G = 4
        TOPK_G = 2
        INTER = 64
        N_SHARED = 2
        ROUTE_SCALE = 1.0

        def _gate(xf, gate_w, gate_b):
            scores = xf @ gate_w.T
            scores = jax.nn.softmax(scores.astype(jnp.float32), axis=-1)
            orig = scores
            scores = scores + gate_b
            T = xf.shape[0]
            sg = scores.reshape(T, G, E // G)
            group_scores = jax.lax.top_k(sg, 2)[0].sum(-1)
            _, gidx = jax.lax.top_k(group_scores, TOPK_G)
            keep = jax.nn.one_hot(gidx, G).sum(axis=1) > 0
            sg = jnp.where(keep[:, :, None], sg, -jnp.inf)
            scores = sg.reshape(T, E)
            _, idx = jax.lax.top_k(scores, TOPK)
            weights = jnp.take_along_axis(orig, idx, axis=1)
            weights = (weights * ROUTE_SCALE).astype(xf.dtype)
            return (weights, idx)
        key = jax.random.key(seed)
        ks = jax.random.split(key, 16)
        s = lambda fan_in: 1.0 / np.sqrt(fan_in)
        inp = {'x': jax.random.normal(ks[0], (4, 128, DIM), dtype=jnp.float32), 'gate_w': jax.random.normal(ks[1], (E, DIM), dtype=jnp.float32) * s(DIM), 'gate_b': jnp.zeros((E,), dtype=jnp.float32), 'We1': jax.random.normal(ks[2], (E, DIM, INTER), dtype=jnp.float32) * s(DIM), 'be1': jnp.zeros((E, INTER), dtype=jnp.float32), 'We2': jax.random.normal(ks[3], (E, INTER, DIM), dtype=jnp.float32) * s(INTER), 'be2': jnp.zeros((E, DIM), dtype=jnp.float32), 'We3': jax.random.normal(ks[4], (E, DIM, INTER), dtype=jnp.float32) * s(DIM), 'be3': jnp.zeros((E, INTER), dtype=jnp.float32), 'ws1': jax.random.normal(ks[5], (DIM, N_SHARED * INTER), dtype=jnp.float32) * s(DIM), 'bs1': jnp.zeros((N_SHARED * INTER,), dtype=jnp.float32), 'ws2': jax.random.normal(ks[6], (N_SHARED * INTER, DIM), dtype=jnp.float32) * s(N_SHARED * INTER), 'bs2': jnp.zeros((DIM,), dtype=jnp.float32), 'ws3': jax.random.normal(ks[7], (DIM, N_SHARED * INTER), dtype=jnp.float32) * s(DIM), 'bs3': jnp.zeros((N_SHARED * INTER,), dtype=jnp.float32)}
        return inp
    _L0_ffn_all = _L0_ffn_setup()
    _L0_ffn_in = {k: v for k, v in _L0_ffn_all.items() if k in ('gate_w', 'gate_b', 'We1', 'be1', 'We2', 'be2', 'We3', 'be3', 'ws1', 'bs1', 'ws2', 'bs2', 'ws3', 'bs3')}
    del _L0_ffn_all

    def _L1_xattn_setup():
        import jax, jax.numpy as jnp
        import numpy as np
        HEADS = 16
        key = jax.random.key(seed)
        ks = jax.random.split(key, 8)
        N, S, E = (2, 256, 128)
        D = E // HEADS
        return {'values': jax.random.normal(ks[0], (N, S, E), jnp.float32), 'keys': jax.random.normal(ks[1], (N, S, E), jnp.float32), 'queries': jax.random.normal(ks[2], (N, S, E), jnp.float32), 'mask': jnp.ones((N, 1, S, S), jnp.int32), 'Wv': jax.random.normal(ks[3], (D, D), jnp.float32) * D ** (-0.5), 'Wk': jax.random.normal(ks[4], (D, D), jnp.float32) * D ** (-0.5), 'Wq': jax.random.normal(ks[5], (D, D), jnp.float32) * D ** (-0.5), 'Wo': jax.random.normal(ks[6], (E, E), jnp.float32) * E ** (-0.5), 'bo': jnp.zeros((E,), jnp.float32)}
    _L1_xattn_all = _L1_xattn_setup()
    _L1_xattn_in = {k: v for k, v in _L1_xattn_all.items() if k in ('Wv', 'Wk', 'Wq', 'Wo', 'bo')}
    del _L1_xattn_all

    def _L1_ffn_setup():
        import math
        import jax, jax.numpy as jnp
        import numpy as np
        B, L, D, FF, E, K = (4, 256, 128, 512, 8, 2)
        CAPACITY_FACTOR = 1.25
        T = B * L
        CAP = math.ceil(CAPACITY_FACTOR * T * K / E)
        key = jax.random.key(seed)
        ks = jax.random.split(key, 7)
        return {'h': jax.random.normal(ks[0], (B, L, D), dtype=jnp.float32), 'gate_w': 0.02 * jax.random.normal(ks[1], (E, D), dtype=jnp.float32), 'gate_b': jnp.zeros((E,), dtype=jnp.float32), 'W1': 0.02 * jax.random.normal(ks[2], (E, D, FF), dtype=jnp.float32), 'b1': jnp.zeros((E, FF), dtype=jnp.float32), 'W2': 0.02 * jax.random.normal(ks[3], (E, FF, D), dtype=jnp.float32), 'b2': jnp.zeros((E, D), dtype=jnp.float32)}
    _L1_ffn_all = _L1_ffn_setup()
    _L1_ffn_in = {k: v for k, v in _L1_ffn_all.items() if k in ('gate_w', 'gate_b', 'W1', 'b1', 'W2', 'b2')}
    del _L1_ffn_all

    def _L2_xattn_setup():
        import jax, jax.numpy as jnp
        import numpy as np
        DIM, DIM_HEAD, HEADS, SCALE = (128, 64, 8, 8.0)
        INNER = DIM_HEAD * HEADS
        LN_EPS = 1e-05
        L2_EPS = 1e-12

        def layer_norm(x, w, b):
            mu = jnp.mean(x, axis=-1, keepdims=True)
            var = jnp.mean(jnp.square(x - mu), axis=-1, keepdims=True)
            return (x - mu) * jax.lax.rsqrt(var + LN_EPS) * w + b

        def l2norm(t):
            n = jnp.sqrt(jnp.sum(jnp.square(t), axis=-1, keepdims=True))
            return t / jnp.maximum(n, L2_EPS)
        key = jax.random.key(seed)
        ks = jax.random.split(key, 8)
        b, n, m = (8, 1024, 64)
        x = jax.random.normal(ks[0], (b, n, DIM), dtype=jnp.float32)
        latents = jax.random.normal(ks[1], (b, m, DIM), dtype=jnp.float32)
        mask = jax.random.randint(ks[2], (b, n), 0, 2) > 0
        Wq = jax.random.normal(ks[3], (DIM, INNER), dtype=jnp.float32) * DIM ** (-0.5)
        Wkv = jax.random.normal(ks[4], (DIM, 2 * INNER), dtype=jnp.float32) * DIM ** (-0.5)
        Wo = jax.random.normal(ks[5], (INNER, DIM), dtype=jnp.float32) * INNER ** (-0.5)
        return {'x': x, 'latents': latents, 'mask': mask, 'ln_x_w': jnp.ones((DIM,)), 'ln_x_b': jnp.zeros((DIM,)), 'ln_l_w': jnp.ones((DIM,)), 'ln_l_b': jnp.zeros((DIM,)), 'Wq': Wq, 'Wkv': Wkv, 'q_scale': jnp.ones((DIM_HEAD,)), 'k_scale': jnp.ones((DIM_HEAD,)), 'Wo': Wo, 'ln_o_w': jnp.ones((DIM,)), 'ln_o_b': jnp.zeros((DIM,))}
    _L2_xattn_all = _L2_xattn_setup()
    _L2_xattn_in = {k: v for k, v in _L2_xattn_all.items() if k in ('ln_x_w', 'ln_x_b', 'ln_l_w', 'ln_l_b', 'Wq', 'Wkv', 'q_scale', 'k_scale', 'Wo', 'ln_o_w', 'ln_o_b')}
    del _L2_xattn_all

    def _L2_ffn_setup():
        import jax, jax.numpy as jnp
        import numpy as np
        TOP_K = 2
        NUM_EXPERTS = 8
        DIM = 128
        HIDDEN = 352
        BS, SLEN = (2, 128)

        def _grouped_ffn(x, w1, w2, w3, counts):
            num_experts = w1.shape[0]
            ends = jnp.cumsum(counts)
            starts = ends - counts
            t = jnp.arange(x.shape[0])
            out = jnp.zeros((x.shape[0], w2.shape[-1]), x.dtype)
            for e in range(num_experts):
                m = ((t >= starts[e]) & (t < ends[e])).astype(x.dtype)[:, None]
                xe = x * m
                h = jax.nn.silu(xe @ w1[e]) * (xe @ w3[e])
                out = out + h @ w2[e] * m
            return out
        key = jax.random.key(seed)
        k = jax.random.split(key, 5)
        std = 0.02
        return {'x': jax.random.normal(k[0], (BS, SLEN, DIM), jnp.float32), 'gate_w': jax.random.normal(k[1], (NUM_EXPERTS, DIM), jnp.float32) * std, 'expert_bias': jnp.zeros((NUM_EXPERTS,), jnp.float32), 'w1': jax.random.normal(k[2], (NUM_EXPERTS, DIM, HIDDEN), jnp.float32) * std, 'w2': jax.random.normal(k[3], (NUM_EXPERTS, HIDDEN, DIM), jnp.float32) * std, 'w3': jax.random.normal(k[4], (NUM_EXPERTS, DIM, HIDDEN), jnp.float32) * std}
    _L2_ffn_all = _L2_ffn_setup()
    _L2_ffn_in = {k: v for k, v in _L2_ffn_all.items() if k in ('gate_w', 'expert_bias', 'w1', 'w2', 'w3')}
    del _L2_ffn_all

    def _L3_xattn_setup():
        import jax, jax.numpy as jnp
        import numpy as np
        E = 128
        NUM_HEADS = 16
        DK = E // NUM_HEADS
        EPS = 1e-05
        NEG_INF = -jnp.inf

        def layer_norm(x, g, b):
            mu = jnp.mean(x, axis=-1, keepdims=True)
            var = jnp.var(x, axis=-1, keepdims=True)
            return (x - mu) * jax.lax.rsqrt(var + EPS) * g + b

        def self_attn(x, Wq, Wk, Wv):
            Q, K, V = (x @ Wq, x @ Wk, x @ Wv)
            energy = jnp.einsum('bqd,bkd->bqk', Q, K)
            S = energy.shape[-1]
            lengths = jnp.sum(energy[:, 0] != 0, axis=-1)
            kidx = jnp.arange(S)
            pad = kidx[None, None, :] >= lengths[:, None, None]
            causal = kidx[None, :] < kidx[:, None]
            causal = (kidx[None, :] > kidx[:, None])[None]
            energy = jnp.where(pad | causal, NEG_INF, energy)
            score = jax.nn.softmax(energy / np.sqrt(DK), axis=-1)
            return jnp.einsum('bqk,bkd->bqd', score, V)

        def cross_attn(x, context, Wq, Wk, Wv):
            Q = x @ Wq
            K, V = (context @ Wk, context @ Wv)
            energy = jnp.einsum('bqd,bkd->bqk', Q, K)
            Sk = energy.shape[-1]
            lengths = jnp.sum(energy[:, 0] != 0, axis=-1)
            kidx = jnp.arange(Sk)
            pad = kidx[None, None, :] >= lengths[:, None, None]
            energy = jnp.where(pad, NEG_INF, energy)
            score = jax.nn.softmax(energy / np.sqrt(DK), axis=-1)
            return jnp.einsum('bqk,bkd->bqd', score, V)
        key = jax.random.key(seed)
        ks = jax.random.split(key, 12)
        B, S = (8, 256)
        s = 1.0 / np.sqrt(E)
        inp = {'x': jax.random.normal(ks[0], (B, S, E), jnp.float32), 'context': jax.random.normal(ks[1], (B, S, E), jnp.float32), 'Wq1': jax.random.normal(ks[2], (E, E), jnp.float32) * s, 'Wk1': jax.random.normal(ks[3], (E, E), jnp.float32) * s, 'Wv1': jax.random.normal(ks[4], (E, E), jnp.float32) * s, 'Wq2': jax.random.normal(ks[5], (E, E), jnp.float32) * s, 'Wk2': jax.random.normal(ks[6], (E, E), jnp.float32) * s, 'Wv2': jax.random.normal(ks[7], (E, E), jnp.float32) * s, 'fc1_w': jax.random.normal(ks[8], (E, E), jnp.float32) * s, 'fc1_b': jnp.zeros((E,), jnp.float32), 'fc2_w': jax.random.normal(ks[9], (E, E), jnp.float32) * s, 'fc2_b': jnp.zeros((E,), jnp.float32), 'ln1_g': jnp.ones((E,), jnp.float32), 'ln1_b': jnp.zeros((E,), jnp.float32), 'ln2_g': jnp.ones((E,), jnp.float32), 'ln2_b': jnp.zeros((E,), jnp.float32), 'ln3_g': jnp.ones((E,), jnp.float32), 'ln3_b': jnp.zeros((E,), jnp.float32)}
        return inp
    _L3_xattn_all = _L3_xattn_setup()
    _L3_xattn_in = {k: v for k, v in _L3_xattn_all.items() if k in ('Wq1', 'Wk1', 'Wv1', 'Wq2', 'Wk2', 'Wv2', 'fc1_w', 'fc1_b', 'fc2_w', 'fc2_b', 'ln1_g', 'ln1_b', 'ln2_g', 'ln2_b', 'ln3_g', 'ln3_b')}
    del _L3_xattn_all

    def _L3_ffn_setup():
        import jax, jax.numpy as jnp
        import numpy as np
        BITS = 8
        LORA_RANK = 16
        LORA_ALPHA = 32
        SCALING = LORA_ALPHA / LORA_RANK

        def fake_quant_weight(w, bits=BITS):
            qmax = 2.0 ** (bits - 1) - 1
            scale = jnp.max(jnp.abs(w)) / qmax
            wq = jnp.clip(jnp.round(w / scale), -qmax - 1, qmax) * scale
            return w + jax.lax.stop_gradient(wq - w)

        def qat_lora_linear(x, W, b, A, B):
            Wq = fake_quant_weight(W)
            base = jnp.einsum('bsi,oi->bso', x, Wq) + b
            lora = jnp.einsum('bsr,or->bso', jnp.einsum('bsi,ri->bsr', x, A), B)
            return base + SCALING * lora
        key = jax.random.key(seed)
        ks = jax.random.split(key, 9)
        d, f = (128, 512)
        s_in = 1.0 / np.sqrt(d)
        s_ff = 1.0 / np.sqrt(f)
        return {'hidden_states': jax.random.normal(ks[0], (4, 256, d), jnp.float32), 'W_fc': jax.random.normal(ks[1], (f, d), jnp.float32) * s_in, 'b_fc': jnp.zeros((f,), jnp.float32), 'A_fc': jax.random.normal(ks[2], (LORA_RANK, d), jnp.float32) * s_in, 'B_fc': jnp.zeros((f, LORA_RANK), jnp.float32), 'W_proj': jax.random.normal(ks[3], (d, f), jnp.float32) * s_ff, 'b_proj': jnp.zeros((d,), jnp.float32), 'A_proj': jax.random.normal(ks[4], (LORA_RANK, f), jnp.float32) * s_ff, 'B_proj': jnp.zeros((d, LORA_RANK), jnp.float32)}
    _L3_ffn_all = _L3_ffn_setup()
    _L3_ffn_in = {k: v for k, v in _L3_ffn_all.items() if k in ('W_fc', 'b_fc', 'A_fc', 'B_fc', 'W_proj', 'b_proj', 'A_proj', 'B_proj')}
    del _L3_ffn_all
    return {'x': x, 'ctx_1024': ctx_1024, 'mask_Bx1xSxS2_if1': mask_Bx1xSxS2_if1, 'mask_BxS2_bk0': mask_BxS2_bk0, 'g_xattn': g_xattn, 'g_ffn': g_ffn, 'L0_xattn_qkv_w': _L0_xattn_in['qkv_w'], 'L0_xattn_qkv_b': _L0_xattn_in['qkv_b'], 'L0_xattn_sa_out_w': _L0_xattn_in['sa_out_w'], 'L0_xattn_sa_out_b': _L0_xattn_in['sa_out_b'], 'L0_xattn_in_proj_w': _L0_xattn_in['in_proj_w'], 'L0_xattn_in_proj_b': _L0_xattn_in['in_proj_b'], 'L0_xattn_mha_out_w': _L0_xattn_in['mha_out_w'], 'L0_xattn_mha_out_b': _L0_xattn_in['mha_out_b'], 'L0_xattn_lin1_w': _L0_xattn_in['lin1_w'], 'L0_xattn_lin1_b': _L0_xattn_in['lin1_b'], 'L0_xattn_lin2_w': _L0_xattn_in['lin2_w'], 'L0_xattn_lin2_b': _L0_xattn_in['lin2_b'], 'L0_xattn_ln1_g': _L0_xattn_in['ln1_g'], 'L0_xattn_ln1_b': _L0_xattn_in['ln1_b'], 'L0_xattn_ln2_g': _L0_xattn_in['ln2_g'], 'L0_xattn_ln2_b': _L0_xattn_in['ln2_b'], 'L0_xattn_ln3_g': _L0_xattn_in['ln3_g'], 'L0_xattn_ln3_b': _L0_xattn_in['ln3_b'], 'L0_ffn_gate_w': _L0_ffn_in['gate_w'], 'L0_ffn_gate_b': _L0_ffn_in['gate_b'], 'L0_ffn_We1': _L0_ffn_in['We1'], 'L0_ffn_be1': _L0_ffn_in['be1'], 'L0_ffn_We2': _L0_ffn_in['We2'], 'L0_ffn_be2': _L0_ffn_in['be2'], 'L0_ffn_We3': _L0_ffn_in['We3'], 'L0_ffn_be3': _L0_ffn_in['be3'], 'L0_ffn_ws1': _L0_ffn_in['ws1'], 'L0_ffn_bs1': _L0_ffn_in['bs1'], 'L0_ffn_ws2': _L0_ffn_in['ws2'], 'L0_ffn_bs2': _L0_ffn_in['bs2'], 'L0_ffn_ws3': _L0_ffn_in['ws3'], 'L0_ffn_bs3': _L0_ffn_in['bs3'], 'L1_xattn_Wv': _L1_xattn_in['Wv'], 'L1_xattn_Wk': _L1_xattn_in['Wk'], 'L1_xattn_Wq': _L1_xattn_in['Wq'], 'L1_xattn_Wo': _L1_xattn_in['Wo'], 'L1_xattn_bo': _L1_xattn_in['bo'], 'L1_ffn_gate_w': _L1_ffn_in['gate_w'], 'L1_ffn_gate_b': _L1_ffn_in['gate_b'], 'L1_ffn_W1': _L1_ffn_in['W1'], 'L1_ffn_b1': _L1_ffn_in['b1'], 'L1_ffn_W2': _L1_ffn_in['W2'], 'L1_ffn_b2': _L1_ffn_in['b2'], 'L2_xattn_ln_x_w': _L2_xattn_in['ln_x_w'], 'L2_xattn_ln_x_b': _L2_xattn_in['ln_x_b'], 'L2_xattn_ln_l_w': _L2_xattn_in['ln_l_w'], 'L2_xattn_ln_l_b': _L2_xattn_in['ln_l_b'], 'L2_xattn_Wq': _L2_xattn_in['Wq'], 'L2_xattn_Wkv': _L2_xattn_in['Wkv'], 'L2_xattn_q_scale': _L2_xattn_in['q_scale'], 'L2_xattn_k_scale': _L2_xattn_in['k_scale'], 'L2_xattn_Wo': _L2_xattn_in['Wo'], 'L2_xattn_ln_o_w': _L2_xattn_in['ln_o_w'], 'L2_xattn_ln_o_b': _L2_xattn_in['ln_o_b'], 'L2_ffn_gate_w': _L2_ffn_in['gate_w'], 'L2_ffn_expert_bias': _L2_ffn_in['expert_bias'], 'L2_ffn_w1': _L2_ffn_in['w1'], 'L2_ffn_w2': _L2_ffn_in['w2'], 'L2_ffn_w3': _L2_ffn_in['w3'], 'L3_xattn_Wq1': _L3_xattn_in['Wq1'], 'L3_xattn_Wk1': _L3_xattn_in['Wk1'], 'L3_xattn_Wv1': _L3_xattn_in['Wv1'], 'L3_xattn_Wq2': _L3_xattn_in['Wq2'], 'L3_xattn_Wk2': _L3_xattn_in['Wk2'], 'L3_xattn_Wv2': _L3_xattn_in['Wv2'], 'L3_xattn_fc1_w': _L3_xattn_in['fc1_w'], 'L3_xattn_fc1_b': _L3_xattn_in['fc1_b'], 'L3_xattn_fc2_w': _L3_xattn_in['fc2_w'], 'L3_xattn_fc2_b': _L3_xattn_in['fc2_b'], 'L3_xattn_ln1_g': _L3_xattn_in['ln1_g'], 'L3_xattn_ln1_b': _L3_xattn_in['ln1_b'], 'L3_xattn_ln2_g': _L3_xattn_in['ln2_g'], 'L3_xattn_ln2_b': _L3_xattn_in['ln2_b'], 'L3_xattn_ln3_g': _L3_xattn_in['ln3_g'], 'L3_xattn_ln3_b': _L3_xattn_in['ln3_b'], 'L3_ffn_W_fc': _L3_ffn_in['W_fc'], 'L3_ffn_b_fc': _L3_ffn_in['b_fc'], 'L3_ffn_A_fc': _L3_ffn_in['A_fc'], 'L3_ffn_B_fc': _L3_ffn_in['B_fc'], 'L3_ffn_W_proj': _L3_ffn_in['W_proj'], 'L3_ffn_b_proj': _L3_ffn_in['b_proj'], 'L3_ffn_A_proj': _L3_ffn_in['A_proj'], 'L3_ffn_B_proj': _L3_ffn_in['B_proj']}

def reference(x, ctx_1024, mask_Bx1xSxS2_if1, mask_BxS2_bk0, g_xattn, g_ffn, L0_xattn_qkv_w, L0_xattn_qkv_b, L0_xattn_sa_out_w, L0_xattn_sa_out_b, L0_xattn_in_proj_w, L0_xattn_in_proj_b, L0_xattn_mha_out_w, L0_xattn_mha_out_b, L0_xattn_lin1_w, L0_xattn_lin1_b, L0_xattn_lin2_w, L0_xattn_lin2_b, L0_xattn_ln1_g, L0_xattn_ln1_b, L0_xattn_ln2_g, L0_xattn_ln2_b, L0_xattn_ln3_g, L0_xattn_ln3_b, L0_ffn_gate_w, L0_ffn_gate_b, L0_ffn_We1, L0_ffn_be1, L0_ffn_We2, L0_ffn_be2, L0_ffn_We3, L0_ffn_be3, L0_ffn_ws1, L0_ffn_bs1, L0_ffn_ws2, L0_ffn_bs2, L0_ffn_ws3, L0_ffn_bs3, L1_xattn_Wv, L1_xattn_Wk, L1_xattn_Wq, L1_xattn_Wo, L1_xattn_bo, L1_ffn_gate_w, L1_ffn_gate_b, L1_ffn_W1, L1_ffn_b1, L1_ffn_W2, L1_ffn_b2, L2_xattn_ln_x_w, L2_xattn_ln_x_b, L2_xattn_ln_l_w, L2_xattn_ln_l_b, L2_xattn_Wq, L2_xattn_Wkv, L2_xattn_q_scale, L2_xattn_k_scale, L2_xattn_Wo, L2_xattn_ln_o_w, L2_xattn_ln_o_b, L2_ffn_gate_w, L2_ffn_expert_bias, L2_ffn_w1, L2_ffn_w2, L2_ffn_w3, L3_xattn_Wq1, L3_xattn_Wk1, L3_xattn_Wv1, L3_xattn_Wq2, L3_xattn_Wk2, L3_xattn_Wv2, L3_xattn_fc1_w, L3_xattn_fc1_b, L3_xattn_fc2_w, L3_xattn_fc2_b, L3_xattn_ln1_g, L3_xattn_ln1_b, L3_xattn_ln2_g, L3_xattn_ln2_b, L3_xattn_ln3_g, L3_xattn_ln3_b, L3_ffn_W_fc, L3_ffn_b_fc, L3_ffn_A_fc, L3_ffn_B_fc, L3_ffn_W_proj, L3_ffn_b_proj, L3_ffn_A_proj, L3_ffn_B_proj):
    import jax
    import jax.numpy as jnp

    def _L0_xattn_ref(tgt, memory, qkv_w, qkv_b, sa_out_w, sa_out_b, in_proj_w, in_proj_b, mha_out_w, mha_out_b, lin1_w, lin1_b, lin2_w, lin2_b, ln1_g, ln1_b, ln2_g, ln2_b, ln3_g, ln3_b):
        import jax, jax.numpy as jnp
        import numpy as np
        B, NT, NM, C, H, FF = (8, 128, 256, 128, 8, 512)

        def _ln(x, g, b):
            m = x.mean(-1, keepdims=True)
            v = jnp.mean((x - m) ** 2, axis=-1, keepdims=True)
            return (x - m) / jnp.sqrt(v + 1e-05) * g + b
        Bx, N, Cx = tgt.shape
        qkv = tgt @ qkv_w.T + qkv_b
        q, k, v = jnp.split(qkv, 3, axis=-1)
        scores = jnp.einsum('bnc,bmc->bnm', q, k) * jnp.sqrt(jnp.float32(Cx))
        diag = jnp.eye(N, dtype=bool)
        scores = jnp.where(diag[None, :, :], scores, -jnp.inf)
        attn = jax.nn.softmax(scores, axis=-1)
        sa = jnp.einsum('bnm,bmc->bnc', attn, v) @ sa_out_w.T + sa_out_b
        x = _ln(tgt + sa, ln1_g, ln1_b)
        d = Cx // H
        wq, wk, wv = jnp.split(in_proj_w, 3, axis=0)
        bq, bk, bv = jnp.split(in_proj_b, 3, axis=0)
        qh = (x @ wq.T + bq).reshape(Bx, N, H, d).transpose(0, 2, 1, 3)
        kh = (memory @ wk.T + bk).reshape(Bx, -1, H, d).transpose(0, 2, 1, 3)
        vh = (memory @ wv.T + bv).reshape(Bx, -1, H, d).transpose(0, 2, 1, 3)
        a = jax.nn.softmax(jnp.einsum('bhnd,bhmd->bhnm', qh, kh) / jnp.sqrt(jnp.float32(d)), axis=-1)
        ca = jnp.einsum('bhnm,bhmd->bhnd', a, vh).transpose(0, 2, 1, 3).reshape(Bx, N, Cx)
        ca = ca @ mha_out_w.T + mha_out_b
        x = _ln(x + ca, ln2_g, ln2_b)
        ff = jax.nn.relu(x @ lin1_w.T + lin1_b) @ lin2_w.T + lin2_b
        return _ln(x + ff, ln3_g, ln3_b)

    def _L0_ffn_ref(x, gate_w, gate_b, We1, be1, We2, be2, We3, be3, ws1, bs1, ws2, bs2, ws3, bs3):
        import jax, jax.numpy as jnp
        import numpy as np
        DIM = 128
        E = 16
        TOPK = 2
        G = 4
        TOPK_G = 2
        INTER = 64
        N_SHARED = 2
        ROUTE_SCALE = 1.0

        def _gate(xf, gate_w, gate_b):
            scores = xf @ gate_w.T
            scores = jax.nn.softmax(scores.astype(jnp.float32), axis=-1)
            orig = scores
            scores = scores + gate_b
            T = xf.shape[0]
            sg = scores.reshape(T, G, E // G)
            group_scores = jax.lax.top_k(sg, 2)[0].sum(-1)
            _, gidx = jax.lax.top_k(group_scores, TOPK_G)
            keep = jax.nn.one_hot(gidx, G).sum(axis=1) > 0
            sg = jnp.where(keep[:, :, None], sg, -jnp.inf)
            scores = sg.reshape(T, E)
            _, idx = jax.lax.top_k(scores, TOPK)
            weights = jnp.take_along_axis(orig, idx, axis=1)
            weights = (weights * ROUTE_SCALE).astype(xf.dtype)
            return (weights, idx)
        shape = x.shape
        xf = x.reshape(-1, DIM)
        weights, idx = _gate(xf, gate_w, gate_b)
        combine = (jax.nn.one_hot(idx, E, dtype=xf.dtype) * weights[..., None]).sum(1)
        h1 = jnp.einsum('td,edi->tei', xf, We1) + be1
        h3 = jnp.einsum('td,edi->tei', xf, We3) + be3
        h = jax.nn.silu(h1) * h3
        yo = jnp.einsum('tei,eid->ted', h, We2) + be2
        y = jnp.einsum('te,ted->td', combine, yo)
        z = jax.nn.silu(xf @ ws1 + bs1) * (xf @ ws3 + bs3) @ ws2 + bs2
        return (y + z).reshape(shape)

    def _L1_xattn_ref(values, keys, queries, mask, Wv, Wk, Wq, Wo, bo):
        import jax, jax.numpy as jnp
        import numpy as np
        HEADS = 16
        N, Sq, E = queries.shape
        H = HEADS
        D = E // H
        v = values.reshape(N, -1, H, D)
        k = keys.reshape(N, -1, H, D)
        q = queries.reshape(N, Sq, H, D)
        v = jnp.einsum('nlhd,od->nlho', v, Wv)
        k = jnp.einsum('nlhd,od->nlho', k, Wk)
        q = jnp.einsum('nqhd,od->nqho', q, Wq)
        energy = jnp.einsum('nqhd,nkhd->nhqk', q, k)
        energy = jnp.where(mask == 0, jnp.float32(-1e+20), energy)
        attn = jax.nn.softmax(energy * (1.0 / E ** 0.5), axis=3)
        out = jnp.einsum('nhqk,nkhd->nqhd', attn, v).reshape(N, Sq, E)
        return out @ Wo.T + bo

    def _L1_ffn_ref(h, gate_w, gate_b, W1, b1, W2, b2):
        import math
        import jax, jax.numpy as jnp
        import numpy as np
        B, L, D, FF, E, K = (4, 256, 128, 512, 8, 2)
        CAPACITY_FACTOR = 1.25
        T = B * L
        CAP = math.ceil(CAPACITY_FACTOR * T * K / E)
        Bb, Ll, Dm = h.shape
        Tt = Bb * Ll
        x = h.reshape(Tt, Dm)
        logits = x @ gate_w.T + gate_b
        probs = jax.nn.softmax(logits, axis=-1)
        topk_prob, topk_idx = jax.lax.top_k(probs, K)
        y = jnp.zeros((Tt, Dm), dtype=h.dtype)
        n_slots = E * CAP
        for c in range(K):
            idx = topk_idx[:, c]
            prb = topk_prob[:, c]
            oh = jax.nn.one_hot(idx, E, dtype=jnp.int32)
            pos = jnp.take_along_axis(jnp.cumsum(oh, axis=0) - 1, idx[:, None], axis=1)[:, 0]
            keep = pos < CAP
            buf_idx = jnp.where(keep, idx * CAP + pos, n_slots)
            xbuf = jnp.zeros((n_slots, Dm), x.dtype).at[buf_idx].set(x, mode='drop')
            xb = xbuf.reshape(E, CAP, Dm)
            hmid = jax.nn.relu(jnp.einsum('ecd,edf->ecf', xb, W1) + b1[:, None, :])
            yb = jnp.einsum('ecf,efd->ecd', hmid, W2) + b2[:, None, :]
            ytok = yb.reshape(n_slots, Dm)[jnp.clip(buf_idx, 0, n_slots - 1)]
            y = y + ytok * (prb * keep.astype(prb.dtype))[:, None]
        return y.reshape(Bb, Ll, Dm)

    def _L2_xattn_ref(x, latents, mask, ln_x_w, ln_x_b, ln_l_w, ln_l_b, Wq, Wkv, q_scale, k_scale, Wo, ln_o_w, ln_o_b):
        import jax, jax.numpy as jnp
        import numpy as np
        DIM, DIM_HEAD, HEADS, SCALE = (128, 64, 8, 8.0)
        INNER = DIM_HEAD * HEADS
        LN_EPS = 1e-05
        L2_EPS = 1e-12

        def layer_norm(x, w, b):
            mu = jnp.mean(x, axis=-1, keepdims=True)
            var = jnp.mean(jnp.square(x - mu), axis=-1, keepdims=True)
            return (x - mu) * jax.lax.rsqrt(var + LN_EPS) * w + b

        def l2norm(t):
            n = jnp.sqrt(jnp.sum(jnp.square(t), axis=-1, keepdims=True))
            return t / jnp.maximum(n, L2_EPS)
        b, n, _ = x.shape
        m = latents.shape[1]
        x = layer_norm(x, ln_x_w, ln_x_b)
        latents = layer_norm(latents, ln_l_w, ln_l_b)
        q = latents @ Wq
        kv_input = jnp.concatenate([x, latents], axis=1)
        kv = kv_input @ Wkv
        k, v = jnp.split(kv, 2, axis=-1)

        def to_heads(t):
            return t.reshape(t.shape[0], t.shape[1], HEADS, DIM_HEAD).transpose(0, 2, 1, 3)
        q, k, v = map(to_heads, (q, k, v))
        q = l2norm(q) * q_scale
        k = l2norm(k) * k_scale
        sim = jnp.einsum('bhid,bhjd->bhij', q, k) * SCALE
        full_mask = jnp.concatenate([mask, jnp.ones((b, m), dtype=bool)], axis=1)[:, None, None, :]
        max_neg = -jnp.finfo(sim.dtype).max
        sim = jnp.where(full_mask, sim, max_neg)
        attn = jax.nn.softmax(sim.astype(jnp.float32), axis=-1).astype(sim.dtype)
        out = jnp.einsum('bhij,bhjd->bhid', attn, v)
        out = out.transpose(0, 2, 1, 3).reshape(b, m, INNER)
        return layer_norm(out @ Wo, ln_o_w, ln_o_b)

    def _L2_ffn_ref(x, gate_w, expert_bias, w1, w2, w3):
        import jax, jax.numpy as jnp
        import numpy as np
        TOP_K = 2
        NUM_EXPERTS = 8
        DIM = 128
        HIDDEN = 352
        BS, SLEN = (2, 128)

        def _grouped_ffn(x, w1, w2, w3, counts):
            num_experts = w1.shape[0]
            ends = jnp.cumsum(counts)
            starts = ends - counts
            t = jnp.arange(x.shape[0])
            out = jnp.zeros((x.shape[0], w2.shape[-1]), x.dtype)
            for e in range(num_experts):
                m = ((t >= starts[e]) & (t < ends[e])).astype(x.dtype)[:, None]
                xe = x * m
                h = jax.nn.silu(xe @ w1[e]) * (xe @ w3[e])
                out = out + h @ w2[e] * m
            return out
        bs, slen, dim = x.shape
        num_experts = gate_w.shape[0]
        xf = x.reshape(bs * slen, dim)
        scores = jax.nn.softmax((xf @ gate_w.T).astype(jnp.float32), axis=-1)
        _, sel = jax.lax.top_k(scores + expert_bias, TOP_K)
        top_scores = jnp.take_along_axis(scores, sel, axis=1).reshape(-1)
        sel_flat = sel.reshape(-1)
        counts = jnp.zeros((num_experts,), jnp.int32).at[sel_flat].add(1)
        order = jnp.argsort(sel_flat, stable=True)
        top_scores_sorted = top_scores[order]
        token_idx = order // TOP_K
        routed = xf[token_idx] * top_scores_sorted[:, None].astype(xf.dtype)
        routed_out = _grouped_ffn(routed, w1, w2, w3, counts)
        out = jnp.zeros_like(xf).at[token_idx].add(routed_out)
        return out.reshape(bs, slen, dim)

    def _L3_xattn_ref(x, context, Wq1, Wk1, Wv1, Wq2, Wk2, Wv2, fc1_w, fc1_b, fc2_w, fc2_b, ln1_g, ln1_b, ln2_g, ln2_b, ln3_g, ln3_b):
        import jax, jax.numpy as jnp
        import numpy as np
        E = 128
        NUM_HEADS = 16
        DK = E // NUM_HEADS
        EPS = 1e-05
        NEG_INF = -jnp.inf

        def layer_norm(x, g, b):
            mu = jnp.mean(x, axis=-1, keepdims=True)
            var = jnp.var(x, axis=-1, keepdims=True)
            return (x - mu) * jax.lax.rsqrt(var + EPS) * g + b

        def self_attn(x, Wq, Wk, Wv):
            Q, K, V = (x @ Wq, x @ Wk, x @ Wv)
            energy = jnp.einsum('bqd,bkd->bqk', Q, K)
            S = energy.shape[-1]
            lengths = jnp.sum(energy[:, 0] != 0, axis=-1)
            kidx = jnp.arange(S)
            pad = kidx[None, None, :] >= lengths[:, None, None]
            causal = kidx[None, :] < kidx[:, None]
            causal = (kidx[None, :] > kidx[:, None])[None]
            energy = jnp.where(pad | causal, NEG_INF, energy)
            score = jax.nn.softmax(energy / np.sqrt(DK), axis=-1)
            return jnp.einsum('bqk,bkd->bqd', score, V)

        def cross_attn(x, context, Wq, Wk, Wv):
            Q = x @ Wq
            K, V = (context @ Wk, context @ Wv)
            energy = jnp.einsum('bqd,bkd->bqk', Q, K)
            Sk = energy.shape[-1]
            lengths = jnp.sum(energy[:, 0] != 0, axis=-1)
            kidx = jnp.arange(Sk)
            pad = kidx[None, None, :] >= lengths[:, None, None]
            energy = jnp.where(pad, NEG_INF, energy)
            score = jax.nn.softmax(energy / np.sqrt(DK), axis=-1)
            return jnp.einsum('bqk,bkd->bqd', score, V)
        z = self_attn(x, Wq1, Wk1, Wv1)
        x = layer_norm(x + z, ln1_g, ln1_b)
        z = cross_attn(x, context, Wq2, Wk2, Wv2)
        x = layer_norm(x + z, ln2_g, ln2_b)
        z = jax.nn.relu(x @ fc1_w + fc1_b)
        z = z @ fc2_w + fc2_b
        return layer_norm(x + z, ln3_g, ln3_b)

    def _L3_ffn_ref(hidden_states, W_fc, b_fc, A_fc, B_fc, W_proj, b_proj, A_proj, B_proj):
        import jax, jax.numpy as jnp
        import numpy as np
        BITS = 8
        LORA_RANK = 16
        LORA_ALPHA = 32
        SCALING = LORA_ALPHA / LORA_RANK

        def fake_quant_weight(w, bits=BITS):
            qmax = 2.0 ** (bits - 1) - 1
            scale = jnp.max(jnp.abs(w)) / qmax
            wq = jnp.clip(jnp.round(w / scale), -qmax - 1, qmax) * scale
            return w + jax.lax.stop_gradient(wq - w)

        def qat_lora_linear(x, W, b, A, B):
            Wq = fake_quant_weight(W)
            base = jnp.einsum('bsi,oi->bso', x, Wq) + b
            lora = jnp.einsum('bsr,or->bso', jnp.einsum('bsi,ri->bsr', x, A), B)
            return base + SCALING * lora
        h = qat_lora_linear(hidden_states, W_fc, b_fc, A_fc, B_fc)
        h = jax.nn.gelu(h, approximate=False)
        h = qat_lora_linear(h, W_proj, b_proj, A_proj, B_proj)
        return h
    x = x + jnp.tanh(g_xattn[0]) * _L0_xattn_ref(_layernorm(x, axis=-1), ctx_1024, L0_xattn_qkv_w, L0_xattn_qkv_b, L0_xattn_sa_out_w, L0_xattn_sa_out_b, L0_xattn_in_proj_w, L0_xattn_in_proj_b, L0_xattn_mha_out_w, L0_xattn_mha_out_b, L0_xattn_lin1_w, L0_xattn_lin1_b, L0_xattn_lin2_w, L0_xattn_lin2_b, L0_xattn_ln1_g, L0_xattn_ln1_b, L0_xattn_ln2_g, L0_xattn_ln2_b, L0_xattn_ln3_g, L0_xattn_ln3_b)
    x = x + jnp.tanh(g_ffn[0]) * _L0_ffn_ref(_layernorm(x, axis=-1), L0_ffn_gate_w, L0_ffn_gate_b, L0_ffn_We1, L0_ffn_be1, L0_ffn_We2, L0_ffn_be2, L0_ffn_We3, L0_ffn_be3, L0_ffn_ws1, L0_ffn_bs1, L0_ffn_ws2, L0_ffn_bs2, L0_ffn_ws3, L0_ffn_bs3)
    x = x + jnp.tanh(g_xattn[1]) * _L1_xattn_ref(ctx_1024, ctx_1024, _layernorm(x, axis=-1), mask_Bx1xSxS2_if1, L1_xattn_Wv, L1_xattn_Wk, L1_xattn_Wq, L1_xattn_Wo, L1_xattn_bo)
    x = x + jnp.tanh(g_ffn[1]) * _L1_ffn_ref(_layernorm(x, axis=-1), L1_ffn_gate_w, L1_ffn_gate_b, L1_ffn_W1, L1_ffn_b1, L1_ffn_W2, L1_ffn_b2)
    x = x + jnp.tanh(g_xattn[2]) * _L2_xattn_ref(ctx_1024, _layernorm(x, axis=-1), mask_BxS2_bk0, L2_xattn_ln_x_w, L2_xattn_ln_x_b, L2_xattn_ln_l_w, L2_xattn_ln_l_b, L2_xattn_Wq, L2_xattn_Wkv, L2_xattn_q_scale, L2_xattn_k_scale, L2_xattn_Wo, L2_xattn_ln_o_w, L2_xattn_ln_o_b)
    x = x + jnp.tanh(g_ffn[2]) * _L2_ffn_ref(_layernorm(x, axis=-1), L2_ffn_gate_w, L2_ffn_expert_bias, L2_ffn_w1, L2_ffn_w2, L2_ffn_w3)
    x = x + jnp.tanh(g_xattn[3]) * _L3_xattn_ref(_layernorm(x, axis=-1), ctx_1024, L3_xattn_Wq1, L3_xattn_Wk1, L3_xattn_Wv1, L3_xattn_Wq2, L3_xattn_Wk2, L3_xattn_Wv2, L3_xattn_fc1_w, L3_xattn_fc1_b, L3_xattn_fc2_w, L3_xattn_fc2_b, L3_xattn_ln1_g, L3_xattn_ln1_b, L3_xattn_ln2_g, L3_xattn_ln2_b, L3_xattn_ln3_g, L3_xattn_ln3_b)
    x = x + jnp.tanh(g_ffn[3]) * _L3_ffn_ref(_layernorm(x, axis=-1), L3_ffn_W_fc, L3_ffn_b_fc, L3_ffn_A_fc, L3_ffn_B_fc, L3_ffn_W_proj, L3_ffn_b_proj, L3_ffn_A_proj, L3_ffn_B_proj)
    return x

_drawn_inputs = setup_inputs


def setup_inputs(seed=0):
    import zlib

    import numpy as np

    out = dict(_drawn_inputs(seed))
    spreads = {'L0_xattn_qkv_b': (0.0, 0.49),
     'L0_xattn_sa_out_b': (0.0, 0.1),
     'L0_xattn_in_proj_b': (0.0, 0.459),
     'L0_xattn_mha_out_b': (0.0, 0.1),
     'L0_xattn_lin1_b': (0.0, 0.368),
     'L0_xattn_lin2_b': (0.0, 0.1),
     'L0_xattn_ln1_g': (1.0, 0.2),
     'L0_xattn_ln1_b': (0.0, 0.1),
     'L0_xattn_ln2_g': (1.0, 0.2),
     'L0_xattn_ln2_b': (0.0, 0.1),
     'L0_xattn_ln3_g': (1.0, 0.2),
     'L0_xattn_ln3_b': (0.0, 0.1),
     'L0_ffn_gate_b': (0.0, 0.1),
     'L0_ffn_be1': (0.0, 0.8),
     'L0_ffn_be2': (0.0, 0.556),
     'L0_ffn_be3': (0.0, 0.8),
     'L0_ffn_bs1': (0.0, 0.273),
     'L0_ffn_bs2': (0.0, 0.1),
     'L0_ffn_bs3': (0.0, 0.293),
     'L1_xattn_bo': (0.0, 0.1),
     'L1_ffn_gate_b': (0.0, 0.8),
     'L1_ffn_b1': (0.0, 0.8),
     'L1_ffn_b2': (0.0, 0.532),
     'L2_xattn_ln_x_w': (1.0, 0.6),
     'L2_xattn_ln_x_b': (0.0, 0.8),
     'L2_xattn_ln_l_w': (1.0, 0.2),
     'L2_xattn_ln_l_b': (0.0, 0.1),
     'L2_xattn_q_scale': (1.0, 0.2),
     'L2_xattn_k_scale': (1.0, 0.2),
     'L2_xattn_ln_o_w': (1.0, 0.2),
     'L2_xattn_ln_o_b': (0.0, 0.1),
     'L2_ffn_expert_bias': (0.0, 0.8),
     'L3_xattn_fc1_b': (0.0, 0.319),
     'L3_xattn_fc2_b': (0.0, 0.399),
     'L3_xattn_ln1_g': (1.0, 0.2),
     'L3_xattn_ln1_b': (0.0, 0.269),
     'L3_xattn_ln2_g': (1.0, 0.2),
     'L3_xattn_ln2_b': (0.0, 0.303),
     'L3_xattn_ln3_g': (1.0, 0.2),
     'L3_xattn_ln3_b': (0.0, 0.325),
     'L3_ffn_b_fc': (0.0, 0.327),
     'L3_ffn_B_fc': (0.0, 0.1),
     'L3_ffn_b_proj': (0.0, 0.287),
     'L3_ffn_B_proj': (0.0, 0.1)}
    factors = {'g_ffn': 22.424,
     'L0_xattn_in_proj_w': 2.854,
     'L1_ffn_gate_w': 3.919,
     'L1_ffn_W1': 7.22,
     'L1_ffn_W2': 5.44,
     'L2_ffn_gate_w': 8.0,
     'L2_ffn_w1': 8.0,
     'L2_ffn_w2': 8.0,
     'L2_ffn_w3': 8.0}
    for name, (base, spread) in spreads.items():
        noise = np.random.default_rng([zlib.crc32(name.encode()), seed]).standard_normal(out[name].shape)
        drawn = base * np.exp(spread * noise) if base else spread * noise
        out[name] = jnp.asarray(drawn.astype(out[name].dtype))
    for name, factor in factors.items():
        out[name] = (out[name] * factor).astype(out[name].dtype)
    return out
```

```python
from contextlib import ExitStack

import concourse.bass as bass
from concourse import mybir

F32 = mybir.dt.float32
I32 = mybir.dt.int32
U8 = mybir.dt.uint8
ALU = mybir.AluOpType
ACT = mybir.ActivationFunctionType
AX = mybir.AxisListType

P = 128
B, T, S2 = 4, 512, 77
NT = T // P
J = 2
PASSES = B // J
EPS = 1e-5
LOW = -1e30
CAP = 320

BLOCKS = (["l0_v", "l0_sa", "l0_q", "l0_k", "l0_mv", "l0_mo"] + [f"l0_up{c}" for c in range(4)]
          + [f"l0_down{c}" for c in range(4)] + ["l0_s1", "l0_s3", "l0_s2"]
          + ["l1_q", "l1_k", "l1_v", "l1_o"]
          + [f"l2_q{c}" for c in range(4)] + [f"l2_k{c}" for c in range(4)] + [f"l2_v{c}" for c in range(4)]
          + [f"l2_o{c}" for c in range(4)]
          + ["l3_q1", "l3_k1", "l3_v1", "l3_q2", "l3_k2", "l3_v2", "l3_f1", "l3_f2"]
          + [f"l3_up{c}" for c in range(4)] + [f"l3_down{c}" for c in range(4)])
COLS = (["l0_bv", "l0_bo", "l0_bq", "l0_bk", "l0_bmv", "l0_bmo"] + [f"l0_bup{c}" for c in range(4)]
        + ["l0_bdown", "ln1_g", "ln1_b", "ln2_g", "ln2_b", "ln3_g", "ln3_b"]
        + [f"be1_{p}" for p in range(8)] + [f"be3_{p}" for p in range(8)] + ["bs1", "bs3", "bs2"]
        + ["l1_bo"] + [f"l1_b1_{e}_{c}" for e in range(8) for c in range(4)] + [f"l1_b2_{e}" for e in range(8)]
        + ["l2_xg", "l2_xb", "l2_lg", "l2_lb", "l2_og", "l2_ob", "l2_qs", "l2_ks"]
        + ["l3_b1", "l3_b2", "l3_n1g", "l3_n1b", "l3_n2g", "l3_n2b", "l3_n3g", "l3_n3b"]
        + [f"l3_bfc{c}" for c in range(4)] + ["l3_bproj"])
CONSTS = {"ident": 128, "upto": 128, "ones": 128, "causal": 128, "heads16": 8, "heads8": 16,
          "halves": 2, "first16": 16, "first8": 8, "first4": 4, "keys": 512}
NORMS = ["l0_in", "l0_1", "l0_2", "l0_3", "l0_moe", "l1_in", "l1_moe", "l2_in", "l2_lat", "l2_out", "l2_moe",
         "l3_in", "l3_1", "l3_2", "l3_3", "l3_ffn"]


def starts(widths):
    out, at = {}, 0
    for name, w in widths.items():
        out[name] = (at, at + w)
        at += w
    return out, at


CONST_AT, CONST_N = starts(CONSTS)


class Order:

    def __init__(self, *names):
        self.names = list(names)

    def __call__(self, name, j):
        return self.names.index(name) * J + j + 1


def flamingo_kernel(nc, x, ctx_t, ctx_k, attn_mask, key_mask, gates, blocks, cols, rows, consts, pair_sel, gate16, be2, l1_gate, l2_gate, We1, We2, We3, W1, W2, w1, w2, w3,
                    A_fc, B_fc, A_proj, B_proj, out):
    with ExitStack() as ctx:
        def sb(name, shape, dt=F32):
            return ctx.enter_context(nc.sbuf_tensor(name, shape, dt))

        def sem(name):
            return ctx.enter_context(nc.semaphore(name))

        psum = ctx.enter_context(nc.psum_tensor("psum", [P, 8, 512], F32))

        def bank(j, k):
            return psum[:, 4 * j + k, :]

        blocks_sb = sb("blocks_sb", [P, len(BLOCKS), P])
        cols_sb = sb("cols_sb", [P, len(COLS)])
        rows_sb = sb("rows_sb", [P, 32])
        consts_sb = sb("consts_sb", [P, CONST_N])
        pair_sel_sb = sb("pair_sel_sb", [16, 8 * P])
        gate16_sb = sb("gate16_sb", [P, 16])
        l1_gate_sb = sb("l1_gate_sb", [P, 8])
        l2_gate_sb = sb("l2_gate_sb", [P, 8])
        be2_sb = sb("be2_sb", [16, P])
        we1_sb = sb("we1_sb", [P, 16, 64])
        we3_sb = sb("we3_sb", [P, 16, 64])
        we2_sb = sb("we2_sb", [P, 8, P])
        HID = w1.shape[2]
        l1w1_sb = sb("l1w1_sb", [P, 8, 512])
        l1w2_sb = sb("l1w2_sb", [P, 8, 4, P])
        l2w1_sb = sb("l2w1_sb", [P, 8, HID])
        l2w3_sb = sb("l2w3_sb", [P, 8, HID])
        l2w2_sb = sb("l2w2_sb", [P, 8, 3, P])
        gates_sb = sb("gates_sb", [P, 8])
        tg_sb = sb("tg_sb", [P, 8])
        gb_sb = sb("gb_sb", [P, 8])
        half_sb = sb("half_sb", [P, 16])
        carry_sb = sb("carry_sb", [P, 16])
        lora_sb = sb("lora_sb", [16, 2, 512 + P])

        def blk(name):
            return blocks_sb[:, BLOCKS.index(name), :]

        def col(name):
            i = COLS.index(name)
            return cols_sb[:, i:i + 1]

        def const(name):
            a, b = CONST_AT[name]
            return consts_sb[:, a:b]

        ident = const("ident")

        def expert_pick(e):
            return ident[0:8, e:e + 1].to_broadcast([8, P])

        def pair_pick(p):
            return pair_sel_sb[:, p * P:(p + 1) * P]

        XT = [sb(f"XT{j}", [P, T]) for j in range(J)]
        FA = [sb(f"FA{j}", [P, T]) for j in range(J)]
        FB = [sb(f"FB{j}", [P, T]) for j in range(J)]
        FC = [sb(f"FC{j}", [P, T]) for j in range(J)]
        XN = [sb(f"XN{j}", [P, NT, P]) for j in range(J)]
        ctxT = [sb(f"ctxT{j}", [P, S2]) for j in range(J)]
        stats = [sb(f"stats{j}", [P, NT, 6]) for j in range(J)]
        mv = [sb(f"mv{j}", [P, NT, 2]) for j in range(J)]
        var = [sb(f"var{j}", [P, NT]) for j in range(J)]
        rstd = [sb(f"rstd{j}", [P, NT]) for j in range(J)]
        arena = sb("arena", [P, 15104])
        used = [0]

        def take(n, rows_=P):
            a = arena[0:rows_, used[0]:used[0] + n]
            used[0] += n
            assert used[0] <= 15104, used[0]
            return a

        ctx_tok = [sb(f"ctx_tok{j}", [S2, P]) for j in range(J)]
        key_ok = [sb(f"key_ok{j}", [S2, 1], U8) for j in range(J)]

        loaded = sem("loaded")
        loaded_l0_moe = sem("loaded_l0_moe")
        loaded_later = sem("loaded_later")
        inputs = sem("inputs")
        outputs = sem("outputs")
        chain_d = sem("vector_chain")
        chain_a = sem("scalar_chain")
        chain_p = sem("pool_chain")
        pass_done = sem("pass_done")
        cleared = sem("cleared")
        setup_done = sem("setup_done")
        setup_pe = sem("setup_pe")
        setup_act = sem("setup_act")
        setup_pool = sem("setup_pool")
        per_pass = []

        def psem(name):
            per_pass.append(sem(name))
            return per_pass[-1]

        norm_in = psem("norm_in")
        norm_var = psem("norm_var")
        norm_rstd = psem("norm_rstd")
        norm_xn = psem("norm_xn")
        norm_out = psem("norm_out")
        norm_T = psem("norm_T")
        norm = Order(*NORMS)

        class Chain:

            def __init__(self, eng, s):
                self.eng, self.s, self.n = eng, s, 0

            def tag(self, ins):
                ins.then_inc(self.s, 1)
                self.n += 1

            def settle(self):
                if self.n:
                    self.eng.wait_ge(self.s, self.n)

            def link(self, ins):
                self.tag(ins)
                self.settle()

        def pe_turn(pe, src, dst):
            for t in range(NT):
                last = nc.tensor.transpose(dst[:, t * P:(t + 1) * P], src[:, t * P:(t + 1) * P], ident)
            return last

        def pe_norm_in(pe, name, j, src):
            pe_turn(pe, src, bank(j, 3)).then_inc(norm_in, 1)

        def pe_norm_out(pe, name, j):
            pe.wait_ge(norm_xn, norm(name, j))
            pe_turn(pe, XN[j][:, :, :].rearrange("p t f -> p (t f)"), bank(j, 2)).then_inc(norm_out, 1)

        def dve_norm(dve, ch, name):
            for j in range(J):
                dve.wait_ge(norm_in, norm(name, j))
                for t in range(NT):
                    ch.tag(nc.vector.bn_stats(stats[j][:, t, :], bank(j, 3)[:, t * P:(t + 1) * P]))
                ch.settle()
                for t in range(NT):
                    ch.tag(nc.vector.bn_aggr(mv[j][:, t, :], stats[j][:, t, :]))
                ch.settle()
                nc.vector.tensor_scalar(var[j][:, :], mv[j][:, :, 1], EPS, None, ALU.add).then_inc(norm_var, 1)
            for j in range(J):
                dve.wait_ge(norm_rstd, norm(name, j))
                for t in range(NT):
                    last = nc.vector.tensor_scalar(XN[j][:, t, :], bank(j, 3)[:, t * P:(t + 1) * P],
                                                   mv[j][:, t, 0:1], rstd[j][:, t:t + 1],
                                                   ALU.subtract, ALU.mult)
                last.then_inc(norm_xn, 1)

        def pool_norm(pool, name):
            for j in range(J):
                pool.wait_ge(norm_var, norm(name, j))
                nc.gpsimd.tensor_tensor(rstd[j][:, :], var[j][:, :], half_sb[:, 0:NT], ALU.pow)\
                    .then_inc(norm_rstd, 1)

        def act_norm(act, name, dst, g=None, b=None):
            for j in range(J):
                act.wait_ge(norm_out, norm(name, j))
                if g is None:
                    ins = nc.scalar.activation(dst[j][:, :], bank(j, 2), ACT.Identity)
                else:
                    ins = nc.scalar.activation(dst[j][:, :], bank(j, 2), ACT.Identity, bias=col(b), scale=col(g))
                ins.then_inc(norm_T, 1)

        def first_max(ch, src, oh, mx, first, n):
            wide = [P, NT, n]
            ch.link(nc.vector.tensor_reduce(mx, src, AX.X, ALU.max))
            ch.link(nc.vector.tensor_tensor(oh, src, mx.unsqueeze(2).to_broadcast(wide), ALU.is_equal))
            ch.link(nc.vector.tensor_tensor(oh, oh, first.unsqueeze(1).to_broadcast(wide), ALU.mult))
            ch.link(nc.vector.tensor_reduce(mx, oh, AX.X, ALU.max))
            ch.link(nc.vector.tensor_tensor(oh, oh, mx.unsqueeze(2).to_broadcast(wide), ALU.is_equal))

        att_scores = psem("att_scores")
        att_centred = psem("att_centred")
        att_exps = psem("att_exps")
        att_inv = psem("att_inv")
        att_normed = psem("att_normed")
        att_turned = psem("att_turned")
        att_moved = psem("att_moved")
        att_pv = psem("att_pv")
        att_zeros = psem("att_zeros")
        HU = 8
        att_units = {"l0": [(j, t, 0) for j in range(J) for t in range(NT)],
                     "l1": [(j, 2 * tp + s, h) for j in range(J) for tp in range(NT // 2) for h in range(2)
                            for s in range(2)]}
        att_base = {"l0": 0, "l1": len(att_units["l0"])}
        used[0] = 0
        weights = [take(HU * S2) for _ in range(3)]
        weights_t = [take(HU * 2 * P, S2).rearrange("p (h q) -> p h q", q=2 * P) for _ in range(2)]
        k_heads = [take(2 * HU * S2) for _ in range(J)]
        v_heads = [take(16 * (P + 8), S2) for _ in range(J)]
        k_feat = [take(S2) for _ in range(J)]
        row_max = [take(HU) for _ in range(3)]
        row_sum = [take(HU) for _ in range(3)]
        row_inv = [take(HU) for _ in range(3)]
        blocked = [sb(f"blocked{j}", [P, NT * S2])[:, :] for j in range(J)]
        mask_in = [m.bitcast(I32) for m in blocked]

        def head_values(j, hd):
            n = P // hd
            return v_heads[j][:, 0:n * P].rearrange("p (h n) -> p h n", n=P)

        def head_blocks(j, hd):
            n = P // hd
            return v_heads[j][:, 0:n * (P + hd)].rearrange("p (h n) -> p h n", n=P + hd)[:, :, 0:hd]

        def score_banks(u):
            return psum[:, 2 * (u % 2):2 * (u % 2) + 2, 0:4 * S2].rearrange("p b (h s) -> p b h s", s=S2)

        def by_bank(w):
            return w.rearrange("p (b h s) -> p b h s", b=2, s=S2)

        def by_head(w):
            return w.rearrange("p (h s) -> p h s", s=S2)

        def att_pe(pe, layer, Q):
            units, base = att_units[layer], att_base[layer]
            hd, halves = (16, 1) if layer == "l0" else (8, 2)

            def scores(n):
                j, t, half = units[n]
                u = base + n
                if n >= 2:
                    pe.wait_ge(att_centred, u - 1)
                for q in range(2):
                    h = half * HU + 4 * q
                    last = nc.tensor.matmul(psum[:, 2 * (u % 2) + q, 0:4 * S2], Q[j][:, t * P:(t + 1) * P],
                                            k_heads[j][:, h * S2:(h + 4) * S2], start=True, stop=True)
                last.then_inc(att_scores, 1)

            def turn(n):
                u = base + n
                pe.wait_ge(att_normed, u + 1)
                if n >= 1:
                    pe.wait_ge(att_moved, u)
                for h in range(HU):
                    last = nc.tensor.transpose(psum[0:S2, 4 + h // 4, (h % 4) * P:(h % 4 + 1) * P],
                                               weights[u % 3][:, h * S2:(h + 1) * S2], ident)
                last.then_inc(att_turned, 1)

            def outputs_of(g, part):
                j, t, half = units[2 * g]
                pe.wait_ge(att_moved, base + 2 * g + 2)
                for h in range(part * HU // 2, (part + 1) * HU // 2):
                    nh = half * HU + h
                    last = nc.tensor.matmul(psum[:, 6 + j, t * P:(t + 2) * P], head_values(j, hd)[:, nh, :],
                                            weights_t[g % 2][:, h, :], start=(nh == 0), stop=(nh == halves * HU - 1))
                last.then_inc(att_pv, 1)

            scores(0)
            scores(1)
            for n in range(len(units)):
                if n + 2 < len(units):
                    scores(n + 2)
                turn(n)
                if n >= 2:
                    outputs_of(n // 2 - 1, n % 2)
            for part in range(2):
                outputs_of(len(units) // 2 - 1, part)

        def att_act(act, layer, scale):
            units, base = att_units[layer], att_base[layer]

            def exps(n):
                u = base + n
                act.wait_ge(att_centred, u + 1)
                nc.scalar.activation(weights[u % 3], weights[u % 3], ACT.Exp, scale=scale).then_inc(att_exps, 1)

            exps(0)
            exps(1)
            for n in range(len(units)):
                u, g, s = base + n, n // 2, n % 2
                act.wait_ge(att_turned, u + 1)
                if g >= 2:
                    act.wait_ge(att_pv, base + 2 * g - 2)
                nc.scalar.activation(weights_t[g % 2][:, :, s * P:(s + 1) * P].rearrange("p (b h) q -> p b h q", b=2),
                                     psum[0:S2, 4:6, :].rearrange("p b (h q) -> p b h q", q=P),
                                     ACT.Copy).then_inc(att_moved, 1)
                if n + 2 < len(units):
                    exps(n + 2)

        def att_dve(dve, ch, layer):
            units, base = att_units[layer], att_base[layer]

            def centre(n):
                j, t, half = units[n]
                u = base + n
                w, m = weights[u % 3], row_max[u % 3]
                s = score_banks(u)
                dve.wait_ge(att_scores, u + 1)
                if n >= 3:
                    dve.wait_ge(att_turned, u - 2)
                if layer == "l1":
                    block = blocked[j][:, t * S2:(t + 1) * S2].unsqueeze(1).unsqueeze(1).to_broadcast([P, 2, 4, S2])
                    ch.link(nc.vector.tensor_tensor(by_bank(w), s, block, ALU.add))
                    s = by_bank(w)
                ch.link(nc.vector.tensor_reduce(m.rearrange("p (b h) -> p b h", b=2), s, AX.X, ALU.max))
                nc.vector.tensor_tensor(by_bank(w), s, m.rearrange("p (b h) -> p b h", b=2).unsqueeze(3)
                                        .to_broadcast([P, 2, 4, S2]), ALU.subtract).then_inc(att_centred, 1)

            centre(0)
            centre(1)
            for n in range(len(units)):
                u = base + n
                dve.wait_ge(att_exps, u + 1)
                ch.link(nc.vector.tensor_reduce(row_sum[u % 3], by_head(weights[u % 3]), AX.X, ALU.add))
                if n >= 3:
                    dve.wait_ge(att_normed, u - 2)
                nc.vector.reciprocal(row_inv[u % 3], row_sum[u % 3]).then_inc(att_inv, 1)
                if n + 2 < len(units):
                    centre(n + 2)

        def att_pool(pool, layer):
            for u in range(att_base[layer], att_base[layer] + len(att_units[layer])):
                pool.wait_ge(att_inv, u + 1)
                w = by_head(weights[u % 3])
                nc.gpsimd.tensor_tensor(w, w, row_inv[u % 3].unsqueeze(2).to_broadcast([P, HU, S2]), ALU.mult)\
                    .then_inc(att_normed, 1)

        def att_halves(layer):
            return att_base[layer] + len(att_units[layer])

        x_new = psem("x_new")
        x_blk = Order("l0_attn", "l0_moe", "l1_attn", "l1_moe", "l2_attn", "l2_moe", "l3_attn", "l3_ffn")

        l0_prod = psem("l0_prod")
        l0_p = Order("kv", "v", "sa", "q", "mo", "up", "down")
        l0_act = psem("l0_act")
        l0_a = Order("k", "v", "q", "ca", "up", "y")
        l0_dve = psem("l0_dve")
        l0_d = Order("r1", "kv", "r2", "r3")
        used[0] = 0
        hidden = [take(4 * T) for _ in range(J)]

        def l0_attn_pe(pe):
            for j in range(J):
                pe_norm_in(pe, "l0_in", j, XT[j][:, :])
            for j in range(J):
                nc.tensor.matmul(bank(j, 0)[:, 0:S2], blk("l0_k"), ctxT[j][:, :], start=True, stop=True)
                nc.tensor.matmul(bank(j, 1)[0:S2, 0:P], ctxT[j][:, :], blk("l0_mv"), start=True, stop=True)\
                    .then_inc(l0_prod, 1)
            for j in range(J):
                pe_norm_out(pe, "l0_in", j)
            for j in range(J):
                pe.wait_ge(norm_T, norm("l0_in", j))
                nc.tensor.matmul(bank(j, 3), blk("l0_v"), FA[j][:, :], start=True, stop=True).then_inc(l0_prod, 1)
            for j in range(J):
                pe.wait_ge(l0_act, l0_a("v", j))
                nc.tensor.matmul(bank(j, 2), blk("l0_sa"), FB[j][:, :], start=True, stop=True).then_inc(l0_prod, 1)
            for j in range(J):
                pe.wait_ge(l0_dve, l0_d("r1", j))
                pe_norm_in(pe, "l0_1", j, FC[j][:, :])
            for j in range(J):
                pe_norm_out(pe, "l0_1", j)
            for j in range(J):
                pe.wait_ge(norm_T, norm("l0_1", j))
                nc.tensor.matmul(bank(j, 3), blk("l0_q"), FA[j][:, :], start=True, stop=True).then_inc(l0_prod, 1)
            pe.wait_ge(l0_act, l0_a("q", J - 1))
            pe.wait_ge(l0_dve, l0_d("kv", J - 1))
            att_pe(pe, "l0", FB)
            for j in range(J):
                pe.wait_ge(l0_act, l0_a("ca", j))
                nc.tensor.matmul(bank(j, 2), blk("l0_mo"), FC[j][:, :], start=True, stop=True).then_inc(l0_prod, 1)
            for j in range(J):
                pe.wait_ge(l0_dve, l0_d("r2", j))
                pe_norm_in(pe, "l0_2", j, FB[j][:, :])
            for j in range(J):
                pe_norm_out(pe, "l0_2", j)
            for j in range(J):
                pe.wait_ge(norm_T, norm("l0_2", j))
                for c in range(4):
                    last = nc.tensor.matmul(bank(j, c), blk(f"l0_up{c}"), FA[j][:, :], start=True, stop=True)
                last.then_inc(l0_prod, 1)
            for j in range(J):
                pe.wait_ge(l0_act, l0_a("up", j))
                for c in range(4):
                    last = nc.tensor.matmul(bank(j, 0), blk(f"l0_down{c}"), hidden[j][:, c * T:(c + 1) * T],
                                            start=(c == 0), stop=(c == 3))
                last.then_inc(l0_prod, 1)
            for j in range(J):
                pe.wait_ge(l0_dve, l0_d("r3", j))
                pe_norm_in(pe, "l0_3", j, FB[j][:, :])
            for j in range(J):
                pe_norm_out(pe, "l0_3", j)

        def l0_attn_act(act):
            for j in range(J):
                act.wait_ge(l0_prod, l0_p("kv", j))
                nc.scalar.activation(k_feat[j], bank(j, 0)[:, 0:S2], ACT.Identity, bias=col("l0_bk"))\
                    .then_inc(l0_act, 1)
            act_norm(act, "l0_in", FA)
            for j in range(J):
                act.wait_ge(l0_prod, l0_p("v", j))
                nc.scalar.activation(FB[j][:, :], bank(j, 3), ACT.Identity, bias=col("l0_bv")).then_inc(l0_act, 1)
            act_norm(act, "l0_1", FA, "ln1_g", "ln1_b")
            for j in range(J):
                act.wait_ge(l0_prod, l0_p("q", j))
                nc.scalar.activation(FB[j][:, :], bank(j, 3), ACT.Identity, bias=col("l0_bq")).then_inc(l0_act, 1)
            att_act(act, "l0", 0.25)
            for j in range(J):
                act.wait_ge(att_pv, att_halves("l0"))
                nc.scalar.activation(FC[j][:, :], psum[:, 6 + j, :], ACT.Identity, bias=col("l0_bmv")).then_inc(l0_act, 1)
            act_norm(act, "l0_2", FA, "ln2_g", "ln2_b")
            for j in range(J):
                act.wait_ge(l0_prod, l0_p("up", j))
                for c in range(4):
                    last = nc.scalar.activation(hidden[j][:, c * T:(c + 1) * T], bank(j, c), ACT.Relu,
                                                bias=col(f"l0_bup{c}"))
                last.then_inc(l0_act, 1)
            act_norm(act, "l0_3", FA, "ln3_g", "ln3_b")

        def l0_attn_dve(dve, ch):
            dve_norm(dve, ch, "l0_in")
            for j in range(J):
                dve.wait_ge(l0_prod, l0_p("sa", j))
                nc.vector.scalar_tensor_tensor(FC[j][:, :], bank(j, 2), col("l0_bo"), FA[j][:, :],
                                               ALU.add, ALU.add).then_inc(l0_dve, 1)
            for j in range(J):
                dve.wait_ge(l0_act, l0_a("k", j))
                dve.wait_ge(att_zeros, 1)
                ch.tag(nc.vector.tensor_copy(head_blocks(j, 16), bank(j, 1)[0:S2, 0:P].rearrange("p (h d) -> p h d", d=16)))
                nc.vector.tensor_tensor(k_heads[j][:, 0:HU * S2].rearrange("p (h s) -> p h s", s=S2),
                                        k_feat[j].unsqueeze(1).to_broadcast([P, HU, S2]),
                                        const("heads16").unsqueeze(2).to_broadcast([P, HU, S2]), ALU.mult)\
                    .then_inc(l0_dve, 1)
            dve_norm(dve, ch, "l0_1")
            att_dve(dve, ch, "l0")
            for j in range(J):
                dve.wait_ge(l0_prod, l0_p("mo", j))
                nc.vector.scalar_tensor_tensor(FB[j][:, :], bank(j, 2), col("l0_bmo"), FA[j][:, :],
                                               ALU.add, ALU.add).then_inc(l0_dve, 1)
            dve_norm(dve, ch, "l0_2")
            for j in range(J):
                dve.wait_ge(l0_prod, l0_p("down", j))
                nc.vector.scalar_tensor_tensor(FB[j][:, :], bank(j, 0), col("l0_bdown"), FA[j][:, :],
                                               ALU.add, ALU.add).then_inc(l0_dve, 1)
            dve_norm(dve, ch, "l0_3")
            for j in range(J):
                dve.wait_ge(norm_T, norm("l0_3", j))
                nc.vector.scalar_tensor_tensor(XT[j][:, :], FA[j][:, :], tg_sb[:, 0:1], XT[j][:, :],
                                               ALU.mult, ALU.add).then_inc(x_new, 1)

        def l0_attn_pool(pool):
            pool_norm(pool, "l0_in")
            for j in range(J):
                last = nc.gpsimd.memset(v_heads[j], 0.0)
            last.then_inc(att_zeros, 1)
            pool_norm(pool, "l0_1")
            att_pool(pool, "l0")
            pool_norm(pool, "l0_2")
            pool_norm(pool, "l0_3")

        route_e = psem("route_e")
        route_x = psem("route_x")
        route = Order("l0", "l1", "l2")
        logit = [sb(f"logit{j}", [P, NT, 16]) for j in range(J)]
        score = [sb(f"score{j}", [P, NT, 16]) for j in range(J)]
        chosen = [sb(f"chosen{j}", [P, 2, NT, 16]) for j in range(J)]
        combine = [sb(f"combine{j}", [P, NT, 16]) for j in range(J)]
        route_max = [sb(f"route_max{j}", [P, NT]) for j in range(J)]

        def route_exp(act, name):
            for j in range(J):
                act.wait_ge(route_e, route(name, j))
                n = 16 if name == "l0" else 8
                nc.scalar.activation(logit[j][:, :, 0:n], logit[j][:, :, 0:n], ACT.Exp).then_inc(route_x, 1)

        def route_centre(ch, name, j, logits, n, bias=None):
            l, wide = logit[j][:, :, 0:n], [P, NT, n]
            if bias is not None:
                ch.link(nc.vector.tensor_tensor(l, logits, bias.unsqueeze(1).to_broadcast(wide), ALU.add))
                logits = l
            ch.link(nc.vector.tensor_reduce(route_max[j][:, :], logits, AX.X, ALU.max))
            nc.vector.tensor_tensor(l, logits, route_max[j][:, :].unsqueeze(2).to_broadcast(wide), ALU.subtract)\
                .then_inc(route_e, 1)

        def route_softmax(dve, ch, name, j, n):
            l, wide = logit[j][:, :, 0:n], [P, NT, n]
            dve.wait_ge(route_x, route(name, j))
            ch.link(nc.vector.tensor_reduce(route_max[j][:, :], l, AX.X, ALU.add))
            ch.link(nc.vector.reciprocal(route_max[j][:, :], route_max[j][:, :]))
            ch.link(nc.vector.tensor_tensor(l, l, route_max[j][:, :].unsqueeze(2).to_broadcast(wide), ALU.mult))

        def choose_two(ch, j, src, n, first):
            a, b = chosen[j][:, 0, :, 0:n], chosen[j][:, 1, :, 0:n]
            first_max(ch, src, a, route_max[j][:, :], first, n)
            ch.link(nc.vector.scalar_tensor_tensor(src, a, 2 * LOW, src, ALU.mult, ALU.add))
            first_max(ch, src, b, route_max[j][:, :], first, n)

        def pe_logits(pe, j, xT, gate, n):
            for t in range(NT):
                last = nc.tensor.matmul(bank(j, 0)[:, t * n:(t + 1) * n], xT[:, t * P:(t + 1) * P], gate,
                                        start=True, stop=True)
            return last

        def pe_turn_combine(pe, j, n):
            for t in range(NT):
                last = nc.tensor.transpose(bank(j, 1)[0:n, t * P:(t + 1) * P], combine[j][:, t, 0:n], ident)
            return last

        used[0] = 0
        combine_t = [take(T, 16) for _ in range(J)]
        m0_gate = [take(T) for _ in range(J)]
        m0_mid = [take(T) for _ in range(J)]
        m0_hid = [take(T) for _ in range(J)]
        pair_sums = [take(16 * 6) for _ in range(J)]
        group_sc = [take(16) for _ in range(J)]
        group_a = [take(16) for _ in range(J)]
        group_b = [take(16) for _ in range(J)]

        PAIRS = 8
        l0m_prod = psem("l0m_prod")
        l0m_p = Order("gate", "turn", "y")
        l0m_route = psem("l0m_route")
        l0m_ct = psem("l0m_ct")
        l0m_front = psem("l0m_front")
        l0m_silu = psem("l0m_silu")
        l0m_hid = psem("l0m_hid")
        l0m_back = psem("l0m_back")
        l0m_y = psem("l0m_y")
        l0m_units = [(p, j) for p in range(PAIRS + 1) for j in range(J)]

        def l0_moe_pe(pe):
            for j in range(J):
                pe.wait_ge(x_new, x_blk("l0_attn", j))
                pe_norm_in(pe, "l0_moe", j, XT[j][:, :])
            for j in range(J):
                pe_norm_out(pe, "l0_moe", j)
            pe.wait_ge(loaded_l0_moe, 16 * len(L0_MOE_LOADS))
            for j in range(J):
                pe.wait_ge(norm_T, norm("l0_moe", j))
                pe_logits(pe, j, FA[j], gate16_sb[:, :], 16).then_inc(l0m_prod, 1)
            for j in range(J):
                pe.wait_ge(l0m_route, j + 1)
                pe_turn_combine(pe, j, 16).then_inc(l0m_prod, 1)

            def front(u):
                p, j = l0m_units[u]
                pe.wait_ge(l0m_ct, j + 1)
                if u >= J:
                    pe.wait_ge(l0m_hid, u - J + 1)
                if p < PAIRS:
                    w1_, w3_ = we1_sb[:, 2 * p:2 * p + 2, :], we3_sb[:, 2 * p:2 * p + 2, :]
                    nc.tensor.matmul(bank(j, 2), pair_pick(p), combine_t[j], start=True, stop=True)
                else:
                    w1_, w3_ = blk("l0_s1"), blk("l0_s3")
                nc.tensor.matmul(bank(j, 0), w1_, FA[j][:, :], start=True, stop=True)
                nc.tensor.matmul(bank(j, 1), w3_, FA[j][:, :], start=True, stop=True).then_inc(l0m_front, 1)

            def back(u):
                p, j = l0m_units[u]
                pe.wait_ge(l0m_hid, u + 1)
                w = we2_sb[:, p, :] if p < PAIRS else blk("l0_s2")
                nc.tensor.matmul(bank(j, 3), w, m0_hid[j], start=False, stop=(p == PAIRS)).then_inc(l0m_back, 1)

            for u in range(len(l0m_units)):
                front(u)
                if u < J:
                    nc.tensor.matmul(bank(u, 3), be2_sb[:, :], combine_t[u], start=True, stop=False)
                if u >= 1:
                    back(u - 1)
            back(len(l0m_units) - 1)

        def l0_moe_act(act):
            act_norm(act, "l0_moe", FA)
            route_exp(act, "l0")
            for j in range(J):
                act.wait_ge(l0m_prod, l0m_p("turn", j))
                nc.scalar.activation(combine_t[j], bank(j, 1)[0:16, :], ACT.Copy).then_inc(l0m_ct, 1)
            for u, (p, j) in enumerate(l0m_units):
                act.wait_ge(l0m_front, u + 1)
                if u >= J:
                    act.wait_ge(l0m_hid, u - J + 1)
                nc.scalar.activation(m0_gate[j], bank(j, 0), ACT.Silu,
                                     bias=col(f"be1_{p}" if p < PAIRS else "bs1")).then_inc(l0m_silu, 1)
            for j in range(J):
                act.wait_ge(l0m_back, len(l0m_units) - J + j + 1)
                nc.scalar.activation(FB[j][:, :], bank(j, 3), ACT.Identity, bias=col("bs2")).then_inc(l0m_y, 1)

        def l0_moe_dve(dve, ch):
            dve_norm(dve, ch, "l0_moe")
            for j in range(J):
                dve.wait_ge(l0m_prod, l0m_p("gate", j))
                route_centre(ch, "l0", j, bank(j, 0)[:, 0:64].rearrange("p (t e) -> p t e", e=16), 16)
            for j in range(J):
                route_softmax(dve, ch, "l0", j, 16)
                sc, s16 = score[j], score[j][:, :, :].rearrange("p t (g i) -> p (t g) i", i=4)
                ch.link(nc.vector.tensor_tensor(sc[:, :, :], logit[j][:, :, :],
                                                rows_sb[:, 0:16].unsqueeze(1).to_broadcast([P, NT, 16]), ALU.add))
                ps = pair_sums[j].rearrange("p (g k) -> p g k", k=6)
                ch.tag(nc.vector.tensor_tensor(ps[:, :, 0:3], s16[:, :, 0:3], s16[:, :, 1:4], ALU.add))
                ch.tag(nc.vector.tensor_tensor(ps[:, :, 3:5], s16[:, :, 0:2], s16[:, :, 2:4], ALU.add))
                ch.link(nc.vector.tensor_tensor(ps[:, :, 5:6], s16[:, :, 0:1], s16[:, :, 3:4], ALU.add))
                ch.link(nc.vector.tensor_reduce(group_sc[j], ps, AX.X, ALU.max))
                g = group_sc[j].rearrange("p (t g) -> p t g", g=4)
                ga = group_a[j].rearrange("p (t g) -> p t g", g=4)
                gb = group_b[j].rearrange("p (t g) -> p t g", g=4)
                first_max(ch, g, ga, route_max[j][:, :], const("first4"), 4)
                ch.link(nc.vector.scalar_tensor_tensor(g, ga, LOW, g, ALU.mult, ALU.add))
                first_max(ch, g, gb, route_max[j][:, :], const("first4"), 4)
                ch.link(nc.vector.tensor_tensor(group_a[j], group_a[j], group_b[j], ALU.add))
                ch.link(nc.vector.tensor_scalar(group_a[j], group_a[j], 1.0, -LOW, ALU.subtract, ALU.mult))
                ch.link(nc.vector.tensor_tensor(s16, s16, group_a[j].unsqueeze(2).to_broadcast([P, 16, 4]), ALU.add))
                choose_two(ch, j, sc[:, :, :], 16, const("first16"))
                ch.link(nc.vector.tensor_tensor(combine[j][:, :, :], chosen[j][:, 0, :, :], chosen[j][:, 1, :, :],
                                                ALU.add))
                nc.vector.tensor_tensor(combine[j][:, :, :], combine[j][:, :, :], logit[j][:, :, :], ALU.mult)\
                    .then_inc(l0m_route, 1)
            for u, (p, j) in enumerate(l0m_units):
                dve.wait_ge(l0m_silu, u + 1)
                if u >= J:
                    dve.wait_ge(l0m_back, u - J + 1)
                mid = m0_mid[j] if p < PAIRS else m0_hid[j]
                ins = nc.vector.scalar_tensor_tensor(mid, bank(j, 1), col(f"be3_{p}" if p < PAIRS else "bs3"),
                                                     m0_gate[j], ALU.add, ALU.mult)
                if p < PAIRS:
                    ch.link(ins)
                    ins = nc.vector.tensor_tensor(m0_hid[j], bank(j, 2), mid, ALU.mult)
                ins.then_inc(l0m_hid, 1)
            for j in range(J):
                dve.wait_ge(l0m_y, j + 1)
                nc.vector.scalar_tensor_tensor(XT[j][:, :], FB[j][:, :], tg_sb[:, 4:5], XT[j][:, :],
                                               ALU.mult, ALU.add).then_inc(x_new, 1)

        def l0_moe_pool(pool):
            pool_norm(pool, "l0_moe")

        l1_prod = psem("l1_prod")
        l1_p = Order("kv", "q", "o")
        l1_act = psem("l1_act")
        l1_a = Order("k", "q", "ca", "y")
        l1_dve = psem("l1_dve")

        def l1_attn_pe(pe):
            for j in range(J):
                pe.wait_ge(x_new, x_blk("l0_moe", j))
                pe_norm_in(pe, "l1_in", j, XT[j][:, :])
            pe.wait_ge(loaded_later, 16 * len(LATER_LOADS))
            for j in range(J):
                nc.tensor.matmul(bank(j, 0)[:, 0:S2], blk("l1_k"), ctxT[j][:, :], start=True, stop=True)
                nc.tensor.matmul(bank(j, 1)[0:S2, 0:P], ctxT[j][:, :], blk("l1_v"), start=True, stop=True)\
                    .then_inc(l1_prod, 1)
            for j in range(J):
                pe_norm_out(pe, "l1_in", j)
            for j in range(J):
                pe.wait_ge(norm_T, norm("l1_in", j))
                nc.tensor.matmul(bank(j, 3), blk("l1_q"), FA[j][:, :], start=True, stop=True).then_inc(l1_prod, 1)
            pe.wait_ge(l1_act, l1_a("q", J - 1))
            pe.wait_ge(l1_dve, J)
            att_pe(pe, "l1", FB)
            for j in range(J):
                pe.wait_ge(l1_act, l1_a("ca", j))
                nc.tensor.matmul(bank(j, 2), blk("l1_o"), FC[j][:, :], start=True, stop=True).then_inc(l1_prod, 1)

        def l1_attn_act(act):
            for j in range(J):
                act.wait_ge(l1_prod, l1_p("kv", j))
                nc.scalar.activation(k_feat[j], bank(j, 0)[:, 0:S2], ACT.Copy).then_inc(l1_act, 1)
            act_norm(act, "l1_in", FA)
            for j in range(J):
                act.wait_ge(l1_prod, l1_p("q", j))
                nc.scalar.activation(FB[j][:, :], bank(j, 3), ACT.Copy).then_inc(l1_act, 1)
            att_act(act, "l1", 1.0 / float(P) ** 0.5)
            for j in range(J):
                act.wait_ge(att_pv, att_halves("l1"))
                nc.scalar.activation(FC[j][:, :], psum[:, 6 + j, :], ACT.Copy).then_inc(l1_act, 1)
            for j in range(J):
                act.wait_ge(l1_prod, l1_p("o", j))
                nc.scalar.activation(FA[j][:, :], bank(j, 2), ACT.Identity, bias=col("l1_bo")).then_inc(l1_act, 1)

        def l1_attn_dve(dve, ch):
            for j in range(J):
                dve.wait_ge(l1_act, l1_a("k", j))
                dve.wait_ge(att_zeros, 2)
                ch.tag(nc.vector.tensor_copy(head_blocks(j, 8), bank(j, 1)[0:S2, 0:P].rearrange("p (h d) -> p h d", d=8)))
                ch.tag(nc.vector.tensor_scalar(blocked[j], mask_in[j], 0.0, -1e20, ALU.is_equal, ALU.mult))
                nc.vector.tensor_tensor(k_heads[j].rearrange("p (h s) -> p h s", s=S2),
                                        k_feat[j].unsqueeze(1).to_broadcast([P, 16, S2]),
                                        const("heads8").unsqueeze(2).to_broadcast([P, 16, S2]), ALU.mult)\
                    .then_inc(l1_dve, 1)
            dve_norm(dve, ch, "l1_in")
            att_dve(dve, ch, "l1")
            for j in range(J):
                dve.wait_ge(l1_act, l1_a("y", j))
                nc.vector.scalar_tensor_tensor(XT[j][:, :], FA[j][:, :], tg_sb[:, 1:2], XT[j][:, :],
                                               ALU.mult, ALU.add).then_inc(x_new, 1)

        def l1_attn_pool(pool):
            pool.wait_ge(x_new, x_blk("l0_moe", J - 1))
            for j in range(J):
                last = nc.gpsimd.memset(v_heads[j], 0.0)
            last.then_inc(att_zeros, 1)
            pool_norm(pool, "l1_in")
            att_pool(pool, "l1")

        E8 = 8
        l1m_prod = psem("l1m_prod")
        l1m_p = Order("gate", "count", "turn")
        l1m_route = psem("l1m_route")
        l1m_r = Order("chosen", "combine")
        l1m_ct = psem("l1m_ct")
        l1m_front = psem("l1m_front")
        l1m_act = psem("l1m_act")
        l1m_back = psem("l1m_back")
        l1m_sum = psem("l1m_sum")
        e8_units = [(e, j) for e in range(E8) for j in range(J)]
        used[0] = 2 * T
        m1_hid = [take(4 * T) for _ in range(2)]
        m1_w = [take(T) for _ in range(2)]
        m1_part = [take(T) for _ in range(2)]

        def l1_moe_pe(pe):
            for j in range(J):
                pe.wait_ge(x_new, x_blk("l1_attn", j))
                pe_norm_in(pe, "l1_moe", j, XT[j][:, :])
            for j in range(J):
                pe_norm_out(pe, "l1_moe", j)
            for j in range(J):
                pe.wait_ge(norm_T, norm("l1_moe", j))
                pe_logits(pe, j, FA[j], l1_gate_sb[:, :], E8).then_inc(l1m_prod, 1)
            for j in range(J):
                pe.wait_ge(l1m_route, l1m_r("chosen", j))
                for t in range(NT):
                    for s in range(t + 1):
                        nc.tensor.matmul(bank(j, 1)[:, t * 16:(t + 1) * 16], const("upto" if s == t else "ones"),
                                         chosen[j][:, :, s, 0:E8], start=(s == 0), stop=(s == t))
                for s in range(NT):
                    last = nc.tensor.matmul(bank(j, 1)[:, 64:80], const("ones"), chosen[j][:, :, s, 0:E8],
                                            start=(s == 0), stop=(s == NT - 1))
                last.then_inc(l1m_prod, 1)
            for j in range(J):
                pe.wait_ge(l1m_route, l1m_r("combine", j))
                pe_turn_combine(pe, j, E8).then_inc(l1m_prod, 1)

            def front(u):
                e, j = e8_units[u]
                if u >= 1:
                    pe.wait_ge(l1m_act, u)
                else:
                    pe.wait_ge(l1m_ct, J)
                for c in range(4):
                    nc.tensor.matmul(psum[:, c, :], l1w1_sb[:, e, c * P:(c + 1) * P], FA[j][:, :],
                                     start=True, stop=True)
                nc.tensor.matmul(psum[:, 4 + u % 2, :], expert_pick(e), combine_t[j][0:E8, :],
                                 start=True, stop=True).then_inc(l1m_front, 1)

            def back(u):
                e, j = e8_units[u]
                pe.wait_ge(l1m_act, u + 1)
                if u >= 2:
                    pe.wait_ge(l1m_sum, u - 1)
                for c in range(4):
                    last = nc.tensor.matmul(psum[:, 6 + u % 2, :], l1w2_sb[:, e, c, :],
                                            m1_hid[u % 2][:, c * T:(c + 1) * T], start=(c == 0), stop=(c == 3))
                last.then_inc(l1m_back, 1)

            for u in range(len(e8_units)):
                front(u)
                if u >= 1:
                    back(u - 1)
            back(len(e8_units) - 1)

        def l1_moe_act(act):
            act_norm(act, "l1_moe", FA)
            route_exp(act, "l1")
            for j in range(J):
                act.wait_ge(l1m_prod, l1m_p("turn", j))
                nc.scalar.activation(combine_t[j][0:E8, :], bank(j, 1)[0:E8, :], ACT.Copy).then_inc(l1m_ct, 1)
            for u, (e, j) in enumerate(e8_units):
                act.wait_ge(l1m_front, u + 1)
                if u >= 2:
                    act.wait_ge(l1m_back, u - 1)
                    act.wait_ge(l1m_sum, u - 1)
                for c in range(4):
                    nc.scalar.activation(m1_hid[u % 2][:, c * T:(c + 1) * T], psum[:, c, :], ACT.Relu,
                                         bias=col(f"l1_b1_{e}_{c}"))
                nc.scalar.activation(m1_w[u % 2], psum[:, 4 + u % 2, :], ACT.Copy).then_inc(l1m_act, 1)

        def l1_moe_dve(dve, ch):
            dve_norm(dve, ch, "l1_moe")
            for j in range(J):
                dve.wait_ge(l1m_prod, l1m_p("gate", j))
                route_centre(ch, "l1", j, bank(j, 0)[:, 0:NT * E8].rearrange("p (t e) -> p t e", e=E8), E8,
                             rows_sb[:, 16:24])
            for j in range(J):
                route_softmax(dve, ch, "l1", j, E8)
                sc = score[j][:, :, 0:E8]
                ch.link(nc.vector.tensor_copy(sc, logit[j][:, :, 0:E8]))
                first_max(ch, sc, chosen[j][:, 0, :, 0:E8], route_max[j][:, :], const("first8"), E8)
                ch.link(nc.vector.scalar_tensor_tensor(sc, chosen[j][:, 0, :, 0:E8], LOW, sc, ALU.mult, ALU.add))
                first_max(ch, sc, chosen[j][:, 1, :, 0:E8], route_max[j][:, :], const("first8"), E8)
                nc.vector.tensor_copy(combine[j][:, :, 0:E8], logit[j][:, :, 0:E8]).then_inc(l1m_route, 1)
            for j in range(J):
                dve.wait_ge(l1m_prod, l1m_p("count", j))
                place = score[j][:, :, :]
                ch.link(nc.vector.tensor_tensor(place, bank(j, 1)[:, 0:64].rearrange("p (t c) -> p t c", c=16),
                                                carry_sb[:, :].unsqueeze(1).to_broadcast([P, NT, 16]), ALU.add))
                ch.link(nc.vector.tensor_scalar(place, place, float(CAP), None, ALU.is_le))
                both = chosen[j][:, :, :, 0:E8]
                ch.link(nc.vector.tensor_tensor(both, both, place.rearrange("p t (c e) -> p c t e", c=2), ALU.mult))
                ch.link(nc.vector.tensor_tensor(combine[j][:, :, 0:E8], both[:, 0], both[:, 1], ALU.add))
                ch.link(nc.vector.tensor_tensor(carry_sb[:, :], bank(j, 1)[:, 64:80], carry_sb[:, :], ALU.add))
                nc.vector.tensor_tensor(combine[j][:, :, 0:E8], combine[j][:, :, 0:E8], logit[j][:, :, 0:E8],
                                        ALU.mult).then_inc(l1m_route, 1)
            for u, (e, j) in enumerate(e8_units):
                if u >= 2:
                    dve.wait_ge(l1m_sum, u - 1)
                dve.wait_ge(l1m_back, u + 1)
                dst = FB[j][:, :] if e == 0 else m1_part[u % 2]
                ins = nc.vector.scalar_tensor_tensor(dst, psum[:, 6 + u % 2, :], col(f"l1_b2_{e}"), m1_w[u % 2],
                                                     ALU.add, ALU.mult)
                if e > 0:
                    ch.link(ins)
                    ins = nc.vector.tensor_tensor(FB[j][:, :], FB[j][:, :], m1_part[u % 2], ALU.add)
                ins.then_inc(l1m_sum, 1)
            for j in range(J):
                dve.wait_ge(l1m_sum, len(e8_units))
                nc.vector.scalar_tensor_tensor(XT[j][:, :], FB[j][:, :], tg_sb[:, 5:6], XT[j][:, :],
                                               ALU.mult, ALU.add).then_inc(x_new, 1)

        def l1_moe_pool(pool):
            pool_norm(pool, "l1_moe")

        L2H, KC = 8, 5
        HD = 64
        used[0] = 0
        v_wide = take(KC * L2H * P).rearrange("p (k h n) -> p k h n", k=KC, h=L2H)
        k_t = take(4 * (T + S2)).rearrange("p (c n) -> p c n", c=4)
        k_sq = [take(T + S2) for _ in range(2)]
        q_tok = take(4 * T).rearrange("p (t n) -> p t n", t=NT)
        o_t = q_tok
        q_t = take(4 * T).rearrange("p (c n) -> p c n", c=4)
        p_t = [take(T) for _ in range(3)]
        q_sq = p_t[0:2]
        recip = take(T)
        kv_ctx = [sb(f"kv_ctx{j}", [P, S2]) for j in range(J)]
        q_len = sb("q_len", [P, NT, L2H])
        q_inv = sb("q_inv", [P, NT, L2H])
        k_len = sb("k_len", [P, KC, L2H])
        k_inv = sb("k_inv", [P, KC, L2H])
        qk_scale = sb("qk_scale", [P, 1])
        qk_most = sb("qk_most", [P, 1])
        shift = sb("shift", [P, 1])
        shift_ctx = [sb(f"shift_ctx{j}", [S2, 1]) for j in range(J)]
        ctx_stats = [sb(f"ctx_stats{j}", [S2, 6]) for j in range(J)]
        ctx_mv = [sb(f"ctx_mv{j}", [S2, 2]) for j in range(J)]
        ctx_var = [sb(f"ctx_var{j}", [S2, 1]) for j in range(J)]
        ctx_rstd = [sb(f"ctx_rstd{j}", [S2, 1]) for j in range(J)]
        cn_var = psem("cn_var")
        cn_rstd = psem("cn_rstd")
        cn_xn = psem("cn_xn")
        cn_out = psem("cn_out")
        cn_T = psem("cn_T")
        l2_ones = psem("l2_ones")
        l2_q = psem("l2_q")
        l2_qsq = psem("l2_qsq")
        l2_qred = psem("l2_qred")
        l2_qlen = psem("l2_qlen")
        l2_qinv = psem("l2_qinv")
        l2_qn = psem("l2_qn")
        l2_qturn = psem("l2_qturn")
        l2_qt = psem("l2_qt")
        l2_k = psem("l2_k")
        l2_kact = psem("l2_kact")
        l2_klen = psem("l2_klen")
        l2_kmax = psem("l2_kmax")
        l2_kinv = psem("l2_kinv")
        l2_kscale = psem("l2_kscale")
        l2_v = psem("l2_v")
        l2_vw = psem("l2_vw")
        l2_s = psem("l2_s")
        l2_e = psem("l2_e")
        l2_o = psem("l2_o")
        l2_on = psem("l2_on")
        l2_y = psem("l2_y")
        l2_yT = psem("l2_yT")
        NU = L2H * KC

        def key_rows(kc):
            return P if kc < 4 else S2

        def key_cols(kc):
            return slice(kc * P, kc * P + key_rows(kc))

        def blk4(name):
            i = BLOCKS.index(name)
            return blocks_sb[:, i:i + 4, :].rearrange("p c n -> p (c n)")

        def l2_attn_pe(pe):
            for j in range(J):
                pe.wait_ge(x_new, x_blk("l1_moe", j))
                pe_norm_in(pe, "l2_in", j, XT[j][:, :])
            for j in range(J):
                pe_norm_out(pe, "l2_in", j)
            for j in range(J):
                pe.wait_ge(cn_xn, j + 1)
                nc.tensor.transpose(bank(j, 1)[:, 0:S2], ctx_tok[j][:, :], ident[0:S2, 0:S2]).then_inc(cn_out, 1)
            for j in range(J):
                pe.wait_ge(norm_T, norm("l2_in", j))
                pe_norm_in(pe, "l2_lat", j, FA[j][:, :])
            for j in range(J):
                pe_norm_out(pe, "l2_lat", j)
            for j in range(J):
                pe.wait_ge(norm_T, norm("l2_lat", J - 1))
                pe.wait_ge(cn_T, J)
                if j:
                    pe.wait_ge(l2_yT, j)
                for t in range(NT):
                    nc.tensor.matmul(psum[:, t, :], FB[j][:, t * P:(t + 1) * P], blk4("l2_q0"),
                                     start=True, stop=True).then_inc(l2_q, 1)

                def lengths(c):
                    pe.wait_ge(l2_kact, 4 * j + c + 1)
                    for kc in range(KC):
                        last = nc.tensor.matmul(psum[0:key_rows(kc), 7, kc * 8 + 2 * c:kc * 8 + 2 * c + 2],
                                                k_sq[c % 2][:, key_cols(kc)], const("halves"),
                                                start=True, stop=True)
                    last.then_inc(l2_klen, 1)

                for c in range(4):
                    if c >= 2:
                        pe.wait_ge(l2_kact, 4 * j + c - 1)
                    nc.tensor.matmul(psum[:, 4 + c % 2, :], blk(f"l2_k{c}"), FB[j][:, :], start=True, stop=True)
                    if c >= 1:
                        pe.wait_ge(l2_kact, 4 * j + c)
                    nc.tensor.matmul(psum[:, 6, 0:S2], blk(f"l2_k{c}"), kv_ctx[j][:, :],
                                     start=True, stop=True).then_inc(l2_k, 1)
                    if c >= 1:
                        lengths(c - 1)
                lengths(3)
                for kc in range(KC):
                    if kc >= 2:
                        pe.wait_ge(l2_vw, KC * j + kc - 1)
                    lhs = FB[j][:, key_cols(kc)] if kc < 4 else kv_ctx[j][:, :]
                    nc.tensor.matmul(psum[0:key_rows(kc), 4 + kc % 2, :], lhs, blk4("l2_v0"),
                                     start=True, stop=True).then_inc(l2_v, 1)
                pe.wait_ge(l2_qn, NT * (j + 1))
                for c in range(4):
                    for t in range(NT):
                        last = nc.tensor.transpose(psum[:, c, t * P:(t + 1) * P], q_tok[:, t, c * P:(c + 1) * P],
                                                   ident)
                    last.then_inc(l2_qturn, 1)

                def scores(n):
                    h, kc = n // KC, n % KC
                    if n < 4:
                        pe.wait_ge(l2_qt, 4 * j + 4)
                    else:
                        pe.wait_ge(l2_e, NU * j + n - 3)
                    r = slice(HD * (h % 2), HD * (h % 2) + HD)
                    nc.tensor.matmul(psum[0:key_rows(kc), n % 4, :], k_t[r, h // 2, key_cols(kc)],
                                     q_t[r, h // 2, :], start=True, stop=True).then_inc(l2_s, 1)

                def weighted(n):
                    h, kc = n // KC, n % KC
                    pe.wait_ge(l2_e, NU * j + n + 1)
                    if kc == 0 and h < 2:
                        pe.wait_ge(l2_vw, KC * (j + 1))
                        pe.wait_ge(l2_ones, 1)
                    elif kc == 0:
                        pe.wait_ge(l2_on, L2H * j + h - 1)
                    k = key_rows(kc)
                    nc.tensor.matmul(psum[:, 4 + h % 2, :], v_wide[0:k, kc, h, :], p_t[n % 3][0:k, :],
                                     start=(kc == 0), stop=(kc == KC - 1)).then_inc(l2_o, 1)

                for n in range(NU + 2):
                    if n < NU:
                        scores(n)
                    if n >= 2:
                        weighted(n - 2)
                pe.wait_ge(l2_on, L2H * (j + 1))
                for c in range(4):
                    last = nc.tensor.matmul(psum[:, 6, :], blk(f"l2_o{c}"), o_t[:, c, :], start=(c == 0), stop=(c == 3))
                last.then_inc(l2_y, 1)
            for j in range(J):
                pe.wait_ge(l2_yT, J)
                pe_norm_in(pe, "l2_out", j, FA[j][:, :])
            for j in range(J):
                pe_norm_out(pe, "l2_out", j)

        def l2_attn_act(act):
            act_norm(act, "l2_in", FA)
            for j in range(J):
                act.wait_ge(cn_out, j + 1)
                nc.scalar.activation(kv_ctx[j][:, :], bank(j, 1)[:, 0:S2], ACT.Identity, bias=col("l2_xb"),
                                     scale=col("l2_xg")).then_inc(cn_T, 1)
            act_norm(act, "l2_lat", FB, "l2_lg", "l2_lb")
            for j in range(J):
                for t in range(NT):
                    act.wait_ge(l2_q, NT * j + t + 1)
                    if t >= 2:
                        act.wait_ge(l2_qred, NT * j + t - 1)
                    nc.scalar.activation(q_sq[t % 2], psum[:, t, :], ACT.Square).then_inc(l2_qsq, 1)
                for c in range(4):
                    act.wait_ge(l2_k, 4 * j + c + 1)
                    if c >= 2:
                        act.wait_ge(l2_klen, 4 * j + c - 1)
                    nc.scalar.activation(k_t[:, c, 0:T], psum[:, 4 + c % 2, :], ACT.Identity, scale=qk_scale[:, :])
                    nc.scalar.activation(k_t[:, c, T:T + S2], psum[:, 6, 0:S2], ACT.Identity, scale=qk_scale[:, :])
                    nc.scalar.activation(k_sq[c % 2][:, 0:T], psum[:, 4 + c % 2, :], ACT.Square)
                    nc.scalar.activation(k_sq[c % 2][:, T:T + S2], psum[:, 6, 0:S2], ACT.Square).then_inc(l2_kact, 1)
                act.wait_ge(l2_kscale, j + 1)
                for n in range(NU):
                    h, kc = n // KC, n % KC
                    k = key_rows(kc)
                    act.wait_ge(l2_s, NU * j + n + 1)
                    if n >= 3:
                        act.wait_ge(l2_o, NU * j + n - 2)
                    elif n < 2:
                        act.wait_ge(l2_qred, NT * (j + 1))
                    nc.scalar.activation(p_t[n % 3][0:k, :], psum[0:k, n % 4, :], ACT.Exp,
                                         bias=shift[:, :] if kc < 4 else shift_ctx[j][:, :],
                                         scale=k_inv[0:k, kc, h:h + 1]).then_inc(l2_e, 1)
                act.wait_ge(l2_y, j + 1)
                nc.scalar.activation(FA[j][:, :], psum[:, 6, :], ACT.Copy).then_inc(l2_yT, 1)
            act_norm(act, "l2_out", FB, "l2_og", "l2_ob")

        def l2_attn_dve(dve, ch):
            for j in range(J):
                ch.link(nc.vector.bn_stats(ctx_stats[j][:, :], ctx_tok[j][:, :]))
                ch.link(nc.vector.bn_aggr(ctx_mv[j][:, :], ctx_stats[j][:, :]))
                ch.tag(nc.vector.tensor_scalar(shift_ctx[j][:, :], key_ok[j][:, :], 0.0, LOW, ALU.is_equal, ALU.mult))
                nc.vector.tensor_scalar(ctx_var[j][:, :], ctx_mv[j][:, 1:2], EPS, None, ALU.add).then_inc(cn_var, 1)
                ch.settle()
                ch.tag(nc.vector.tensor_tensor(shift_ctx[j][:, :], shift_ctx[j][:, :], shift[0:S2, :], ALU.add))
            for j in range(J):
                dve.wait_ge(cn_rstd, j + 1)
                nc.vector.tensor_scalar(ctx_tok[j][:, :], ctx_tok[j][:, :], ctx_mv[j][:, 0:1], ctx_rstd[j][:, :],
                                        ALU.subtract, ALU.mult).then_inc(cn_xn, 1)
            dve_norm(dve, ch, "l2_in")
            dve_norm(dve, ch, "l2_lat")
            for j in range(J):
                for t in range(NT):
                    dve.wait_ge(l2_qsq, NT * j + t + 1)
                    nc.vector.tensor_reduce(q_len[:, t, :], q_sq[t % 2].rearrange("p (h d) -> p h d", d=HD),
                                            AX.X, ALU.add).then_inc(l2_qred, 1)
                dve.wait_ge(l2_qred, NT * (j + 1))
                nc.vector.tensor_scalar(q_len[:, :, :], q_len[:, :, :], 1e-24, None, ALU.max).then_inc(l2_qlen, 1)
                dve.wait_ge(l2_qinv, j + 1)
                if j:
                    dve.wait_ge(l2_y, j)
                for t in range(NT):
                    nc.vector.tensor_tensor(q_tok[:, t, :].rearrange("p (h d) -> p h d", d=HD),
                                            psum[:, t, :].rearrange("p (h d) -> p h d", d=HD),
                                            q_inv[:, t, :].unsqueeze(2).to_broadcast([P, L2H, HD]),
                                            ALU.mult).then_inc(l2_qn, 1)
                dve.wait_ge(l2_klen, 4 * (j + 1))
                ch.tag(nc.vector.tensor_scalar(k_len[:, 0:4, :],
                                               psum[:, 7, 0:32].rearrange("p (k h) -> p k h", h=8), 1e-24, None,
                                               ALU.max))
                nc.vector.tensor_scalar(k_len[0:S2, 4, :], psum[0:S2, 7, 32:40], 1e-24, None, ALU.max)\
                    .then_inc(l2_kmax, 1)
                for kc in range(KC):
                    k = key_rows(kc)
                    dve.wait_ge(l2_v, KC * j + kc + 1)
                    v = psum[0:k, 4 + kc % 2, :].rearrange("p (h two d) -> p h two d", two=2, d=HD)
                    dst = v_wide[0:k, kc, :, :].rearrange("p (h two) n -> p h two n", two=2)
                    ch.tag(nc.vector.tensor_copy(dst[:, :, 0, 0:HD], v[:, :, 0, :]))
                    nc.vector.tensor_copy(dst[:, :, 1, HD:P], v[:, :, 1, :]).then_inc(l2_vw, 1)
                dve.wait_ge(l2_kinv, j + 1)
                ch.tag(nc.vector.tensor_scalar(k_inv[:, 0:4, :], k_inv[:, 0:4, :], 8.0, None, ALU.mult))
                nc.vector.tensor_scalar(k_inv[0:S2, 4, :], k_inv[0:S2, 4, :], 8.0, None, ALU.mult)\
                    .then_inc(l2_kscale, 1)
                for c in range(4):
                    dve.wait_ge(l2_qturn, 4 * j + c + 1)
                    nc.vector.tensor_copy(q_t[:, c, :], psum[:, c, :]).then_inc(l2_qt, 1)
                for h in range(L2H):
                    dve.wait_ge(l2_o, NU * j + KC * (h + 1))
                    o = slice(HD * (h % 2), HD * (h % 2) + HD)
                    s = slice(HD - HD * (h % 2), P - HD * (h % 2))
                    ch.link(nc.vector.reciprocal(recip[o, :], psum[s, 4 + h % 2, :]))
                    nc.vector.tensor_tensor(o_t[o, h // 2, :], psum[o, 4 + h % 2, :], recip[o, :], ALU.mult)\
                        .then_inc(l2_on, 1)
            dve_norm(dve, ch, "l2_out")
            for j in range(J):
                dve.wait_ge(norm_T, norm("l2_out", j))
                nc.vector.scalar_tensor_tensor(XT[j][:, :], FB[j][:, :], tg_sb[:, 2:3], XT[j][:, :],
                                               ALU.mult, ALU.add).then_inc(x_new, 1)

        def l2_attn_pool(pool):
            for j in range(J):
                pool.wait_ge(cn_var, j + 1)
                nc.gpsimd.tensor_tensor(ctx_rstd[j][:, :], ctx_var[j][:, :], half_sb[0:S2, 0:1], ALU.pow)\
                    .then_inc(cn_rstd, 1)
            pool_norm(pool, "l2_in")
            pool.wait_ge(x_new, x_blk("l1_moe", J - 1))
            ones = v_wide.rearrange("p k (h two) n -> p (k h) (two n)", two=2)[:, :, HD:HD + P]
            nc.gpsimd.memset(ones, 1.0).then_inc(l2_ones, 1)
            pool_norm(pool, "l2_lat")
            half = half_sb[:, 0:8]
            for j in range(J):
                pool.wait_ge(l2_qlen, j + 1)
                nc.gpsimd.tensor_tensor(q_inv[:, :, :], q_len[:, :, :], half.unsqueeze(1).to_broadcast([P, NT, 8]),
                                        ALU.pow).then_inc(l2_qinv, 1)
                pool.wait_ge(l2_kmax, j + 1)
                if j:
                    pool.wait_ge(l2_e, NU * j)
                nc.gpsimd.tensor_tensor(k_inv[0:S2, 4, :], k_len[0:S2, 4, :], half[0:S2], ALU.pow)\
                    .then_inc(chain_p, 1)
                nc.gpsimd.tensor_tensor(k_inv[:, 0:4, :], k_len[:, 0:4, :], half.unsqueeze(1).to_broadcast([P, 4, 8]),
                                        ALU.pow).then_inc(l2_kinv, 1)
            pool_norm(pool, "l2_out")

        HC = 3
        l2m_prod = psem("l2m_prod")
        l2m_p = Order("gate", "turn")
        l2m_route = psem("l2m_route")
        l2m_ct = psem("l2m_ct")
        l2m_w = psem("l2m_w")
        l2m_x = psem("l2m_x")
        l2m_front = psem("l2m_front")
        l2m_silu = psem("l2m_silu")
        l2m_hid = psem("l2m_hid")
        l2m_back = psem("l2m_back")
        used[0] = 2 * T
        m2_x = [take(T) for _ in range(2)]
        m2_silu = [take(T) for _ in range(2)]
        m2_hid = [take(T) for _ in range(2)]

        def hid_rows(c):
            return min(P, HID - c * P)

        def l2_moe_pe(pe):
            for j in range(J):
                pe.wait_ge(x_new, x_blk("l2_attn", j))
                pe_norm_in(pe, "l2_moe", j, XT[j][:, :])
            for j in range(J):
                pe_norm_out(pe, "l2_moe", j)
            for j in range(J):
                pe.wait_ge(norm_T, norm("l2_moe", j))
                pe_logits(pe, j, FA[j], l2_gate_sb[:, :], E8).then_inc(l2m_prod, 1)
            for j in range(J):
                pe.wait_ge(l2m_route, j + 1)
                pe_turn_combine(pe, j, E8).then_inc(l2m_prod, 1)

            def spread(u):
                e, j = e8_units[u]
                if u < 2:
                    pe.wait_ge(l2m_ct, J)
                else:
                    pe.wait_ge(l2m_x, u - 1)
                nc.tensor.matmul(psum[:, 4 + u % 2, :], expert_pick(e), combine_t[j][0:E8, :],
                                 start=True, stop=True).then_inc(l2m_w, 1)

            def front(n):
                u, c = n // HC, n % HC
                e, j = e8_units[u]
                m = hid_rows(c)
                if c == 0:
                    pe.wait_ge(l2m_x, u + 1)
                if n >= 2:
                    pe.wait_ge(l2m_hid, n - 1)
                at = slice(c * P, c * P + m)
                b = 2 * (n % 2)
                nc.tensor.matmul(psum[0:m, b, :], l2w1_sb[:, e, at], m2_x[u % 2], start=True, stop=True)
                nc.tensor.matmul(psum[0:m, b + 1, :], l2w3_sb[:, e, at], m2_x[u % 2], start=True, stop=True)\
                    .then_inc(l2m_front, 1)

            def back(n):
                u, c = n // HC, n % HC
                e, j = e8_units[u]
                m = hid_rows(c)
                pe.wait_ge(l2m_hid, n + 1)
                nc.tensor.matmul(psum[:, 6 + j, :], l2w2_sb[0:m, e, c, :], m2_hid[n % 2][0:m, :],
                                 start=(e == 0 and c == 0), stop=(e == E8 - 1 and c == HC - 1)).then_inc(l2m_back, 1)

            units = len(e8_units)
            spread(0)
            for n in range(units * HC):
                front(n)
                if n % HC == 1 and n // HC + 1 < units:
                    spread(n // HC + 1)
                if n >= 1:
                    back(n - 1)
            back(units * HC - 1)

        def l2_moe_act(act):
            act_norm(act, "l2_moe", FA)
            route_exp(act, "l2")
            for j in range(J):
                act.wait_ge(l2m_prod, l2m_p("turn", j))
                nc.scalar.activation(combine_t[j][0:E8, :], bank(j, 1)[0:E8, :], ACT.Copy).then_inc(l2m_ct, 1)
            for n in range(len(e8_units) * HC):
                m = hid_rows(n % HC)
                act.wait_ge(l2m_front, n + 1)
                if n >= 2:
                    act.wait_ge(l2m_hid, n - 1)
                nc.scalar.activation(m2_silu[n % 2][0:m, :], psum[0:m, 2 * (n % 2), :], ACT.Silu).then_inc(l2m_silu, 1)

        def l2_moe_dve(dve, ch):
            dve_norm(dve, ch, "l2_moe")
            for j in range(J):
                dve.wait_ge(l2m_prod, l2m_p("gate", j))
                route_centre(ch, "l2", j, bank(j, 0)[:, 0:NT * E8].rearrange("p (t e) -> p t e", e=E8), E8)
            for j in range(J):
                route_softmax(dve, ch, "l2", j, E8)
                sc = score[j][:, :, 0:E8]
                ch.link(nc.vector.tensor_tensor(sc, logit[j][:, :, 0:E8],
                                                rows_sb[:, 24:32].unsqueeze(1).to_broadcast([P, NT, E8]), ALU.add))
                choose_two(ch, j, sc, E8, const("first8"))
                ch.link(nc.vector.tensor_tensor(combine[j][:, :, 0:E8], chosen[j][:, 0, :, 0:E8],
                                                chosen[j][:, 1, :, 0:E8], ALU.add))
                nc.vector.tensor_tensor(combine[j][:, :, 0:E8], combine[j][:, :, 0:E8], logit[j][:, :, 0:E8],
                                        ALU.mult).then_inc(l2m_route, 1)
            units = len(e8_units)

            def scale_input(u):
                e, j = e8_units[u]
                dve.wait_ge(l2m_w, u + 1)
                if u >= 2:
                    dve.wait_ge(l2m_front, HC * (u - 1))
                nc.vector.tensor_tensor(m2_x[u % 2], psum[:, 4 + u % 2, :], FA[j][:, :], ALU.mult).then_inc(l2m_x, 1)

            scale_input(0)
            for n in range(units * HC):
                m = hid_rows(n % HC)
                if n % HC == 1 and n // HC + 1 < units:
                    scale_input(n // HC + 1)
                dve.wait_ge(l2m_silu, n + 1)
                if n >= 2:
                    dve.wait_ge(l2m_back, n - 1)
                nc.vector.tensor_tensor(m2_hid[n % 2][0:m, :], psum[0:m, 2 * (n % 2) + 1, :], m2_silu[n % 2][0:m, :],
                                        ALU.mult).then_inc(l2m_hid, 1)
            for j in range(J):
                dve.wait_ge(l2m_back, units * HC)
                nc.vector.scalar_tensor_tensor(XT[j][:, :], psum[:, 6 + j, :], tg_sb[:, 6:7], XT[j][:, :],
                                               ALU.mult, ALU.add).then_inc(x_new, 1)

        def l2_moe_pool(pool):
            pool_norm(pool, "l2_moe")

        INV_SQRT8 = 1.0 / 8.0 ** 0.5
        l3_prod = psem("l3_prod")
        l3_p = Order("qkv", "row", "qk2", "s2", "turn2", "z2", "f1", "f2")
        l3_act = psem("l3_act")
        l3_a = Order("qk", "qk2", "exp2", "turn2", "f1")
        l3_dve = psem("l3_dve")
        l3_d = Order("v", "pad", "r1", "v2", "e2", "w2", "r2", "r3")
        s3_score = psem("s3_score")
        s3_max = psem("s3_max")
        s3_exp = psem("s3_exp")
        s3_norm = psem("s3_norm")
        s3_turn = psem("s3_turn")
        s3_move = psem("s3_move")
        s3_z = psem("s3_z")
        s3_units = [(j, t) for j in range(J) for t in range(NT)]
        used[0] = 0
        v1 = [take(NT * P).rearrange("p (t n) -> p t n", t=NT) for _ in range(J)]
        pad = [take(T) for _ in range(J)]
        s3_e = [take(T) for _ in range(2)]
        s3_p = [take(T) for _ in range(2)]
        s3_m = [take(1) for _ in range(2)]
        s3_sum = [take(1) for _ in range(2)]
        count = [take(1) for _ in range(J)]
        k2 = [take(S2) for _ in range(J)]
        v2 = [take(P, S2) for _ in range(J)]
        e2 = [take(NT * S2).rearrange("p (t s) -> p t s", t=NT) for _ in range(J)]
        p2 = [take(T, S2) for _ in range(J)]
        max2 = [take(NT) for _ in range(J)]

        def l3_attn_pe(pe):
            for j in range(J):
                pe.wait_ge(x_new, x_blk("l2_moe", j))
                pe_norm_in(pe, "l3_in", j, XT[j][:, :])
            for j in range(J):
                pe_norm_out(pe, "l3_in", j)
            for j in range(J):
                pe.wait_ge(norm_T, norm("l3_in", j))
                nc.tensor.matmul(bank(j, 0), blk("l3_q1"), FA[j][:, :], start=True, stop=True)
                nc.tensor.matmul(bank(j, 1), blk("l3_k1"), FA[j][:, :], start=True, stop=True)
                for t in range(NT):
                    last = nc.tensor.matmul(bank(j, 3)[:, t * P:(t + 1) * P], FA[j][:, t * P:(t + 1) * P],
                                            blk("l3_v1"), start=True, stop=True)
                last.then_inc(l3_prod, 1)
            for j in range(J):
                pe.wait_ge(l3_act, l3_a("qk", j))
                nc.tensor.matmul(bank(j, 2), FB[j][:, 0:1].to_broadcast([P, P]), FC[j][:, :],
                                 start=True, stop=True).then_inc(l3_prod, 1)

            def scores(u):
                j, t = s3_units[u]
                if u >= 2:
                    pe.wait_ge(s3_max, u - 1)
                k = (t + 1) * P
                nc.tensor.matmul(psum[:, u % 2, 0:k], FB[j][:, t * P:k], FC[j][:, 0:k], start=True, stop=True)\
                    .then_inc(s3_score, 1)

            def outputs_of(u):
                j, t = s3_units[u]
                pe.wait_ge(s3_move, u + 1)
                for s in range(t + 1):
                    last = nc.tensor.matmul(psum[:, 4 + j, t * P:(t + 1) * P], v1[j][:, s, :],
                                            s3_p[u % 2][:, s * P:(s + 1) * P], start=(s == 0), stop=(s == t))
                last.then_inc(s3_z, 1)

            pe.wait_ge(l3_dve, l3_d("pad", J - 1))
            scores(0)
            scores(1)
            for u, (j, t) in enumerate(s3_units):
                pe.wait_ge(s3_norm, u + 1)
                if u >= 2:
                    pe.wait_ge(s3_move, u - 1)
                for s in range(t + 1):
                    last = nc.tensor.transpose(psum[:, 2 + u % 2, s * P:(s + 1) * P], s3_e[u % 2][:, s * P:(s + 1) * P],
                                               ident)
                last.then_inc(s3_turn, 1)
                if u + 2 < len(s3_units):
                    scores(u + 2)
                if u >= 1:
                    outputs_of(u - 1)
            outputs_of(len(s3_units) - 1)
            for j in range(J):
                pe.wait_ge(l3_dve, l3_d("r1", j))
                if j == 0:
                    pe.wait_ge(s3_move, len(s3_units))
                pe_norm_in(pe, "l3_1", j, FB[j][:, :])
            for j in range(J):
                pe_norm_out(pe, "l3_1", j)
            for j in range(J):
                pe.wait_ge(norm_T, norm("l3_1", j))
                nc.tensor.matmul(bank(j, 0), blk("l3_q2"), FA[j][:, :], start=True, stop=True)
                nc.tensor.matmul(bank(j, 1)[:, 0:S2], blk("l3_k2"), ctxT[j][:, :], start=True, stop=True)
                nc.tensor.matmul(bank(j, 1)[0:S2, P:2 * P], ctxT[j][:, :], blk("l3_v2"), start=True, stop=True)\
                    .then_inc(l3_prod, 1)
            for j in range(J):
                pe.wait_ge(l3_act, l3_a("qk2", j))
                nc.tensor.matmul(bank(j, 2)[:, 0:S2], FB[j][:, 0:1].to_broadcast([P, P]), k2[j],
                                 start=True, stop=True)
                for t in range(NT):
                    last = nc.tensor.matmul(bank(j, 3)[:, t * S2:(t + 1) * S2], FB[j][:, t * P:(t + 1) * P], k2[j],
                                            start=True, stop=True)
                last.then_inc(l3_prod, 1)
            for j in range(J):
                pe.wait_ge(l3_dve, l3_d("w2", j))
                for t in range(NT):
                    last = nc.tensor.transpose(bank(j, 0)[0:S2, t * P:(t + 1) * P], e2[j][:, t, :], ident)
                last.then_inc(l3_prod, 1)
            for j in range(J):
                pe.wait_ge(l3_act, l3_a("turn2", j))
                nc.tensor.matmul(bank(j, 1), v2[j], p2[j], start=True, stop=True).then_inc(l3_prod, 1)
            for j in range(J):
                pe.wait_ge(l3_dve, l3_d("r2", j))
                pe_norm_in(pe, "l3_2", j, FB[j][:, :])
            for j in range(J):
                pe_norm_out(pe, "l3_2", j)
            for j in range(J):
                pe.wait_ge(norm_T, norm("l3_2", j))
                nc.tensor.matmul(bank(j, 0), blk("l3_f1"), FA[j][:, :], start=True, stop=True).then_inc(l3_prod, 1)
            for j in range(J):
                pe.wait_ge(l3_act, l3_a("f1", j))
                nc.tensor.matmul(bank(j, 1), blk("l3_f2"), FC[j][:, :], start=True, stop=True).then_inc(l3_prod, 1)
            for j in range(J):
                pe.wait_ge(l3_dve, l3_d("r3", j))
                pe_norm_in(pe, "l3_3", j, FB[j][:, :])
            for j in range(J):
                pe_norm_out(pe, "l3_3", j)

        def l3_attn_act(act):
            act_norm(act, "l3_in", FA)
            for j in range(J):
                act.wait_ge(l3_prod, l3_p("qkv", j))
                nc.scalar.activation(FB[j][:, :], bank(j, 0), ACT.Copy)
                nc.scalar.activation(FC[j][:, :], bank(j, 1), ACT.Copy).then_inc(l3_act, 1)

            for u, (j, t) in enumerate(s3_units):
                k = (t + 1) * P
                act.wait_ge(s3_max, u + 1)
                nc.scalar.activation(s3_e[u % 2][:, 0:k], s3_e[u % 2][:, 0:k], ACT.Exp, bias=s3_m[u % 2],
                                     scale=INV_SQRT8, accum_out=s3_sum[u % 2]).then_inc(s3_exp, 1)
                if u >= 1:
                    move3(act, u - 1)
            move3(act, len(s3_units) - 1)
            act_norm(act, "l3_1", FA, "l3_n1g", "l3_n1b")
            for j in range(J):
                act.wait_ge(l3_prod, l3_p("qk2", j))
                nc.scalar.activation(FB[j][:, :], bank(j, 0), ACT.Copy)
                nc.scalar.activation(k2[j], bank(j, 1)[:, 0:S2], ACT.Copy).then_inc(l3_act, 1)
            for j in range(J):
                act.wait_ge(l3_dve, l3_d("e2", j))
                nc.scalar.activation(e2[j], e2[j], ACT.Exp, scale=INV_SQRT8).then_inc(l3_act, 1)
            for j in range(J):
                act.wait_ge(l3_prod, l3_p("turn2", j))
                nc.scalar.activation(p2[j], bank(j, 0)[0:S2, :], ACT.Copy).then_inc(l3_act, 1)
            act_norm(act, "l3_2", FA, "l3_n2g", "l3_n2b")
            for j in range(J):
                act.wait_ge(l3_prod, l3_p("f1", j))
                nc.scalar.activation(FC[j][:, :], bank(j, 0), ACT.Relu, bias=col("l3_b1")).then_inc(l3_act, 1)
            act_norm(act, "l3_3", FA, "l3_n3g", "l3_n3b")

        def move3(act, u):
            j, t = s3_units[u]
            act.wait_ge(s3_turn, u + 1)
            if u >= 2:
                act.wait_ge(s3_z, u - 1)
            nc.scalar.activation(s3_p[u % 2][:, 0:(t + 1) * P], psum[:, 2 + u % 2, 0:(t + 1) * P], ACT.Copy)\
                .then_inc(s3_move, 1)

        def l3_attn_dve(dve, ch):
            def key_pad(j, row, n, dst):
                ch.link(nc.vector.tensor_scalar(dst, row, 0.0, None, ALU.not_equal))
                ch.link(nc.vector.tensor_reduce(count[j], dst, AX.X, ALU.add))
                return nc.vector.tensor_scalar(dst, const("keys")[:, 0:n], count[j], LOW, ALU.is_ge, ALU.mult)

            dve_norm(dve, ch, "l3_in")
            for j in range(J):
                dve.wait_ge(l3_prod, l3_p("qkv", j))
                nc.vector.tensor_copy(v1[j].rearrange("p t n -> p (t n)"), bank(j, 3)).then_inc(l3_dve, 1)
            for j in range(J):
                dve.wait_ge(l3_prod, l3_p("row", j))
                key_pad(j, bank(j, 2), T, pad[j]).then_inc(l3_dve, 1)
            dve.wait_ge(l3_dve, l3_d("pad", J - 1))

            def masked(u):
                j, t = s3_units[u]
                k = (t + 1) * P
                e = s3_e[u % 2]
                dve.wait_ge(s3_score, u + 1)
                if u >= 2:
                    dve.wait_ge(s3_turn, u - 1)
                ch.link(nc.vector.tensor_tensor(e[:, 0:k], psum[:, u % 2, 0:k], pad[j][:, 0:k], ALU.add))
                ch.link(nc.vector.tensor_tensor(e[:, t * P:k], e[:, t * P:k], const("causal"), ALU.add))
                ch.link(nc.vector.tensor_reduce(s3_m[u % 2], e[:, 0:k], AX.X, ALU.max))
                nc.vector.tensor_scalar(s3_m[u % 2], s3_m[u % 2], -INV_SQRT8, None, ALU.mult).then_inc(s3_max, 1)

            masked(0)
            for u, (j, t) in enumerate(s3_units):
                if u + 1 < len(s3_units):
                    masked(u + 1)
                dve.wait_ge(s3_exp, u + 1)
                ch.link(nc.vector.reciprocal(s3_sum[u % 2], s3_sum[u % 2]))
                k = (t + 1) * P
                nc.vector.tensor_scalar(s3_e[u % 2][:, 0:k], s3_e[u % 2][:, 0:k], s3_sum[u % 2], None, ALU.mult)\
                    .then_inc(s3_norm, 1)
            for j in range(J):
                dve.wait_ge(s3_z, NT * (j + 1))
                nc.vector.tensor_tensor(FB[j][:, :], psum[:, 4 + j, :], FA[j][:, :], ALU.add).then_inc(l3_dve, 1)
            dve_norm(dve, ch, "l3_1")
            for j in range(J):
                dve.wait_ge(l3_act, l3_a("qk2", j))
                nc.vector.tensor_copy(v2[j], bank(j, 1)[0:S2, P:2 * P]).then_inc(l3_dve, 1)
            for j in range(J):
                wide = [P, NT, S2]
                dve.wait_ge(l3_prod, l3_p("s2", j))
                ch.link(key_pad(j, bank(j, 2)[:, 0:S2], S2, pad[j][:, 0:S2]))
                ch.link(nc.vector.tensor_tensor(e2[j], bank(j, 3)[:, 0:NT * S2].rearrange("p (t s) -> p t s", t=NT),
                                                pad[j][:, 0:S2].unsqueeze(1).to_broadcast(wide), ALU.add))
                ch.link(nc.vector.tensor_reduce(max2[j], e2[j], AX.X, ALU.max))
                nc.vector.tensor_tensor(e2[j], e2[j], max2[j].unsqueeze(2).to_broadcast(wide), ALU.subtract)\
                    .then_inc(l3_dve, 1)
            for j in range(J):
                dve.wait_ge(l3_act, l3_a("exp2", j))
                ch.link(nc.vector.tensor_reduce(max2[j], e2[j], AX.X, ALU.add))
                ch.link(nc.vector.reciprocal(max2[j], max2[j]))
                nc.vector.tensor_tensor(e2[j], e2[j], max2[j].unsqueeze(2).to_broadcast([P, NT, S2]), ALU.mult)\
                    .then_inc(l3_dve, 1)
            for j in range(J):
                dve.wait_ge(l3_prod, l3_p("z2", j))
                nc.vector.tensor_tensor(FB[j][:, :], bank(j, 1), FA[j][:, :], ALU.add).then_inc(l3_dve, 1)
            dve_norm(dve, ch, "l3_2")
            for j in range(J):
                dve.wait_ge(l3_prod, l3_p("f2", j))
                nc.vector.scalar_tensor_tensor(FB[j][:, :], bank(j, 1), col("l3_b2"), FA[j][:, :],
                                               ALU.add, ALU.add).then_inc(l3_dve, 1)
            dve_norm(dve, ch, "l3_3")
            for j in range(J):
                dve.wait_ge(norm_T, norm("l3_3", j))
                nc.vector.scalar_tensor_tensor(XT[j][:, :], FA[j][:, :], tg_sb[:, 3:4], XT[j][:, :],
                                               ALU.mult, ALU.add).then_inc(x_new, 1)

        def l3_attn_pool(pool):
            for name in ("l3_in", "l3_1", "l3_2", "l3_3"):
                pool_norm(pool, name)

        l3f_prod = psem("l3f_prod")
        l3f_p = Order("up", "down")
        l3f_act = psem("l3f_act")
        l3f_a = Order("up", "y")
        used[0] = 0
        hidden3 = [take(4 * T) for _ in range(J)]

        def l3_ffn_pe(pe):
            for j in range(J):
                pe.wait_ge(x_new, x_blk("l3_attn", j))
                pe_norm_in(pe, "l3_ffn", j, XT[j][:, :])
            for j in range(J):
                pe_norm_out(pe, "l3_ffn", j)
            for j in range(J):
                pe.wait_ge(norm_T, norm("l3_ffn", j))
                for c in range(4):
                    last = nc.tensor.matmul(bank(j, c), blk(f"l3_up{c}"), FA[j][:, :], start=True, stop=True)
                last.then_inc(l3f_prod, 1)
            for j in range(J):
                pe.wait_ge(l3f_act, l3f_a("up", j))
                for c in range(4):
                    last = nc.tensor.matmul(bank(j, 0), blk(f"l3_down{c}"), hidden3[j][:, c * T:(c + 1) * T],
                                            start=(c == 0), stop=(c == 3))
                last.then_inc(l3f_prod, 1)

        def l3_ffn_act(act):
            act_norm(act, "l3_ffn", FA)
            for j in range(J):
                act.wait_ge(l3f_prod, l3f_p("up", j))
                for c in range(4):
                    last = nc.scalar.activation(hidden3[j][:, c * T:(c + 1) * T], bank(j, c), ACT.Gelu,
                                                bias=col(f"l3_bfc{c}"))
                last.then_inc(l3f_act, 1)
            for j in range(J):
                act.wait_ge(l3f_prod, l3f_p("down", j))
                nc.scalar.activation(FB[j][:, :], bank(j, 0), ACT.Identity, bias=col("l3_bproj")).then_inc(l3f_act, 1)

        def l3_ffn_dve(dve, ch):
            dve_norm(dve, ch, "l3_ffn")
            for j in range(J):
                dve.wait_ge(l3f_act, l3f_a("y", j))
                nc.vector.scalar_tensor_tensor(FC[j][:, :], FB[j][:, :], tg_sb[:, 7:8], XT[j][:, :],
                                               ALU.mult, ALU.add).then_inc(x_new, 1)

        def l3_ffn_pool(pool):
            pool_norm(pool, "l3_ffn")

        quant_most = sem("quant_most")
        quant_all = sem("quant_all")
        quant_lora = sem("quant_lora")
        quant = sb("quant", [P, 2, 4])
        ROUND = 1.5 * 2.0 ** 23

        def quant_w(n):
            return blk4(("l3_up0", "l3_down0")[n])

        def quant_pe(pe):
            nc.tensor.matmul(psum[:, 0, :], lora_sb[:, 0, 0:P], lora_sb[:, 1, 0:512], start=True, stop=True)
            for c in range(4):
                last = nc.tensor.matmul(psum[:, 1, c * P:(c + 1) * P], lora_sb[:, 0, P + c * P:2 * P + c * P],
                                        lora_sb[:, 1, 512:512 + P], start=True, stop=True)
            last.then_inc(quant_lora, 1)

        def quant_pool(pool):
            pool.wait_ge(quant_most, 2)
            for n in range(2):
                nc.gpsimd.partition_all_reduce(quant[:, n, 1:2], quant[:, n, 0:1], P, bass.bass_isa.ReduceOp.max)\
                    .then_inc(quant_all, 1)

        def quant_most_dve():
            for n in range(2):
                nc.vector.tensor_reduce(quant[:, n, 0:1], quant_w(n), AX.X, ALU.max, apply_absolute_value=True)\
                    .then_inc(quant_most, 1)

        def quant_dve(dve, ch):
            dve.wait_ge(quant_all, 2)
            both = quant[:, :, 1], quant[:, :, 2], quant[:, :, 3]
            ch.link(nc.vector.tensor_scalar(both[1], both[0], 1.0 / 127.0, None, ALU.mult))
            ch.link(nc.vector.reciprocal(both[2], both[1]))
            r = [arena[:, n * 512:(n + 1) * 512] for n in range(2)]
            w = [quant_w(n) for n in range(2)]
            scale = [quant[:, n, 2:3] for n in range(2)]
            inv = [quant[:, n, 3:4] for n in range(2)]

            def on_both(op):
                for n in range(2):
                    ch.tag(op(n))
                ch.settle()

            on_both(lambda n: nc.vector.tensor_scalar(r[n], w[n], inv[n], ROUND, ALU.mult, ALU.add))
            on_both(lambda n: nc.vector.tensor_scalar(r[n], r[n], ROUND, 127.0, ALU.subtract, ALU.min))
            on_both(lambda n: nc.vector.tensor_scalar(r[n], r[n], -128.0, scale[n], ALU.max, ALU.mult))
            on_both(lambda n: nc.vector.tensor_tensor(r[n], r[n], w[n], ALU.subtract))
            on_both(lambda n: nc.vector.tensor_tensor(w[n], w[n], r[n], ALU.add))
            dve.wait_ge(quant_lora, 1)
            on_both(lambda n: nc.vector.scalar_tensor_tensor(w[n], psum[:, n, :], 2.0, w[n], ALU.mult, ALU.add))
        INPUT_DMAS = 5 * J
        L0_LAST, L3_FIRST = BLOCKS.index("l1_q"), BLOCKS.index("l3_up0")
        FIRST_LOADS = [
            (gates_sb[:, :], gates), (cols_sb[:, :], cols), (rows_sb[:, :], rows), (consts_sb[:, :], consts),
            (blocks_sb[:, L3_FIRST:, :], blocks[:, L3_FIRST:, :]),
            (lora_sb[:, 0, 0:P], A_fc), (lora_sb[:, 1, 0:512], B_fc),
            (lora_sb[:, 0, P:P + 512], A_proj), (lora_sb[:, 1, 512:512 + P], B_proj),
            (blocks_sb[:, 0:L0_LAST, :], blocks[:, 0:L0_LAST, :])]
        L0_MOE_LOADS = [
            (pair_sel_sb[:, :], pair_sel), (gate16_sb[:, :], gate16), (be2_sb[:, :], be2),
            (we1_sb[:, :, :], We1.rearrange("e d i -> d e i")), (we3_sb[:, :, :], We3.rearrange("e d i -> d e i")),
            (we2_sb[:, :, :], We2.rearrange("(p two) i d -> (two i) p d", two=2))]
        LATER_LOADS = [
            (blocks_sb[:, L0_LAST:L3_FIRST, :], blocks[:, L0_LAST:L3_FIRST, :]),
            (l1_gate_sb[:, :], l1_gate), (l2_gate_sb[:, :], l2_gate),
            (l1w1_sb[:, :, :], W1.rearrange("e d f -> d e f"))] + [
            (l1w2_sb[:, e:e + 4, :, :], W2[e:e + 4].rearrange("e (c p) d -> p e c d", p=P)) for e in (0, 4)] + [
            (l2w1_sb[:, :, :], w1.rearrange("e d f -> d e f")), (l2w3_sb[:, :, :], w3.rearrange("e d f -> d e f"))] + [
            (l2w2_sb[0:hid_rows(c), :, c, :], w2[:, c * P:c * P + hid_rows(c), :].rearrange("e p d -> p e d"))
            for c in range(3)]
        ENGINES = 4

        PE_PARTS = [l0_attn_pe, l0_moe_pe, l1_attn_pe, l1_moe_pe, l2_attn_pe, l2_moe_pe, l3_attn_pe, l3_ffn_pe]
        ACT_PARTS = [l0_attn_act, l0_moe_act, l1_attn_act, l1_moe_act, l2_attn_act, l2_moe_act, l3_attn_act, l3_ffn_act]
        DVE_PARTS = [l0_attn_dve, l0_moe_dve, l1_attn_dve, l1_moe_dve, l2_attn_dve, l2_moe_dve, l3_attn_dve, l3_ffn_dve]
        POOL_PARTS = [l0_attn_pool, l0_moe_pool, l1_attn_pool, l1_moe_pool, l2_attn_pool, l2_moe_pool, l3_attn_pool, l3_ffn_pool]

        block = ctx.enter_context(nc.Block())

        def pass_end(eng, i):
            eng.sem_inc(pass_done, 1)
            eng.wait_ge(cleared, i + 1)

        @block.sync
        def _(sp):
            def load(dst, src):
                sp.dma_start(dst, src).then_inc(loaded, 16)

            for dst, src in FIRST_LOADS:
                load(dst, src)

            def load_ctx(b, j):
                sp.dma_start(ctxT[j][:, :], ctx_t[bass.ds(b, 1)].rearrange("o f t -> (o f) t")).then_inc(inputs, 16)
                sp.dma_start(ctx_tok[j][:, :], ctx_k[bass.ds(b, 1)].rearrange("o s f -> (o s) f")).then_inc(inputs, 16)
                sp.dma_start(key_ok[j][:, :], key_mask[bass.ds(b, 1)].rearrange("o s -> s o")).then_inc(inputs, 16)
                sp.dma_start(mask_in[j].rearrange("p (t s) -> p t s", s=S2),
                             attn_mask[bass.ds(b, 1)].rearrange("a o (t p) s -> p (a o t) s", p=P)).then_inc(inputs, 16)

            def load_x(b, j):
                sp.dma_start(XT[j][:, :], x[bass.ds(b, 1)].rearrange("o f t -> (o f) t")).then_inc(inputs, 16)

            def store(b, j):
                sp.wait_ge(x_new, x_blk("l3_ffn", j))
                sp.dma_start(out[bass.ds(b, 1)].rearrange("o f t -> (o f) t"), FC[j][:, :]).then_inc(outputs, 16)

            for j in range(J):
                load_x(j, j)
                load_ctx(j, j)
            with sp.Fori(0, PASSES - 1) as i:
                sp.wait_ge(x_new, x_blk("l3_attn", J - 1))
                for j in range(J):
                    load_ctx((i + 1) * J + j, j)
                for j in range(J):
                    store(i * J + j, j)
                    load_x((i + 1) * J + j, j)
                sp.wait_ge(outputs, 16 * J * (i + 1))
                sp.wait_ge(pass_done, ENGINES * (i + 1))
                for s in per_pass + [chain_d, chain_a, chain_p]:
                    sp.sem_clear(s)
                sp.sem_inc(cleared, 1)
            for j in range(J):
                store((PASSES - 1) * J + j, j)
            sp.wait_ge(outputs, 16 * J * PASSES)
            sp.sem_inc(cleared, 1)


        quant_step = sem("quant_step")

        @block.gpsimd
        def _(pool):
            ch = Chain(pool, setup_pool)
            ch.tag(nc.gpsimd.memset(half_sb[:, :], -0.5))
            ch.tag(nc.gpsimd.memset(carry_sb[:, :], 0.0))
            pool.wait_ge(setup_done, 1)
            ch.tag(nc.gpsimd.partition_all_reduce(qk_most[:, :], qk_scale[:, :], P, bass.bass_isa.ReduceOp.absmax))
            pool.wait_ge(setup_pool, ch.n)
            quant_pool(pool)
            with pool.Fori(0, PASSES) as i:
                for part in POOL_PARTS:
                    part(pool)
                pass_end(pool, i)

        @block.tensor
        def _(pe):
            pe.wait_ge(loaded, 16 * len(FIRST_LOADS))
            quant_pe(pe)
            pe.wait_ge(setup_done, 3)
            with pe.Fori(0, PASSES) as i:
                pe.wait_ge(inputs, 16 * INPUT_DMAS * (i + 1))
                for part in PE_PARTS:
                    part(pe)
                pass_end(pe, i)

        @block.scalar
        def _(act):
            act.wait_ge(loaded, 16 * len(FIRST_LOADS))
            nc.scalar.activation(tg_sb[:, :], gates_sb[:, :], ACT.Tanh).then_inc(setup_act, 1)
            for dst, src in L0_MOE_LOADS:
                nc.scalar.dma_start(dst, src).then_inc(loaded_l0_moe, 16)
            for dst, src in LATER_LOADS:
                nc.scalar.dma_start(dst, src).then_inc(loaded_later, 16)
            with act.Fori(0, PASSES) as i:
                for part in ACT_PARTS:
                    part(act)
                pass_end(act, i)

        @block.vector
        def _(dve):
            ch = Chain(dve, chain_d)
            dve.wait_ge(loaded, 16 * len(FIRST_LOADS))
            quant_most_dve()
            nc.vector.tensor_tensor(qk_scale[:, :], col("l2_qs"), col("l2_ks"), ALU.mult).then_inc(setup_done, 1)
            dve.wait_ge(setup_pool, 3)
            nc.vector.tensor_scalar(shift[:, :], qk_most[:, :], -8.0, None, ALU.mult).then_inc(setup_done, 1)
            dve.wait_ge(setup_done, 2)
            qc = Chain(dve, quant_step)
            quant_dve(dve, qc)
            dve.sem_inc(setup_done, 1)
            dve.wait_ge(setup_act, 1)
            with dve.Fori(0, PASSES) as i:
                for part in DVE_PARTS:
                    part(dve, ch)
                pass_end(dve, i)


def _square(a):
    return [a[:, i * P:(i + 1) * P] for i in range(a.shape[1] // P)]


def _stack_blocks(np, i):
    def per_head(w):
        a = np.zeros((P, P), w.dtype)
        for h in range(16):
            a[8 * h:8 * h + 8, 8 * h:8 * h + 8] = w.T
        return a

    qkv, inp = i["L0_xattn_qkv_w"], i["L0_xattn_in_proj_w"]
    out = [qkv[256:384].T, i["L0_xattn_sa_out_w"].T, inp[0:128].T, inp[128:256].T, inp[256:384].T,
           i["L0_xattn_mha_out_w"].T]
    out += _square(i["L0_xattn_lin1_w"].T)
    out += [i["L0_xattn_lin2_w"].T[c * P:(c + 1) * P] for c in range(4)]
    out += [i["L0_ffn_ws1"], i["L0_ffn_ws3"], i["L0_ffn_ws2"]]
    out += [per_head(i["L1_xattn_Wq"]), per_head(i["L1_xattn_Wk"]), per_head(i["L1_xattn_Wv"]), i["L1_xattn_Wo"].T]
    out += _square(i["L2_xattn_Wq"]) + _square(i["L2_xattn_Wkv"])
    out += [i["L2_xattn_Wo"][c * P:(c + 1) * P] for c in range(4)]
    out += [i[f"L3_xattn_{n}"] for n in ("Wq1", "Wk1", "Wv1", "Wq2", "Wk2", "Wv2", "fc1_w", "fc2_w")]
    out += _square(i["L3_ffn_W_fc"].T)
    out += [i["L3_ffn_W_proj"].T[c * P:(c + 1) * P] for c in range(4)]
    assert len(out) == len(BLOCKS)
    return np.ascontiguousarray(np.stack(out, axis=1))


def _stack_cols(np, i):
    qkv_b, in_b = i["L0_xattn_qkv_b"], i["L0_xattn_in_proj_b"]
    rows = [qkv_b[256:384], i["L0_xattn_sa_out_b"], in_b[0:128], in_b[128:256], in_b[256:384],
            i["L0_xattn_mha_out_b"]]
    rows += list(i["L0_xattn_lin1_b"].reshape(4, P)) + [i["L0_xattn_lin2_b"]]
    rows += [i[f"L0_xattn_ln{n}_{p}"] for n in (1, 2, 3) for p in "gb"]
    rows += list(i["L0_ffn_be1"].reshape(8, P)) + list(i["L0_ffn_be3"].reshape(8, P))
    rows += [i["L0_ffn_bs1"], i["L0_ffn_bs3"], i["L0_ffn_bs2"], i["L1_xattn_bo"]]
    rows += list(i["L1_ffn_b1"].reshape(32, P)) + list(i["L1_ffn_b2"])
    rows += [i[f"L2_xattn_{n}"] for n in ("ln_x_w", "ln_x_b", "ln_l_w", "ln_l_b", "ln_o_w", "ln_o_b")]
    rows += [np.concatenate([i[f"L2_xattn_{n}"]] * 2) for n in ("q_scale", "k_scale")]
    rows += [i["L3_xattn_fc1_b"], i["L3_xattn_fc2_b"]]
    rows += [i[f"L3_xattn_ln{n}_{p}"] for n in (1, 2, 3) for p in "gb"]
    rows += list(i["L3_ffn_b_fc"].reshape(4, P)) + [i["L3_ffn_b_proj"]]
    assert len(rows) == len(COLS)
    return np.ascontiguousarray(np.stack(rows, axis=1))


def _constants(np):
    i = np.arange(P)
    c = {"ident": np.eye(P), "upto": i[:, None] <= i[None, :], "ones": np.ones((P, P)),
         "causal": np.where(i[None, :] > i[:, None], LOW, 0.0),
         "heads16": i[:, None] // 16 == np.arange(8)[None, :], "heads8": i[:, None] // 8 == np.arange(16)[None, :],
         "halves": i[:, None] // 64 == np.arange(2)[None, :],
         "first16": np.broadcast_to(16 - np.arange(16), (P, 16)), "first8": np.broadcast_to(8 - np.arange(8), (P, 8)),
         "first4": np.broadcast_to(4 - np.arange(4), (P, 4)), "keys": np.broadcast_to(np.arange(512), (P, 512))}
    packed = np.concatenate([np.asarray(c[n], np.float32) for n in CONSTS], axis=1)
    pair_sel = np.repeat(np.eye(16, dtype=np.float32), 64, axis=1)
    return np.ascontiguousarray(packed), pair_sel


def kernel(**inputs):
    import numpy as np
    import concourse.bacc as bacc
    from concourse.bass_utils import run_bass_kernel_spmd

    i = {k: np.asarray(v) for k, v in inputs.items()}
    consts, pair_sel = _constants(np)
    laid = {
        "x": i["x"].transpose(0, 2, 1),
        "ctx_t": i["ctx_1024"].transpose(0, 2, 1), "ctx_k": i["ctx_1024"],
        "attn_mask": i["mask_Bx1xSxS2_if1"], "key_mask": i["mask_BxS2_bk0"],
        "gates": np.broadcast_to(np.concatenate([i["g_xattn"], i["g_ffn"]]), (P, 8)),
        "blocks": _stack_blocks(np, i), "cols": _stack_cols(np, i),
        "rows": np.broadcast_to(np.concatenate([i["L0_ffn_gate_b"], i["L1_ffn_gate_b"], i["L2_ffn_expert_bias"]]),
                                (P, 32)),
        "consts": consts, "pair_sel": pair_sel,
        "gate16": i["L0_ffn_gate_w"].T, "be2": i["L0_ffn_be2"], "l1_gate": i["L1_ffn_gate_w"].T,
        "l2_gate": i["L2_ffn_gate_w"].T, "We1": i["L0_ffn_We1"], "We2": i["L0_ffn_We2"], "We3": i["L0_ffn_We3"],
        "W1": i["L1_ffn_W1"], "W2": i["L1_ffn_W2"], "w1": i["L2_ffn_w1"], "w2": i["L2_ffn_w2"], "w3": i["L2_ffn_w3"],
        "A_fc": i["L3_ffn_A_fc"], "B_fc": i["L3_ffn_B_fc"].T, "A_proj": i["L3_ffn_A_proj"],
        "B_proj": i["L3_ffn_B_proj"].T,
    }
    nc = bacc.Bacc("TRN2", target_bir_lowering=False, num_devices=1)
    arrays, args = {}, {}
    for name, a in laid.items():
        a = np.ascontiguousarray(a)
        arrays[f"in_{name}_dram"] = a
        args[name] = nc.dram_tensor(f"in_{name}_dram", a.shape, mybir.dt.from_np(a.dtype), kind="ExternalInput").ap()
    out = nc.dram_tensor("out_0_dram", (B, P, T), F32, kind="ExternalOutput").ap()
    flamingo_kernel(nc, **args, out=out)
    r = run_bass_kernel_spmd(nc, [arrays], core_ids=[0])
    return np.ascontiguousarray(np.asarray(r.results[0]["out_0_dram"]).transpose(0, 2, 1))
```

```python
from contextlib import ExitStack

import concourse.bass as bass
from concourse import mybir

F32 = mybir.dt.float32
I32 = mybir.dt.int32
U8 = mybir.dt.uint8
U16 = mybir.dt.uint16
BF16 = mybir.dt.bfloat16
ALU = mybir.AluOpType
ACT = mybir.ActivationFunctionType
AX = mybir.AxisListType

P = 128
B, T, S2 = 4, 512, 77
NT = T // P
J = 2
PASSES = B // J
EPS = 1e-5
LOW = -1e30
CAP = 320

BLOCKS = (["l0_v", "l0_sa", "l0_q", "l0_k", "l0_mv", "l0_mo"] + [f"l0_up{c}" for c in range(4)]
          + [f"l0_down{c}" for c in range(4)] + ["l0_s1", "l0_s3", "l0_s2"]
          + ["l1_q", "l1_k", "l1_v", "l1_o"]
          + [f"l2_q{c}" for c in range(4)] + [f"l2_k{c}" for c in range(4)] + [f"l2_v{c}" for c in range(4)]
          + [f"l2_o{c}" for c in range(4)]
          + ["l3_q1", "l3_k1", "l3_v1", "l3_q2", "l3_k2", "l3_v2", "l3_f1", "l3_f2"]
          + [f"l3_up{c}" for c in range(4)] + [f"l3_down{c}" for c in range(4)])
COLS = (["l0_bv", "l0_bo", "l0_bq", "l0_bk", "l0_bmv", "l0_bmo"] + [f"l0_bup{c}" for c in range(4)]
        + ["l0_bdown", "ln1_g", "ln1_b", "ln2_g", "ln2_b", "ln3_g", "ln3_b"]
        + [f"be1_{p}" for p in range(8)] + [f"be3_{p}" for p in range(8)] + ["bs1", "bs3", "bs2"]
        + ["l1_bo"] + [f"l1_b1_{e}_{c}" for e in range(8) for c in range(4)] + [f"l1_b2_{e}" for e in range(8)]
        + ["l2_xg", "l2_xb", "l2_lg", "l2_lb", "l2_og", "l2_ob", "l2_qs", "l2_ks"]
        + ["l3_b1", "l3_b2", "l3_n1g", "l3_n1b", "l3_n2g", "l3_n2b", "l3_n3g", "l3_n3b"]
        + [f"l3_bfc{c}" for c in range(4)] + ["l3_bproj"])
CONSTS = {"ident": 128, "upto": 128, "ones": 128, "causal": 128, "heads16": 8, "heads8": 16,
          "halves": 2, "first16": 16, "first8": 8, "first4": 4, "keys": 512}
NORMS = ["l0_in", "l0_1", "l0_2", "l0_3", "l0_moe", "l1_in", "l1_moe", "l2_in", "l2_lat", "l2_out", "l2_moe",
         "l3_in", "l3_1", "l3_2", "l3_3", "l3_ffn"]


def starts(widths):
    out, at = {}, 0
    for name, w in widths.items():
        out[name] = (at, at + w)
        at += w
    return out, at


CONST_AT, CONST_N = starts(CONSTS)


class Order:

    def __init__(self, *names):
        self.names = list(names)

    def __call__(self, name, j):
        return self.names.index(name) * J + j + 1


def flamingo_kernel(nc, x, ctx_t, ctx_k, attn_mask, key_mask, gates, blocks, cols, rows, consts, picks,
                    gate16, be2, l1_gate, l2_gate, We1, We2, We3, W1, W2, w1, w2, w3, A_fc, B_fc, A_proj, B_proj, out):
    with ExitStack() as ctx:
        def sb(name, shape, dt=F32):
            return ctx.enter_context(nc.sbuf_tensor(name, shape, dt))

        def sem(name):
            return ctx.enter_context(nc.semaphore(name))

        psum = ctx.enter_context(nc.psum_tensor("psum", [P, 8, 512], F32))

        def bank(j, k):
            return psum[:, 4 * j + k, :]

        blocks_sb = sb("blocks_sb", [P, len(BLOCKS), P])
        cols_sb = sb("cols_sb", [P, len(COLS)])
        rows_sb = sb("rows_sb", [P, 32])
        consts_sb = sb("consts_sb", [P, CONST_N])
        picks_sb = sb("picks_sb", [P, P + 8 + 8 * P], U16)
        gate16_sb = sb("gate16_sb", [P, 16])
        l1_gate_sb = sb("l1_gate_sb", [P, 8])
        l2_gate_sb = sb("l2_gate_sb", [P, 8])
        be2_sb = sb("be2_sb", [3 * 16, P])
        we1_sb = sb("we1_sb", [P, 16, 64])
        we3_sb = sb("we3_sb", [P, 16, 64])
        we2_sb = sb("we2_sb", [P, 8, P])
        HID = w1.shape[2]
        l1w1_sb = sb("l1w1_sb", [P, 8, 512])
        l1w2_sb = sb("l1w2_sb", [P, 8, 4, P])
        l2w1_sb = sb("l2w1_sb", [P, 8, HID])
        l2w3_sb = sb("l2w3_sb", [P, 8, HID])
        l2w2_sb = sb("l2w2_sb", [P, 8, 3, P])
        gates_sb = sb("gates_sb", [P, 8])
        tg_sb = sb("tg_sb", [P, 8])
        half_sb = sb("half_sb", [P, 16])
        carry_sb = sb("carry_sb", [P, 16])
        lora_sb = sb("lora_sb", [16, 2, 512 + P])

        def blk(name):
            return blocks_sb[:, BLOCKS.index(name), :]

        def col(name):
            i = COLS.index(name)
            return cols_sb[:, i:i + 1]

        def const(name):
            a, b = CONST_AT[name]
            return consts_sb[:, a:b]

        ident = const("ident")

        def expert_pick(e):
            return picks_sb[0:24, P + e:P + e + 1].bitcast(BF16).to_broadcast([24, P])

        def pair_pick(p):
            return picks_sb[0:48, P + 8 + p * P:P + 8 + (p + 1) * P].bitcast(BF16)

        XT = [sb(f"XT{j}", [P, T]) for j in range(J)]
        FA = [sb(f"FA{j}", [P, T]) for j in range(J)]
        FB = [sb(f"FB{j}", [P, T]) for j in range(J)]
        FC = [sb(f"FC{j}", [P, T]) for j in range(J)]
        XN = [sb(f"XN{j}", [P, NT, P]) for j in range(J)]
        ctxT = [sb(f"ctxT{j}", [P, S2]) for j in range(J)]
        stats = [sb(f"stats{j}", [P, NT, 6]) for j in range(J)]
        mv = [sb(f"mv{j}", [P, NT, 2]) for j in range(J)]
        var = [sb(f"var{j}", [P, NT]) for j in range(J)]
        rstd = [sb(f"rstd{j}", [P, NT]) for j in range(J)]
        arena = sb("arena", [P, 15104])
        used = [0]

        def take(n, rows_=P):
            a = arena[0:rows_, used[0]:used[0] + n]
            used[0] += n
            assert used[0] <= 15104, used[0]
            return a

        ctx_tok = [sb(f"ctx_tok{j}", [S2, P]) for j in range(J)]
        key_ok = [sb(f"key_ok{j}", [S2, 1], U8) for j in range(J)]

        loaded = sem("loaded")
        loaded_l0_moe = sem("loaded_l0_moe")
        loaded_later = sem("loaded_later")
        inputs = sem("inputs")
        outputs = sem("outputs")
        chain_d = sem("vector_chain")
        pass_done = sem("pass_done")
        cleared = sem("cleared")
        setup_done = sem("setup_done")
        setup_act = sem("setup_act")
        setup_pool = sem("setup_pool")
        per_pass = []

        def psem(name):
            per_pass.append(sem(name))
            return per_pass[-1]

        norm_in = psem("norm_in")
        norm_var = psem("norm_var")
        norm_eps = psem("norm_eps")
        norm_rstd = psem("norm_rstd")
        norm_xn = psem("norm_xn")
        norm_out = psem("norm_out")
        norm_T = psem("norm_T")
        norm = Order(*NORMS)

        class Chain:

            def __init__(self, eng, s):
                self.eng, self.s, self.n = eng, s, 0

            def tag(self, ins):
                ins.then_inc(self.s, 1)
                self.n += 1

            def settle(self):
                if self.n:
                    self.eng.wait_ge(self.s, self.n)

            def link(self, ins):
                self.tag(ins)
                self.settle()

        def pe_turn(pe, src, dst):
            for t in range(NT):
                last = nc.tensor.transpose(dst[:, t * P:(t + 1) * P], src[:, t * P:(t + 1) * P], ident)
            return last

        def pe_keep_warm(dst, n):
            for _ in range(n):
                nc.tensor.matmul(dst, picks_sb[:, 0:P].bitcast(BF16), picks_sb[:, 0:T].bitcast(BF16),
                                 start=True, stop=True)

        def pe_norm_in(pe, name, j, src):
            pe_turn(pe, src, bank(j, 3)).then_inc(norm_in, 1)
            if j == J - 1:
                pe_keep_warm(bank(j, 2), 12)

        def pe_norm_out(pe, name, j):
            pe.wait_ge(norm_xn, norm(name, j))
            pe_turn(pe, XN[j][:, :, :].rearrange("p t f -> p (t f)"), bank(j, 2)).then_inc(norm_out, 1)

        def dve_norm(dve, ch, name):
            for j in range(J):
                dve.wait_ge(norm_in, norm(name, j))
                for t in range(NT):
                    ch.tag(nc.vector.bn_stats(stats[j][:, t, :], bank(j, 3)[:, t * P:(t + 1) * P]))
                ch.settle()
                for t in range(NT):
                    last = nc.vector.bn_aggr(mv[j][:, t, :], stats[j][:, t, :])
                last.then_inc(norm_var, 1)
            for j in range(J):
                dve.wait_ge(norm_rstd, norm(name, j))
                for t in range(NT):
                    last = nc.vector.tensor_scalar(XN[j][:, t, :], bank(j, 3)[:, t * P:(t + 1) * P],
                                                   mv[j][:, t, 0:1], rstd[j][:, t:t + 1],
                                                   ALU.subtract, ALU.mult)
                last.then_inc(norm_xn, 1)

        def pool_norm(pool, name):
            for j in range(J):
                pool.wait_ge(norm_var, norm(name, j))
                nc.gpsimd.tensor_scalar(var[j][:, :], mv[j][:, :, 1], EPS, None, ALU.add).then_inc(norm_eps, 1)
                pool.wait_ge(norm_eps, norm(name, j))
                nc.gpsimd.tensor_tensor(rstd[j][:, :], var[j][:, :], half_sb[:, 0:NT], ALU.pow)\
                    .then_inc(norm_rstd, 1)

        def act_norm(act, name, dst, g=None, b=None):
            for j in range(J):
                act.wait_ge(norm_out, norm(name, j))
                if g is None:
                    ins = nc.scalar.activation(dst[j][:, :], bank(j, 2), ACT.Identity)
                else:
                    ins = nc.scalar.activation(dst[j][:, :], bank(j, 2), ACT.Identity, bias=col(b), scale=col(g))
                ins.then_inc(norm_T, 1)

        def first_max(ch, src, oh, mx, first, n, t):
            wide = [P, t, n]
            ch.link(nc.vector.tensor_reduce(mx, src, AX.X, ALU.max))
            ch.link(nc.vector.tensor_tensor(oh, src, mx.unsqueeze(2).to_broadcast(wide), ALU.is_equal))
            ch.link(nc.vector.tensor_tensor(oh, oh, first.unsqueeze(1).to_broadcast(wide), ALU.mult))
            ch.link(nc.vector.tensor_reduce(mx, oh, AX.X, ALU.max))
            ch.link(nc.vector.tensor_tensor(oh, oh, mx.unsqueeze(2).to_broadcast(wide), ALU.is_equal))

        att_scores = psem("att_scores")
        att_centred = psem("att_centred")
        att_exps = psem("att_exps")
        att_inv = psem("att_inv")
        att_normed = psem("att_normed")
        att_turned = psem("att_turned")
        att_moved = psem("att_moved")
        att_pv = psem("att_pv")
        att_zeros = psem("att_zeros")
        att_values = psem("att_values")
        HU = 8
        att_units = {"l0": [(j, t, 0) for j in range(J) for t in range(NT)],
                     "l1": [(j, 2 * tp + s, h) for j in range(J) for tp in range(NT // 2) for h in range(2)
                            for s in range(2)]}
        att_base = {"l0": 0, "l1": len(att_units["l0"])}
        used[0] = 0
        weights = [take(HU * S2) for _ in range(3)]
        weights_t = [take(HU * 2 * P, S2).rearrange("p (h q) -> p h q", q=2 * P) for _ in range(2)]
        k_heads = [take(2 * HU * S2) for _ in range(J)]
        k_feat = [take(S2) for _ in range(J)]
        row_max = [take(HU) for _ in range(3)]
        row_sum = [take(HU) for _ in range(3)]
        row_inv = [take(HU) for _ in range(3)]
        used[0] = 15104 - J * 16 * (P + 8)
        v_heads = [take(16 * (P + 8), S2) for _ in range(J)]
        blocked = [sb(f"blocked{j}", [P, NT * S2])[:, :] for j in range(J)]
        mask_in = [m.bitcast(I32) for m in blocked]

        def head_values(j, hd):
            n = P // hd
            return v_heads[j][:, 0:n * P].rearrange("p (h n) -> p h n", n=P)

        def head_blocks(j, hd):
            n = P // hd
            return v_heads[j][:, 0:n * (P + hd)].rearrange("p (h n) -> p h n", n=P + hd)[:, :, 0:hd]

        def score_banks(u):
            return psum[:, 2 * (u % 2):2 * (u % 2) + 2, 0:4 * S2].rearrange("p b (h s) -> p b h s", s=S2)

        def by_bank(w):
            return w.rearrange("p (b h s) -> p b h s", b=2, s=S2)

        def by_head(w):
            return w.rearrange("p (h s) -> p h s", s=S2)

        def att_pe(pe, layer, Q):
            units, base = att_units[layer], att_base[layer]
            hd, halves = (16, 1) if layer == "l0" else (8, 2)

            def scores(n):
                j, t, half = units[n]
                u = base + n
                if n >= 2:
                    pe.wait_ge(att_centred, u - 1)
                for q in range(2):
                    h = half * HU + 4 * q
                    last = nc.tensor.matmul(psum[:, 2 * (u % 2) + q, 0:4 * S2], Q[j][:, t * P:(t + 1) * P],
                                            k_heads[j][:, h * S2:(h + 4) * S2], start=True, stop=True)
                last.then_inc(att_scores, 1)

            def turn(n):
                u = base + n
                pe.wait_ge(att_normed, u + 1)
                if n >= 1:
                    pe.wait_ge(att_moved, u)
                for h in range(HU):
                    last = nc.tensor.transpose(psum[0:S2, 4 + h // 4, (h % 4) * P:(h % 4 + 1) * P],
                                               weights[u % 3][:, h * S2:(h + 1) * S2], ident)
                last.then_inc(att_turned, 1)

            def outputs_of(g, part):
                j, t, half = units[2 * g]
                pe.wait_ge(att_moved, base + 2 * g + 2)
                for h in range(part * HU // 2, (part + 1) * HU // 2):
                    nh = half * HU + h
                    last = nc.tensor.matmul(psum[:, 6 + j, t * P:(t + 2) * P], head_values(j, hd)[:, nh, :],
                                            weights_t[g % 2][:, h, :], start=(nh == 0), stop=(nh == halves * HU - 1))
                last.then_inc(att_pv, 1)

            scores(0)
            scores(1)
            for n in range(len(units)):
                if n + 2 < len(units):
                    scores(n + 2)
                turn(n)
                if n == 2:
                    pe.wait_ge(att_values, J if layer == "l0" else 2 * J)
                if n >= 2:
                    outputs_of(n // 2 - 1, n % 2)
            for part in range(2):
                outputs_of(len(units) // 2 - 1, part)

        def att_act(act, layer, scale):
            units, base = att_units[layer], att_base[layer]

            def exps(n):
                u = base + n
                act.wait_ge(att_centred, u + 1)
                nc.scalar.activation(weights[u % 3], weights[u % 3], ACT.Exp, scale=scale).then_inc(att_exps, 1)

            exps(0)
            exps(1)
            for n in range(len(units)):
                u, g, s = base + n, n // 2, n % 2
                act.wait_ge(att_turned, u + 1)
                if g >= 2:
                    act.wait_ge(att_pv, base + 2 * g - 2)
                nc.scalar.activation(weights_t[g % 2][:, :, s * P:(s + 1) * P].rearrange("p (b h) q -> p b h q", b=2),
                                     psum[0:S2, 4:6, :].rearrange("p b (h q) -> p b h q", q=P),
                                     ACT.Copy).then_inc(att_moved, 1)
                if n + 2 < len(units):
                    exps(n + 2)

        def att_dve(dve, ch, layer):
            units, base = att_units[layer], att_base[layer]

            def centre(n):
                j, t, half = units[n]
                u = base + n
                w, m = weights[u % 3], row_max[u % 3]
                s = score_banks(u)
                dve.wait_ge(att_scores, u + 1)
                if n >= 3:
                    dve.wait_ge(att_turned, u - 2)
                if layer == "l1":
                    block = blocked[j][:, t * S2:(t + 1) * S2].unsqueeze(1).unsqueeze(1).to_broadcast([P, 2, 4, S2])
                    ch.link(nc.vector.tensor_tensor(by_bank(w), s, block, ALU.add))
                    s = by_bank(w)
                ch.link(nc.vector.tensor_reduce(m.rearrange("p (b h) -> p b h", b=2), s, AX.X, ALU.max))
                nc.vector.tensor_tensor(by_bank(w), s, m.rearrange("p (b h) -> p b h", b=2).unsqueeze(3)
                                        .to_broadcast([P, 2, 4, S2]), ALU.subtract).then_inc(att_centred, 1)

            centre(0)
            centre(1)
            for n in range(len(units)):
                u = base + n
                dve.wait_ge(att_exps, u + 1)
                ch.link(nc.vector.tensor_reduce(row_sum[u % 3], by_head(weights[u % 3]), AX.X, ALU.add))
                if n >= 3:
                    dve.wait_ge(att_normed, u - 2)
                nc.vector.reciprocal(row_inv[u % 3], row_sum[u % 3]).then_inc(att_inv, 1)
                if n + 2 < len(units):
                    centre(n + 2)

        def att_pool(pool, layer):
            for u in range(att_base[layer], att_base[layer] + len(att_units[layer])):
                pool.wait_ge(att_inv, u + 1)
                w = by_head(weights[u % 3])
                nc.gpsimd.tensor_tensor(w, w, row_inv[u % 3].unsqueeze(2).to_broadcast([P, HU, S2]), ALU.mult)\
                    .then_inc(att_normed, 1)

        def att_halves(layer):
            return att_base[layer] + len(att_units[layer])

        x_new = psem("x_new")
        x_blk = Order("l0_attn", "l0_moe", "l1_attn", "l1_moe", "l2_attn", "l2_moe", "l3_attn", "l3_ffn")

        l0_prod = psem("l0_prod")
        l0_p = Order("kv", "v", "sa", "q", "mo", "up", "down")
        l0_act = psem("l0_act")
        l0_a = Order("k", "v", "q", "ca", "up", "y")
        l0_dve = psem("l0_dve")
        l0_d = Order("r1", "kv", "r2", "r3")
        used[0] = 0
        hidden = [take(4 * T) for _ in range(J)]

        def l0_attn_pe(pe):
            for j in range(J):
                pe_norm_in(pe, "l0_in", j, XT[j][:, :])
            for j in range(J):
                nc.tensor.matmul(bank(j, 0)[:, 0:S2], blk("l0_k"), ctxT[j][:, :], start=True, stop=True)
                nc.tensor.matmul(bank(j, 1)[0:S2, 0:P], ctxT[j][:, :], blk("l0_mv"), start=True, stop=True)\
                    .then_inc(l0_prod, 1)
            for j in range(J):
                pe_norm_out(pe, "l0_in", j)
            for j in range(J):
                pe.wait_ge(norm_T, norm("l0_in", j))
                nc.tensor.matmul(bank(j, 3), blk("l0_v"), FA[j][:, :], start=True, stop=True).then_inc(l0_prod, 1)
            for j in range(J):
                pe.wait_ge(l0_act, l0_a("v", j))
                nc.tensor.matmul(bank(j, 2), blk("l0_sa"), FB[j][:, :], start=True, stop=True).then_inc(l0_prod, 1)
            for j in range(J):
                pe.wait_ge(l0_dve, l0_d("r1", j))
                pe_norm_in(pe, "l0_1", j, FC[j][:, :])
            for j in range(J):
                pe_norm_out(pe, "l0_1", j)
            for j in range(J):
                pe.wait_ge(norm_T, norm("l0_1", j))
                nc.tensor.matmul(bank(j, 3), blk("l0_q"), FA[j][:, :], start=True, stop=True).then_inc(l0_prod, 1)
            pe.wait_ge(l0_act, l0_a("q", J - 1))
            pe.wait_ge(l0_dve, l0_d("kv", J - 1))
            att_pe(pe, "l0", FB)
            for j in range(J):
                pe.wait_ge(l0_act, l0_a("ca", j))
                nc.tensor.matmul(bank(j, 2), blk("l0_mo"), FC[j][:, :], start=True, stop=True).then_inc(l0_prod, 1)
            for j in range(J):
                pe.wait_ge(l0_dve, l0_d("r2", j))
                pe_norm_in(pe, "l0_2", j, FB[j][:, :])
            for j in range(J):
                pe_norm_out(pe, "l0_2", j)
            for j in range(J):
                pe.wait_ge(norm_T, norm("l0_2", j))
                for c in range(4):
                    last = nc.tensor.matmul(bank(j, c), blk(f"l0_up{c}"), FA[j][:, :], start=True, stop=True)
                last.then_inc(l0_prod, 1)
            for j in range(J):
                pe.wait_ge(l0_act, l0_a("up", j))
                for c in range(4):
                    last = nc.tensor.matmul(bank(j, 0), blk(f"l0_down{c}"), hidden[j][:, c * T:(c + 1) * T],
                                            start=(c == 0), stop=(c == 3))
                last.then_inc(l0_prod, 1)
            for j in range(J):
                pe.wait_ge(l0_dve, l0_d("r3", j))
                pe_norm_in(pe, "l0_3", j, FB[j][:, :])
            for j in range(J):
                pe_norm_out(pe, "l0_3", j)

        def l0_attn_act(act):
            for j in range(J):
                act.wait_ge(l0_prod, l0_p("kv", j))
                nc.scalar.activation(k_feat[j], bank(j, 0)[:, 0:S2], ACT.Identity, bias=col("l0_bk"))\
                    .then_inc(l0_act, 1)
            act_norm(act, "l0_in", FA)
            for j in range(J):
                act.wait_ge(l0_prod, l0_p("v", j))
                nc.scalar.activation(FB[j][:, :], bank(j, 3), ACT.Identity, bias=col("l0_bv")).then_inc(l0_act, 1)
            act_norm(act, "l0_1", FA, "ln1_g", "ln1_b")
            for j in range(J):
                act.wait_ge(l0_prod, l0_p("q", j))
                nc.scalar.activation(FB[j][:, :], bank(j, 3), ACT.Identity, bias=col("l0_bq")).then_inc(l0_act, 1)
            att_act(act, "l0", 0.25)
            for j in range(J):
                act.wait_ge(att_pv, att_halves("l0"))
                nc.scalar.activation(FC[j][:, :], psum[:, 6 + j, :], ACT.Identity, bias=col("l0_bmv")).then_inc(l0_act, 1)
            act_norm(act, "l0_2", FA, "ln2_g", "ln2_b")
            for j in range(J):
                act.wait_ge(l0_prod, l0_p("up", j))
                for c in range(4):
                    last = nc.scalar.activation(hidden[j][:, c * T:(c + 1) * T], bank(j, c), ACT.Relu,
                                                bias=col(f"l0_bup{c}"))
                last.then_inc(l0_act, 1)
            act_norm(act, "l0_3", FA, "ln3_g", "ln3_b")

        def l0_attn_dve(dve, ch):
            dve_norm(dve, ch, "l0_in")
            for j in range(J):
                dve.wait_ge(l0_prod, l0_p("sa", j))
                nc.vector.scalar_tensor_tensor(FC[j][:, :], bank(j, 2), col("l0_bo"), FA[j][:, :],
                                               ALU.add, ALU.add).then_inc(l0_dve, 1)
            dve_norm(dve, ch, "l0_1")
            for j in range(J):
                dve.wait_ge(l0_act, l0_a("k", j))
                dve.wait_ge(att_zeros, 1)
                nc.vector.tensor_copy(head_blocks(j, 16), bank(j, 1)[0:S2, 0:P].rearrange("p (h d) -> p h d", d=16))\
                    .then_inc(att_values, 1)
                nc.vector.tensor_tensor(k_heads[j][:, 0:HU * S2].rearrange("p (h s) -> p h s", s=S2),
                                        k_feat[j].unsqueeze(1).to_broadcast([P, HU, S2]),
                                        const("heads16").unsqueeze(2).to_broadcast([P, HU, S2]), ALU.mult)\
                    .then_inc(l0_dve, 1)
            att_dve(dve, ch, "l0")
            for j in range(J):
                dve.wait_ge(l0_prod, l0_p("mo", j))
                nc.vector.scalar_tensor_tensor(FB[j][:, :], bank(j, 2), col("l0_bmo"), FA[j][:, :],
                                               ALU.add, ALU.add).then_inc(l0_dve, 1)
            dve_norm(dve, ch, "l0_2")
            for j in range(J):
                dve.wait_ge(l0_prod, l0_p("down", j))
                nc.vector.scalar_tensor_tensor(FB[j][:, :], bank(j, 0), col("l0_bdown"), FA[j][:, :],
                                               ALU.add, ALU.add).then_inc(l0_dve, 1)
            dve_norm(dve, ch, "l0_3")
            for j in range(J):
                dve.wait_ge(norm_T, norm("l0_3", j))
                nc.vector.scalar_tensor_tensor(XT[j][:, :], FA[j][:, :], tg_sb[:, 0:1], XT[j][:, :],
                                               ALU.mult, ALU.add).then_inc(x_new, 1)

        def l0_attn_pool(pool):
            pool_norm(pool, "l0_in")
            for j in range(J):
                last = nc.gpsimd.memset(v_heads[j], 0.0)
            last.then_inc(att_zeros, 1)
            pool_norm(pool, "l0_1")
            att_pool(pool, "l0")
            pool_norm(pool, "l0_2")
            pool_norm(pool, "l0_3")

        route_e = psem("route_e")
        route_x = psem("route_x")
        route = Order("l0", "l1", "l2")
        JT = J * NT
        both_logit = sb("both_logit", [P, JT, 16])
        both_score = sb("both_score", [P, JT, 16])
        both_chosen = sb("both_chosen", [P, 2, JT, 16])
        both_combine = sb("both_combine", [P, JT, 16])
        both_max = sb("both_max", [P, JT])

        def tiles(j):
            return slice(j * NT, (j + 1) * NT)

        logit = [both_logit[:, tiles(j), :] for j in range(J)]
        score = [both_score[:, tiles(j), :] for j in range(J)]
        chosen = [both_chosen[:, :, tiles(j), :] for j in range(J)]
        combine = [both_combine[:, tiles(j), :] for j in range(J)]
        route_max = [both_max[:, tiles(j)] for j in range(J)]

        def route_exp(act, name):
            n = 16 if name == "l0" else 8
            if name == "l1":
                for j in range(J):
                    act.wait_ge(route_e, route(name, j))
                    nc.scalar.activation(logit[j][:, :, 0:n], logit[j][:, :, 0:n], ACT.Exp).then_inc(route_x, 1)
            else:
                act.wait_ge(route_e, route(name, J - 1))
                nc.scalar.activation(both_logit[:, :, 0:n], both_logit[:, :, 0:n], ACT.Exp).then_inc(route_x, J)

        def route_centre(ch, name, j, logits, n, bias):
            l, wide = logit[j][:, :, 0:n], [P, NT, n]
            ch.link(nc.vector.tensor_tensor(l, logits, bias.unsqueeze(1).to_broadcast(wide), ALU.add))
            ch.link(nc.vector.tensor_reduce(route_max[j][:, :], l, AX.X, ALU.max))
            nc.vector.tensor_tensor(l, l, route_max[j][:, :].unsqueeze(2).to_broadcast(wide), ALU.subtract)\
                .then_inc(route_e, 1)

        def route_centre_both(ch, name, k, n):
            logits = [bank(j, k)[:, 0:NT * n].rearrange("p (t e) -> p t e", e=n) for j in range(J)]
            for j in range(J):
                ch.tag(nc.vector.tensor_reduce(route_max[j], logits[j], AX.X, ALU.max))
            ch.settle()
            for j in range(J):
                nc.vector.tensor_tensor(logit[j][:, :, 0:n], logits[j], route_max[j].unsqueeze(2)
                                        .to_broadcast([P, NT, n]), ALU.subtract).then_inc(route_e, 1)

        def route_softmax(dve, ch, name, j, n):
            l, m = (both_logit[:, :, 0:n], both_max[:, :]) if j is None else (logit[j][:, :, 0:n], route_max[j][:, :])
            dve.wait_ge(route_x, route(name, J - 1 if j is None else j))
            ch.link(nc.vector.tensor_reduce(m, l, AX.X, ALU.add))
            ch.link(nc.vector.reciprocal(m, m))
            ch.link(nc.vector.tensor_tensor(l, l, m.unsqueeze(2).to_broadcast([P, JT if j is None else NT, n]), ALU.mult))

        def choose_two(ch, src, n, first):
            a, b = both_chosen[:, 0, :, 0:n], both_chosen[:, 1, :, 0:n]
            first_max(ch, src, a, both_max[:, :], first, n, JT)
            ch.link(nc.vector.scalar_tensor_tensor(src, a, 2 * LOW, src, ALU.mult, ALU.add))
            first_max(ch, src, b, both_max[:, :], first, n, JT)

        def combine_two(ch, n):
            c = both_combine[:, :, 0:n]
            ch.link(nc.vector.tensor_tensor(c, both_chosen[:, 0, :, 0:n], both_chosen[:, 1, :, 0:n], ALU.add))
            ch.link(nc.vector.tensor_tensor(c, c, both_logit[:, :, 0:n], ALU.mult))
            return split(ch, c, parts(n))

        both_parts = sb("both_parts", [P, JT * 3 * 16], BF16)

        def parts(n):
            return both_parts[:, 0:JT * 3 * n].rearrange("p (t k e) -> p t k e", k=3, e=n)

        def split(ch, c, dst):
            for k in range(2):
                ch.link(nc.vector.tensor_copy(dst[:, :, k, :], c))
                ch.link(nc.vector.tensor_tensor(c, c, dst[:, :, k, :], ALU.subtract))
            return nc.vector.tensor_copy(dst[:, :, 2, :], c)

        def pe_logits(pe, dst, xT, gate, n):
            for t in range(NT):
                last = nc.tensor.matmul(dst[:, t * n:(t + 1) * n], xT[:, t * P:(t + 1) * P], gate,
                                        start=True, stop=True)
            return last

        def turned(dst, n):
            return dst.bitcast(BF16)[0:3 * n, 0:T]

        def pe_turn_combine(pe, dst, j, n):
            for t in range(NT):
                i = (j * NT + t) * 3 * n
                last = nc.tensor.transpose(turned(dst, n)[:, t * P:(t + 1) * P], both_parts[:, i:i + 3 * n],
                                           picks_sb[:, 0:P].bitcast(BF16))
            return last

        used[0] = 0
        combine_t = [take(T, 48).bitcast(BF16)[:, 0:T] for _ in range(J)]
        combine_f = [take(T, 48) for _ in range(J)]
        m0_gate = [take(T) for _ in range(J)]
        m0_mid = [take(T) for _ in range(J)]
        m0_hid = [take(T) for _ in range(J)]
        m0_lin = [take(T) for _ in range(J)]
        L0_EARLY = 6
        m0_early = [take(T) for _ in range(L0_EARLY)]
        pair_sums = take(4 * JT * 6)
        group_sc = take(4 * JT)
        group_a = take(4 * JT)
        group_b = take(4 * JT)

        PAIRS = 8
        l0m_prod = psem("l0m_prod")
        l0m_p = Order("gate", "turn", "y")
        l0m_route = psem("l0m_route")
        l0m_ct = psem("l0m_ct")
        l0m_early = psem("l0m_early")
        l0m_pair = psem("l0m_pair")
        l0m_mid = psem("l0m_mid")
        l0m_front = psem("l0m_front")
        l0m_silu = psem("l0m_silu")
        l0m_hid = psem("l0m_hid")
        l0m_back = psem("l0m_back")
        l0m_y = psem("l0m_y")
        l0m_units = [(p, j) for p in range(PAIRS) for j in range(J)]
        l0m_ahead = l0m_units[:L0_EARLY] + [(PAIRS, j) for j in range(J)]

        def l0_moe_pe(pe):
            for j in range(J):
                pe.wait_ge(x_new, x_blk("l0_attn", j))
                pe_norm_in(pe, "l0_moe", j, XT[j][:, :])
            for j in range(J):
                pe_norm_out(pe, "l0_moe", j)
            pe.wait_ge(loaded_l0_moe, 16 * len(L0_MOE_LOADS))
            for j in range(J):
                pe.wait_ge(norm_T, norm("l0_moe", j))
                pe_logits(pe, bank(j, 2), FA[j], gate16_sb[:, :], 16).then_inc(l0m_prod, 1)

            def products(p, j):
                if p < PAIRS:
                    w1_, w3_ = we1_sb[:, 2 * p:2 * p + 2, :], we3_sb[:, 2 * p:2 * p + 2, :]
                else:
                    w1_, w3_ = blk("l0_s1"), blk("l0_s3")
                nc.tensor.matmul(bank(j, 0), w1_, FA[j][:, :], start=True, stop=True)
                return nc.tensor.matmul(bank(j, 1), w3_, FA[j][:, :], start=True, stop=True)

            for v, (p, j) in enumerate(l0m_ahead):
                if v == L0_EARLY:
                    for i in range(J):
                        pe.wait_ge(l0m_route, i + 1)
                        pe_turn_combine(pe, bank(i, 2), i, 16).then_inc(l0m_prod, 1)
                if v >= J:
                    pe.wait_ge(l0m_pair, v - J + 1)
                products(p, j).then_inc(l0m_early, 1)
            for j in range(J):
                pe.wait_ge(l0m_mid, len(l0m_ahead) - J + j + 1)
                nc.tensor.matmul(bank(j, 3), blk("l0_s2"), m0_hid[j], start=True, stop=False).then_inc(l0m_back, 1)

            def front(u):
                p, j = l0m_units[u]
                if u < J:
                    pe.wait_ge(l0m_ct, j + 1)
                else:
                    pe.wait_ge(l0m_hid, u - J + 1)
                last = nc.tensor.matmul(bank(j, 2), pair_pick(p), combine_t[j], start=True, stop=True)
                if u >= L0_EARLY:
                    last = products(p, j)
                last.then_inc(l0m_front, 1)

            def back(u):
                p, j = l0m_units[u]
                pe.wait_ge(l0m_hid, u + 1)
                nc.tensor.matmul(bank(j, 3), we2_sb[:, p, :], m0_hid[j], start=False, stop=(p == PAIRS - 1))\
                    .then_inc(l0m_back, 1)

            for u in range(len(l0m_units)):
                front(u)
                if u < J:
                    nc.tensor.matmul(bank(u, 3), be2_sb[:, :], combine_f[u], start=False, stop=False)
                if u >= 1:
                    back(u - 1)
            back(len(l0m_units) - 1)

        def l0_moe_act(act):
            act_norm(act, "l0_moe", FA)
            route_exp(act, "l0")
            for v, (p, j) in enumerate(l0m_ahead):
                if v == L0_EARLY:
                    for i in range(J):
                        act.wait_ge(l0m_prod, l0m_p("turn", i))
                        nc.scalar.activation(combine_f[i], turned(bank(i, 2), 16), ACT.Copy)
                        nc.scalar.activation(combine_t[i], turned(bank(i, 2), 16), ACT.Copy).then_inc(l0m_ct, 1)
                act.wait_ge(l0m_early, v + 1)
                if v >= J:
                    act.wait_ge(l0m_mid, v - J + 1)
                nc.scalar.activation(m0_gate[j], bank(j, 0), ACT.Silu, bias=col(f"be1_{p}" if p < PAIRS else "bs1"))
                nc.scalar.activation(m0_lin[j], bank(j, 1), ACT.Identity,
                                     bias=col(f"be3_{p}" if p < PAIRS else "bs3")).then_inc(l0m_pair, 1)
            for u, (p, j) in enumerate(l0m_units):
                if u >= L0_EARLY:
                    act.wait_ge(l0m_front, u + 1)
                    act.wait_ge(l0m_hid, u - J + 1)
                    nc.scalar.activation(m0_gate[j], bank(j, 0), ACT.Silu, bias=col(f"be1_{p}")).then_inc(l0m_silu, 1)
            for j in range(J):
                act.wait_ge(l0m_back, len(l0m_units) + j + 1)
                nc.scalar.activation(FB[j][:, :], bank(j, 3), ACT.Identity, bias=col("bs2")).then_inc(l0m_y, 1)

        def l0_moe_dve(dve, ch):
            dve_norm(dve, ch, "l0_moe")
            dve.wait_ge(l0m_prod, l0m_p("gate", J - 1))
            route_centre_both(ch, "l0", 2, 16)
            route_softmax(dve, ch, "l0", None, 16)
            sc, s16 = both_score[:, :, :], both_score[:, :, :].rearrange("p t (g i) -> p (t g) i", i=4)
            ch.link(nc.vector.tensor_tensor(sc, both_logit[:, :, :],
                                            rows_sb[:, 0:16].unsqueeze(1).to_broadcast([P, JT, 16]), ALU.add))
            ps = pair_sums.rearrange("p (g k) -> p g k", k=6)
            ch.tag(nc.vector.tensor_tensor(ps[:, :, 0:3], s16[:, :, 0:3], s16[:, :, 1:4], ALU.add))
            ch.tag(nc.vector.tensor_tensor(ps[:, :, 3:5], s16[:, :, 0:2], s16[:, :, 2:4], ALU.add))
            ch.link(nc.vector.tensor_tensor(ps[:, :, 5:6], s16[:, :, 0:1], s16[:, :, 3:4], ALU.add))
            ch.link(nc.vector.tensor_reduce(group_sc, ps, AX.X, ALU.max))
            g = group_sc.rearrange("p (t g) -> p t g", g=4)
            ga = group_a.rearrange("p (t g) -> p t g", g=4)
            gb = group_b.rearrange("p (t g) -> p t g", g=4)
            first_max(ch, g, ga, both_max[:, :], const("first4"), 4, JT)
            ch.link(nc.vector.scalar_tensor_tensor(g, ga, LOW, g, ALU.mult, ALU.add))
            first_max(ch, g, gb, both_max[:, :], const("first4"), 4, JT)
            ch.link(nc.vector.tensor_tensor(group_a, group_a, group_b, ALU.add))
            ch.link(nc.vector.tensor_scalar(group_a, group_a, 1.0, -LOW, ALU.subtract, ALU.mult))
            ch.link(nc.vector.tensor_tensor(s16, s16, group_a.unsqueeze(2).to_broadcast([P, 4 * JT, 4]), ALU.add))
            choose_two(ch, sc, 16, const("first16"))
            combine_two(ch, 16).then_inc(l0m_route, J)
            for u, (p, j) in enumerate(l0m_units):
                if u < L0_EARLY:
                    dve.wait_ge(l0m_mid, u + 1)
                    mid = m0_early[u]
                else:
                    mid = m0_mid[j]
                    dve.wait_ge(l0m_silu, u - L0_EARLY + 1)
                    ch.link(nc.vector.scalar_tensor_tensor(mid, bank(j, 1), col(f"be3_{p}"), m0_gate[j],
                                                           ALU.add, ALU.mult))
                dve.wait_ge(l0m_front, u + 1)
                dve.wait_ge(l0m_back, u + 1)
                nc.vector.tensor_tensor(m0_hid[j], bank(j, 2), mid, ALU.mult).then_inc(l0m_hid, 1)
            for j in range(J):
                dve.wait_ge(l0m_y, j + 1)
                nc.vector.scalar_tensor_tensor(XT[j][:, :], FB[j][:, :], tg_sb[:, 4:5], XT[j][:, :],
                                               ALU.mult, ALU.add).then_inc(x_new, 1)

        def l0_moe_pool(pool):
            pool_norm(pool, "l0_moe")
            for j in range(J):
                last = nc.gpsimd.memset(v_heads[j], 0.0)
            last.then_inc(att_zeros, 1)
            for v, (p, j) in enumerate(l0m_ahead):
                pool.wait_ge(l0m_pair, v + 1)
                dst = m0_early[v] if p < PAIRS else m0_hid[j]
                nc.gpsimd.tensor_tensor(dst, m0_gate[j], m0_lin[j], ALU.mult).then_inc(l0m_mid, 1)

        l1_prod = psem("l1_prod")
        l1_p = Order("kv", "q", "o")
        l1_act = psem("l1_act")
        l1_a = Order("k", "q", "ca", "y")
        l1_dve = psem("l1_dve")

        def l1_attn_pe(pe):
            for j in range(J):
                pe.wait_ge(x_new, x_blk("l0_moe", j))
                pe_norm_in(pe, "l1_in", j, XT[j][:, :])
            pe.wait_ge(loaded_later, 16 * len(LATER_LOADS))
            for j in range(J):
                nc.tensor.matmul(bank(j, 0)[:, 0:S2], blk("l1_k"), ctxT[j][:, :], start=True, stop=True)
                nc.tensor.matmul(bank(j, 1)[0:S2, 0:P], ctxT[j][:, :], blk("l1_v"), start=True, stop=True)\
                    .then_inc(l1_prod, 1)
            for j in range(J):
                pe_norm_out(pe, "l1_in", j)
            for j in range(J):
                pe.wait_ge(norm_T, norm("l1_in", j))
                nc.tensor.matmul(bank(j, 3), blk("l1_q"), FA[j][:, :], start=True, stop=True).then_inc(l1_prod, 1)
            pe.wait_ge(l1_act, l1_a("q", J - 1))
            pe.wait_ge(l1_dve, J)
            att_pe(pe, "l1", FB)
            for j in range(J):
                pe.wait_ge(l1_act, l1_a("ca", j))
                nc.tensor.matmul(bank(j, 2), blk("l1_o"), FC[j][:, :], start=True, stop=True).then_inc(l1_prod, 1)

        def l1_attn_act(act):
            for j in range(J):
                act.wait_ge(l1_prod, l1_p("kv", j))
                nc.scalar.activation(k_feat[j], bank(j, 0)[:, 0:S2], ACT.Copy).then_inc(l1_act, 1)
            act_norm(act, "l1_in", FA)
            for j in range(J):
                act.wait_ge(l1_prod, l1_p("q", j))
                nc.scalar.activation(FB[j][:, :], bank(j, 3), ACT.Copy).then_inc(l1_act, 1)
            att_act(act, "l1", 1.0 / float(P) ** 0.5)
            for j in range(J):
                act.wait_ge(att_pv, att_halves("l1"))
                nc.scalar.activation(FC[j][:, :], psum[:, 6 + j, :], ACT.Copy).then_inc(l1_act, 1)
            for j in range(J):
                act.wait_ge(l1_prod, l1_p("o", j))
                nc.scalar.activation(FA[j][:, :], bank(j, 2), ACT.Identity, bias=col("l1_bo")).then_inc(l1_act, 1)

        def l1_attn_dve(dve, ch):
            dve_norm(dve, ch, "l1_in")
            for j in range(J):
                dve.wait_ge(l1_act, l1_a("k", j))
                dve.wait_ge(att_zeros, 2)
                nc.vector.tensor_copy(head_blocks(j, 8), bank(j, 1)[0:S2, 0:P].rearrange("p (h d) -> p h d", d=8))\
                    .then_inc(att_values, 1)
                ch.tag(nc.vector.tensor_scalar(blocked[j], mask_in[j], 0.0, -1e20, ALU.is_equal, ALU.mult))
                nc.vector.tensor_tensor(k_heads[j].rearrange("p (h s) -> p h s", s=S2),
                                        k_feat[j].unsqueeze(1).to_broadcast([P, 16, S2]),
                                        const("heads8").unsqueeze(2).to_broadcast([P, 16, S2]), ALU.mult)\
                    .then_inc(l1_dve, 1)
            att_dve(dve, ch, "l1")
            for j in range(J):
                dve.wait_ge(l1_act, l1_a("y", j))
                nc.vector.scalar_tensor_tensor(XT[j][:, :], FA[j][:, :], tg_sb[:, 1:2], XT[j][:, :],
                                               ALU.mult, ALU.add).then_inc(x_new, 1)

        def l1_attn_pool(pool):
            pool_norm(pool, "l1_in")
            att_pool(pool, "l1")

        E8 = 8
        l1m_prod = psem("l1m_prod")
        l1m_p = Order("gate", "count", "turn")
        l1m_route = psem("l1m_route")
        l1m_r = Order("chosen", "combine")
        l1m_ct = psem("l1m_ct")
        l1m_front = psem("l1m_front")
        l1m_act = psem("l1m_act")
        l1m_back = psem("l1m_back")
        l1m_early = psem("l1m_early")
        l1m_spread = psem("l1m_spread")
        l1m_sum = psem("l1m_sum")
        e8_units = [(e, j) for e in range(E8) for j in range(J)]
        EARLY = 4
        used[0] = 2 * T
        m1_hid = [take(4 * T) for _ in range(2)]
        m1_w = [take(T) for _ in range(2)]
        m1_part = [take(T) for _ in range(2)]
        m1_out = [take(T) for _ in range(EARLY)]
        before = [sb(f"before{j}", [P, 2, NT + 1, E8]) for j in range(J)]

        def route_bank(j):
            return psum[:, 4 + j, :]

        def l1_moe_pe(pe):
            for j in range(J):
                pe.wait_ge(x_new, x_blk("l1_attn", j))
                pe_norm_in(pe, "l1_moe", j, XT[j][:, :])
            for j in range(J):
                pe_norm_out(pe, "l1_moe", j)
            for j in range(J):
                pe.wait_ge(norm_T, norm("l1_moe", j))
                pe_logits(pe, route_bank(j), FA[j], l1_gate_sb[:, :], E8).then_inc(l1m_prod, 1)

            def counts(j):
                pe.wait_ge(l1m_route, l1m_r("chosen", j))
                nc.tensor.matmul(route_bank(j)[:, 0:64], const("upto"), chosen[j][:, :, :, 0:E8],
                                 start=True, stop=True)
                nc.tensor.matmul(route_bank(j)[:, 64:128], const("ones"), chosen[j][:, :, :, 0:E8],
                                 start=True, stop=True).then_inc(l1m_prod, 1)

            def turn(j):
                pe.wait_ge(l1m_route, l1m_r("combine", j))
                pe_turn_combine(pe, route_bank(j), j, E8).then_inc(l1m_prod, 1)

            def spread(u):
                e, j = e8_units[u]
                return nc.tensor.matmul(psum[:, 4 + u % 2, :], expert_pick(e), combine_t[j][0:3 * E8, :],
                                        start=True, stop=True)

            def front(u):
                e, j = e8_units[u]
                if u >= 1:
                    pe.wait_ge(l1m_act, u)
                for c in range(4):
                    last = nc.tensor.matmul(psum[:, c, :], l1w1_sb[:, e, c * P:(c + 1) * P], FA[j][:, :],
                                            start=True, stop=True)
                if u >= EARLY:
                    if u < EARLY + 2:
                        pe.wait_ge(l1m_sum, u - 1)
                    last = spread(u)
                last.then_inc(l1m_front, 1)

            def back(u):
                e, j = e8_units[u]
                pe.wait_ge(l1m_act, u + 1)
                if u >= EARLY + 2:
                    pe.wait_ge(l1m_sum, u - 1)
                elif u >= 2:
                    pe.wait_ge(l1m_early, u - 1)
                for c in range(4):
                    last = nc.tensor.matmul(psum[:, 6 + u % 2, :], l1w2_sb[:, e, c, :],
                                            m1_hid[u % 2][:, c * T:(c + 1) * T], start=(c == 0), stop=(c == 3))
                last.then_inc(l1m_back, 1)

            for u in range(len(e8_units)):
                front(u)
                if u >= 1:
                    back(u - 1)
                if u == 1:
                    for j in range(J):
                        counts(j)
                elif u == 2:
                    for j in range(J):
                        turn(j)
                    pe.wait_ge(l1m_ct, J)
                    for v in range(2):
                        spread(v).then_inc(l1m_spread, 1)
                elif u == 3:
                    for v in range(2, 4):
                        pe.wait_ge(l1m_sum, v - 1)
                        spread(v).then_inc(l1m_spread, 1)
            back(len(e8_units) - 1)

        def l1_moe_act(act):
            act_norm(act, "l1_moe", FA)
            route_exp(act, "l1")
            for u, (e, j) in enumerate(e8_units):
                act.wait_ge(l1m_front, u + 1)
                if u >= 2:
                    act.wait_ge(l1m_back, u - 1)
                for c in range(4):
                    last = nc.scalar.activation(m1_hid[u % 2][:, c * T:(c + 1) * T], psum[:, c, :], ACT.Relu,
                                                bias=col(f"l1_b1_{e}_{c}"))
                if u >= EARLY:
                    if u >= EARLY + 2:
                        act.wait_ge(l1m_sum, u - 1)
                    last = nc.scalar.activation(m1_w[u % 2], psum[:, 4 + u % 2, :], ACT.Copy)
                last.then_inc(l1m_act, 1)
                if 1 <= u <= EARLY:
                    act.wait_ge(l1m_back, u)
                    nc.scalar.activation(m1_out[u - 1], psum[:, 6 + (u - 1) % 2, :], ACT.Identity,
                                         bias=col(f"l1_b2_{e8_units[u - 1][0]}")).then_inc(l1m_early, 1)
                if u == 2:
                    for i in range(J):
                        act.wait_ge(l1m_prod, l1m_p("turn", i))
                        nc.scalar.activation(combine_t[i][0:3 * E8, :], turned(route_bank(i), E8), ACT.Copy).then_inc(l1m_ct, 1)

        def l1_moe_dve(dve, ch):
            dve_norm(dve, ch, "l1_moe")
            for j in range(J):
                dve.wait_ge(l1m_prod, l1m_p("gate", j))
                route_centre(ch, "l1", j, route_bank(j)[:, 0:NT * E8].rearrange("p (t e) -> p t e", e=E8), E8,
                             rows_sb[:, 16:24])
            for j in range(J):
                route_softmax(dve, ch, "l1", j, E8)
                sc = score[j][:, :, 0:E8]
                ch.link(nc.vector.tensor_copy(sc, logit[j][:, :, 0:E8]))
                first_max(ch, sc, chosen[j][:, 0, :, 0:E8], route_max[j][:, :], const("first8"), E8, NT)
                ch.link(nc.vector.scalar_tensor_tensor(sc, chosen[j][:, 0, :, 0:E8], LOW, sc, ALU.mult, ALU.add))
                first_max(ch, sc, chosen[j][:, 1, :, 0:E8], route_max[j][:, :], const("first8"), E8, NT)
                nc.vector.tensor_copy(combine[j][:, :, 0:E8], logit[j][:, :, 0:E8]).then_inc(l1m_route, 1)
            for j in range(J):
                dve.wait_ge(l1m_prod, l1m_p("count", j))
                totals = route_bank(j)[:, 64:128].rearrange("p (c t e) -> p c t e", c=2, t=NT)
                ch.link(nc.vector.tensor_copy(before[j][:, :, 0, :], carry_sb[:, :].rearrange("p (c e) -> p c e", c=2)))
                for t in range(NT):
                    ch.link(nc.vector.tensor_tensor(before[j][:, :, t + 1, :], totals[:, :, t, :],
                                                    before[j][:, :, t, :], ALU.add))
                ch.tag(nc.vector.tensor_copy(carry_sb[:, :].rearrange("p (c e) -> p c e", c=2), before[j][:, :, NT, :]))
                place = score[j][:, :, :].rearrange("p t (c e) -> p c t e", c=2)
                for c in range(2):
                    ch.tag(nc.vector.tensor_tensor(place[:, c], route_bank(j)[:, c * 32:(c + 1) * 32]
                                                   .rearrange("p (t e) -> p t e", t=NT), before[j][:, c, 0:NT, :],
                                                   ALU.add))
                ch.settle()
                ch.link(nc.vector.tensor_scalar(score[j][:, :, :], score[j][:, :, :], float(CAP), None, ALU.is_le))
                both = chosen[j][:, :, :, 0:E8]
                ch.link(nc.vector.tensor_tensor(both, both, place, ALU.mult))
                ch.link(nc.vector.tensor_tensor(combine[j][:, :, 0:E8], both[:, 0], both[:, 1], ALU.add))
                c = combine[j][:, :, 0:E8]
                ch.link(nc.vector.tensor_tensor(c, c, logit[j][:, :, 0:E8], ALU.mult))
                split(ch, c, parts(E8)[:, tiles(j), :, :]).then_inc(l1m_route, 1)
            for u, (e, j) in enumerate(e8_units):
                if u == 6:
                    context_norm_begin(dve, ch)
                elif u == 8:
                    context_norm_end(dve)
                if u >= 2:
                    dve.wait_ge(l1m_sum, u - 1)
                dst = FB[j][:, :] if e == 0 else m1_part[u % 2]
                if u < EARLY:
                    dve.wait_ge(l1m_early, u + 1)
                    dve.wait_ge(l1m_spread, u + 1)
                    ins = nc.vector.tensor_tensor(dst, psum[:, 4 + u % 2, :], m1_out[u], ALU.mult)
                else:
                    dve.wait_ge(l1m_back, u + 1)
                    ins = nc.vector.scalar_tensor_tensor(dst, psum[:, 6 + u % 2, :], col(f"l1_b2_{e}"), m1_w[u % 2],
                                                         ALU.add, ALU.mult)
                if e > 0:
                    ch.link(ins)
                    ins = nc.vector.tensor_tensor(FB[j][:, :], FB[j][:, :], m1_part[u % 2], ALU.add)
                ins.then_inc(l1m_sum, 1)
            for j in range(J):
                dve.wait_ge(l1m_sum, len(e8_units))
                nc.vector.scalar_tensor_tensor(XT[j][:, :], FB[j][:, :], tg_sb[:, 5:6], XT[j][:, :],
                                               ALU.mult, ALU.add).then_inc(x_new, 1)

        def l1_moe_pool(pool):
            pool_norm(pool, "l1_moe")
            for j in range(J):
                pool.wait_ge(cn_var, j + 1)
                nc.gpsimd.tensor_tensor(ctx_rstd[j][:, :], ctx_var[j][:, :], half_sb[0:S2, 0:1], ALU.pow)\
                    .then_inc(cn_rstd, 1)

        L2H, KC = 8, 5
        HD = 64
        used[0] = 0
        v_wide = take(KC * L2H * P).rearrange("p (k h n) -> p k h n", k=KC, h=L2H)
        k_t = take(4 * (T + S2)).rearrange("p (c n) -> p c n", c=4)
        k_sq = [take(T) for _ in range(2)]
        q_tok = take(4 * T).rearrange("p (t n) -> p t n", t=NT)
        o_t = q_tok
        q_t = take(4 * T).rearrange("p (c n) -> p c n", c=4)
        p_t = [take(T) for _ in range(3)]
        q_sq = p_t[0:2]
        recip = take(T)
        k_sq_ctx = recip[:, 0:4 * S2]
        kv_ctx = [sb(f"kv_ctx{j}", [P, S2]) for j in range(J)]
        table_sb = sb("table_sb", [P, 1])
        q_len = sb("q_len", [P, NT, L2H])
        q_inv = sb("q_inv", [P, NT, L2H])
        k_inv = sb("k_inv", [P, KC, L2H])
        qk_scale = sb("qk_scale", [P, 1])
        qk_most = sb("qk_most", [P, 1])
        shift = sb("shift", [P, 1])
        shift_ctx = [sb(f"shift_ctx{j}", [S2, 1]) for j in range(J)]
        ctx_stats = [sb(f"ctx_stats{j}", [S2, 6]) for j in range(J)]
        ctx_mv = [sb(f"ctx_mv{j}", [S2, 2]) for j in range(J)]
        ctx_var = [sb(f"ctx_var{j}", [S2, 1]) for j in range(J)]
        ctx_rstd = [sb(f"ctx_rstd{j}", [S2, 1]) for j in range(J)]
        cn_var = psem("cn_var")
        cn_rstd = psem("cn_rstd")
        cn_xn = psem("cn_xn")
        cn_out = psem("cn_out")
        cn_T = psem("cn_T")
        l2_ones = psem("l2_ones")
        l2_q = psem("l2_q")
        l2_qsq = psem("l2_qsq")
        l2_qred = psem("l2_qred")
        l2_qroot = psem("l2_qroot")
        l2_qn = psem("l2_qn")
        l2_qturn = psem("l2_qturn")
        l2_qt = psem("l2_qt")
        l2_k = psem("l2_k")
        l2_kact = psem("l2_kact")
        l2_kc = psem("l2_kc")
        l2_kcact = psem("l2_kcact")
        l2_klen = psem("l2_klen")
        l2_kroot = psem("l2_kroot")
        l2_kscale = psem("l2_kscale")
        l2_v = psem("l2_v")
        l2_vw = psem("l2_vw")
        l2_s = psem("l2_s")
        l2_e = psem("l2_e")
        l2_o = psem("l2_o")
        l2_on = psem("l2_on")
        l2_y = psem("l2_y")
        l2_yT = psem("l2_yT")
        NU = L2H * KC
        V_BANKS = [6, 7, 4, 5, 4]

        def key_rows(kc):
            return P if kc < 4 else S2

        def key_cols(kc):
            return slice(kc * P, kc * P + key_rows(kc))

        def blk4(name):
            i = BLOCKS.index(name)
            return blocks_sb[:, i:i + 4, :].rearrange("p c n -> p (c n)")

        def l2_attn_pe(pe):
            for j in range(J):
                pe.wait_ge(x_new, x_blk("l1_moe", j))
                pe_norm_in(pe, "l2_in", j, XT[j][:, :])
            for j in range(J):
                pe.wait_ge(cn_xn, j + 1)
                nc.tensor.transpose(bank(j, 1)[:, 0:S2], ctx_tok[j][:, :], ident[0:S2, 0:S2]).then_inc(cn_out, 1)
            for j in range(J):
                pe_norm_out(pe, "l2_in", j)
            for j in range(J):
                pe.wait_ge(norm_T, norm("l2_in", j))
                pe_norm_in(pe, "l2_lat", j, FA[j][:, :])
            for j in range(J):
                pe_norm_out(pe, "l2_lat", j)
            def queries(j):
                for t in range(NT):
                    nc.tensor.matmul(psum[:, t, :], FB[j][:, t * P:(t + 1) * P], blk4("l2_q0"),
                                     start=True, stop=True).then_inc(l2_q, 1)

            def project(j, c):
                pe.wait_ge(l2_on, L2H * j + 2 * c + 2)
                return nc.tensor.matmul(psum[:, 6, :], blk(f"l2_o{c}"), o_t[:, c, :], start=(c == 0), stop=(c == 3))

            pe.wait_ge(norm_T, norm("l2_lat", J - 1))
            pe.wait_ge(cn_T, J)
            queries(0)
            for j in range(J):
                if j:
                    pe.wait_ge(l2_yT, j)
                def lengths(c):
                    pe.wait_ge(l2_kact, 4 * j + c + 1)
                    for kc in range(KC):
                        sq = k_sq[c % 2][:, key_cols(kc)] if kc < 4 else k_sq_ctx[:, c * S2:(c + 1) * S2]
                        last = nc.tensor.matmul(psum[0:key_rows(kc), 7, kc * 8 + 2 * c:kc * 8 + 2 * c + 2], sq,
                                                const("halves"), start=True, stop=True)
                    last.then_inc(l2_klen, 1)

                def values(kc, bank_):
                    lhs = FB[j][:, key_cols(kc)] if kc < 4 else kv_ctx[j][:, :]
                    nc.tensor.matmul(psum[0:key_rows(kc), bank_, :], lhs, blk4("l2_v0"),
                                     start=True, stop=True).then_inc(l2_v, 1)

                values(0, V_BANKS[0])
                values(1, V_BANKS[1])
                for c in range(4):
                    if c >= 2:
                        pe.wait_ge(l2_kact, 4 * j + c - 1)
                    nc.tensor.matmul(psum[:, 4 + c % 2, :], blk(f"l2_k{c}"), FB[j][:, :], start=True, stop=True)\
                        .then_inc(l2_k, 1)
                    if c == 0:
                        pe.wait_ge(l2_vw, KC * j + 2)
                        for d in range(4):
                            last = nc.tensor.matmul(psum[:, 6, d * S2:(d + 1) * S2], blk(f"l2_k{d}"), kv_ctx[j][:, :],
                                                    start=True, stop=True)
                        last.then_inc(l2_kc, 1)
                    if c == 1:
                        pe.wait_ge(l2_kcact, j + 1)
                    if c >= 1:
                        lengths(c - 1)
                lengths(3)
                pe.wait_ge(l2_qn, NT * (j + 1))
                for c in range(4):
                    for t in range(NT):
                        last = nc.tensor.transpose(psum[:, c, t * P:(t + 1) * P], q_tok[:, t, c * P:(c + 1) * P],
                                                   ident)
                    last.then_inc(l2_qturn, 1)

                def scores(n):
                    h, kc = n // KC, n % KC
                    if n < 4:
                        pe.wait_ge(l2_qt, 4 * j + n + 1)
                    else:
                        pe.wait_ge(l2_e, NU * j + n - 3)
                    r = slice(HD * (h % 2), HD * (h % 2) + HD)
                    nc.tensor.matmul(psum[0:key_rows(kc), n % 4, :], k_t[r, h // 2, key_cols(kc)],
                                     q_t[r, h // 2, :], start=True, stop=True).then_inc(l2_s, 1)

                def weighted(n):
                    h, kc = n // KC, n % KC
                    pe.wait_ge(l2_e, NU * j + n + 1)
                    if kc == 0 and h < 2:
                        pe.wait_ge(l2_vw, KC * (j + 1))
                        pe.wait_ge(l2_ones, 1)
                    elif kc == 0:
                        pe.wait_ge(l2_on, L2H * j + h - 1)
                    k = key_rows(kc)
                    nc.tensor.matmul(psum[:, 4 + h % 2, :], v_wide[0:k, kc, h, :], p_t[n % 3][0:k, :],
                                     start=(kc == 0), stop=(kc == KC - 1)).then_inc(l2_o, 1)

                scores(0)
                scores(1)
                for kc in range(2, KC):
                    if kc == 4:
                        pe.wait_ge(l2_vw, KC * j + 3)
                    values(kc, V_BANKS[kc])
                for n in range(2, NU + 2):
                    if n < NU:
                        scores(n)
                    if n >= 2:
                        weighted(n - 2)
                    if n % (2 * KC) == 3 and n >= 4 * KC:
                        project(j, n // (2 * KC) - 2)
                project(j, 2)
                if j + 1 < J:
                    pe.wait_ge(l2_e, NU * (j + 1))
                    queries(j + 1)
                project(j, 3).then_inc(l2_y, 1)
            for j in range(J):
                pe.wait_ge(l2_yT, J)
                pe_norm_in(pe, "l2_out", j, FA[j][:, :])
            for j in range(J):
                pe_norm_out(pe, "l2_out", j)

        def l2_attn_act(act):
            for j in range(J):
                act.wait_ge(cn_out, j + 1)
                nc.scalar.activation(kv_ctx[j][:, :], bank(j, 1)[:, 0:S2], ACT.Identity, bias=col("l2_xb"),
                                     scale=col("l2_xg")).then_inc(cn_T, 1)
            act_norm(act, "l2_in", FA)
            act_norm(act, "l2_lat", FB, "l2_lg", "l2_lb")
            def squares(j):
                for t in range(NT):
                    act.wait_ge(l2_q, NT * j + t + 1)
                    if t >= 2:
                        act.wait_ge(l2_qred, NT * j + t - 1)
                    nc.scalar.activation(q_sq[t % 2], psum[:, t, :], ACT.Square).then_inc(l2_qsq, 1)

            squares(0)
            for j in range(J):
                for c in range(4):
                    if c == 1:
                        act.wait_ge(l2_qred, NT * (j + 1))
                        nc.scalar.activation(q_inv[:, :, :], q_len[:, :, :], ACT.Sqrt).then_inc(l2_qroot, 1)
                    act.wait_ge(l2_k, 4 * j + c + 1)
                    if c >= 2:
                        act.wait_ge(l2_klen, 4 * j + c - 1)
                    nc.scalar.activation(k_t[:, c, 0:T], psum[:, 4 + c % 2, :], ACT.Identity, scale=qk_scale[:, :])
                    nc.scalar.activation(k_sq[c % 2], psum[:, 4 + c % 2, :], ACT.Square).then_inc(l2_kact, 1)
                    if c == 0:
                        act.wait_ge(l2_kc, j + 1)
                        nc.scalar.activation(k_t[:, :, T:T + S2], psum[:, 6, 0:4 * S2].rearrange("p (c s) -> p c s", s=S2),
                                             ACT.Identity, scale=qk_scale[:, :])
                        nc.scalar.activation(k_sq_ctx, psum[:, 6, 0:4 * S2], ACT.Square).then_inc(l2_kcact, 1)
                act.wait_ge(l2_klen, 4 * (j + 1))
                nc.scalar.activation(k_inv[:, 0:4, :], psum[:, 7, 0:32].rearrange("p (k h) -> p k h", h=8), ACT.Sqrt,
                                     scale=1.0 / 64.0)
                nc.scalar.activation(k_inv[0:S2, 4, :], psum[0:S2, 7, 32:40], ACT.Sqrt, scale=1.0 / 64.0)\
                    .then_inc(l2_kroot, 1)
                nc.scalar.activation(table_sb[:, :], shift[:, :], ACT.Exp)
                act.wait_ge(l2_kscale, j + 1)
                for n in range(NU):
                    h, kc = n // KC, n % KC
                    k = key_rows(kc)
                    act.wait_ge(l2_s, NU * j + n + 1)
                    if n >= 3:
                        act.wait_ge(l2_o, NU * j + n - 2)
                    elif n < 2:
                        act.wait_ge(l2_qred, NT * (j + 1))
                    nc.scalar.activation(p_t[n % 3][0:k, :], psum[0:k, n % 4, :], ACT.Exp,
                                         bias=shift[:, :] if kc < 4 else shift_ctx[j][:, :],
                                         scale=k_inv[0:k, kc, h:h + 1]).then_inc(l2_e, 1)
                if j + 1 < J:
                    act.wait_ge(l2_o, NU * (j + 1))
                    squares(j + 1)
                act.wait_ge(l2_y, j + 1)
                nc.scalar.activation(FA[j][:, :], psum[:, 6, :], ACT.Copy).then_inc(l2_yT, 1)
            act_norm(act, "l2_out", FB, "l2_og", "l2_ob")

        def context_norm_begin(dve, ch):
            for j in range(J):
                ch.link(nc.vector.bn_stats(ctx_stats[j][:, :], ctx_tok[j][:, :]))
                ch.link(nc.vector.bn_aggr(ctx_mv[j][:, :], ctx_stats[j][:, :]))
                ch.tag(nc.vector.tensor_scalar(shift_ctx[j][:, :], key_ok[j][:, :], 0.0, LOW, ALU.is_equal, ALU.mult))
                nc.vector.tensor_scalar(ctx_var[j][:, :], ctx_mv[j][:, 1:2], EPS, None, ALU.add).then_inc(cn_var, 1)
                ch.settle()
                ch.tag(nc.vector.tensor_tensor(shift_ctx[j][:, :], shift_ctx[j][:, :], shift[0:S2, :], ALU.add))

        def context_norm_end(dve):
            for j in range(J):
                dve.wait_ge(cn_rstd, j + 1)
                nc.vector.tensor_scalar(ctx_tok[j][:, :], ctx_tok[j][:, :], ctx_mv[j][:, 0:1], ctx_rstd[j][:, :],
                                        ALU.subtract, ALU.mult).then_inc(cn_xn, 1)

        def l2_attn_dve(dve, ch):
            dve_norm(dve, ch, "l2_in")
            dve_norm(dve, ch, "l2_lat")
            for j in range(J):
                for t in range(NT):
                    dve.wait_ge(l2_qsq, NT * j + t + 1)
                    nc.vector.tensor_reduce(q_len[:, t, :], q_sq[t % 2].rearrange("p (h d) -> p h d", d=HD),
                                            AX.X, ALU.add).then_inc(l2_qred, 1)

                def move_values(kc):
                    k = key_rows(kc)
                    dve.wait_ge(l2_v, KC * j + kc + 1)
                    v = psum[0:k, V_BANKS[kc], :].rearrange("p (h two d) -> p h two d", two=2, d=HD)
                    dst = v_wide[0:k, kc, :, :].rearrange("p (h two) n -> p h two n", two=2)
                    ch.tag(nc.vector.tensor_copy(dst[:, :, 0, 0:HD], v[:, :, 0, :]))
                    nc.vector.tensor_copy(dst[:, :, 1, HD:P], v[:, :, 1, :]).then_inc(l2_vw, 1)

                if j:
                    dve.wait_ge(l2_y, j)
                move_values(0)
                move_values(1)
                dve.wait_ge(l2_qroot, j + 1)
                ch.link(nc.vector.tensor_scalar(q_inv[:, :, :], q_inv[:, :, :], 1e-12, None, ALU.max))
                ch.link(nc.vector.reciprocal(q_inv[:, :, :], q_inv[:, :, :]))
                for t in range(NT):
                    nc.vector.tensor_tensor(q_tok[:, t, :].rearrange("p (h d) -> p h d", d=HD),
                                            psum[:, t, :].rearrange("p (h d) -> p h d", d=HD),
                                            q_inv[:, t, :].unsqueeze(2).to_broadcast([P, L2H, HD]),
                                            ALU.mult).then_inc(l2_qn, 1)
                dve.wait_ge(l2_kroot, j + 1)
                ch.tag(nc.vector.tensor_scalar(k_inv[:, 0:4, :], k_inv[:, 0:4, :], 1e-12 / 8.0, None, ALU.max))
                ch.link(nc.vector.tensor_scalar(k_inv[0:S2, 4, :], k_inv[0:S2, 4, :], 1e-12 / 8.0, None, ALU.max))
                ch.tag(nc.vector.reciprocal(k_inv[:, 0:4, :], k_inv[:, 0:4, :]))
                nc.vector.reciprocal(k_inv[0:S2, 4, :], k_inv[0:S2, 4, :]).then_inc(l2_kscale, 1)
                for c in range(4):
                    dve.wait_ge(l2_qturn, 4 * j + c + 1)
                    nc.vector.tensor_copy(q_t[:, c, :], psum[:, c, :]).then_inc(l2_qt, 1)
                move_values(2)
                move_values(3)
                move_values(4)
                for h in range(L2H):
                    dve.wait_ge(l2_o, NU * j + KC * (h + 1))
                    o = slice(HD * (h % 2), HD * (h % 2) + HD)
                    s = slice(HD - HD * (h % 2), P - HD * (h % 2))
                    ch.link(nc.vector.reciprocal(recip[o, :], psum[s, 4 + h % 2, :]))
                    nc.vector.tensor_tensor(o_t[o, h // 2, :], psum[o, 4 + h % 2, :], recip[o, :], ALU.mult)\
                        .then_inc(l2_on, 1)
            dve_norm(dve, ch, "l2_out")
            for j in range(J):
                dve.wait_ge(norm_T, norm("l2_out", j))
                nc.vector.scalar_tensor_tensor(XT[j][:, :], FB[j][:, :], tg_sb[:, 2:3], XT[j][:, :],
                                               ALU.mult, ALU.add).then_inc(x_new, 1)

        def l2_attn_pool(pool):
            pool_norm(pool, "l2_in")
            pool.wait_ge(x_new, x_blk("l1_moe", J - 1))
            ones = v_wide.rearrange("p k (h two) n -> p (k h) (two n)", two=2)[:, :, HD:HD + P]
            nc.gpsimd.memset(ones, 1.0).then_inc(l2_ones, 1)
            pool_norm(pool, "l2_lat")
            pool_norm(pool, "l2_out")

        HC = 3
        l2m_prod = psem("l2m_prod")
        l2m_p = Order("gate", "turn")
        l2m_route = psem("l2m_route")
        l2m_ct = psem("l2m_ct")
        l2m_w = psem("l2m_w")
        l2m_x = psem("l2m_x")
        l2m_front = psem("l2m_front")
        l2m_silu = psem("l2m_silu")
        l2m_hid = psem("l2m_hid")
        l2m_back = psem("l2m_back")
        used[0] = 2 * T
        m2_x = [take(T) for _ in range(2)]
        m2_silu = [take(T) for _ in range(2)]
        m2_hid = [take(T) for _ in range(2)]

        def hid_rows(c):
            return min(P, HID - c * P)

        def l2_moe_pe(pe):
            for j in range(J):
                pe.wait_ge(x_new, x_blk("l2_attn", j))
                pe_norm_in(pe, "l2_moe", j, XT[j][:, :])
            for j in range(J):
                pe_norm_out(pe, "l2_moe", j)
            for j in range(J):
                pe.wait_ge(norm_T, norm("l2_moe", j))
                pe_logits(pe, bank(j, 0), FA[j], l2_gate_sb[:, :], E8).then_inc(l2m_prod, 1)
            pe_keep_warm(psum[:, 3, :], 28)
            for j in range(J):
                pe.wait_ge(l2m_route, j + 1)
                pe_turn_combine(pe, bank(j, 1), j, E8).then_inc(l2m_prod, 1)

            def spread(u):
                e, j = e8_units[u]
                if u < 2:
                    pe.wait_ge(l2m_ct, J)
                else:
                    pe.wait_ge(l2m_x, u - 1)
                nc.tensor.matmul(psum[:, 4 + u % 2, :], expert_pick(e), combine_t[j][0:3 * E8, :],
                                 start=True, stop=True).then_inc(l2m_w, 1)

            def front(n):
                u, c = n // HC, n % HC
                e, j = e8_units[u]
                m = hid_rows(c)
                if c == 0:
                    pe.wait_ge(l2m_x, u + 1)
                if n >= 2:
                    pe.wait_ge(l2m_hid, n - 1)
                at = slice(c * P, c * P + m)
                b = 2 * (n % 2)
                nc.tensor.matmul(psum[0:m, b, :], l2w1_sb[:, e, at], m2_x[u % 2], start=True, stop=True)
                nc.tensor.matmul(psum[0:m, b + 1, :], l2w3_sb[:, e, at], m2_x[u % 2], start=True, stop=True)\
                    .then_inc(l2m_front, 1)

            def back(n):
                u, c = n // HC, n % HC
                e, j = e8_units[u]
                m = hid_rows(c)
                pe.wait_ge(l2m_hid, n + 1)
                nc.tensor.matmul(psum[:, 6 + j, :], l2w2_sb[0:m, e, c, :], m2_hid[n % 2][0:m, :],
                                 start=(e == 0 and c == 0), stop=(e == E8 - 1 and c == HC - 1)).then_inc(l2m_back, 1)

            units = len(e8_units)
            spread(0)
            for n in range(units * HC):
                front(n)
                if n % HC == 1 and n // HC + 1 < units:
                    spread(n // HC + 1)
                if n >= 1:
                    back(n - 1)
            back(units * HC - 1)

        def l2_moe_act(act):
            act_norm(act, "l2_moe", FA)
            route_exp(act, "l2")
            for j in range(J):
                act.wait_ge(l2m_prod, l2m_p("turn", j))
                nc.scalar.activation(combine_t[j][0:3 * E8, :], turned(bank(j, 1), E8), ACT.Copy).then_inc(l2m_ct, 1)
            for n in range(len(e8_units) * HC):
                m = hid_rows(n % HC)
                act.wait_ge(l2m_front, n + 1)
                if n >= 2:
                    act.wait_ge(l2m_hid, n - 1)
                nc.scalar.activation(m2_silu[n % 2][0:m, :], psum[0:m, 2 * (n % 2), :], ACT.Silu).then_inc(l2m_silu, 1)

        def l2_moe_dve(dve, ch):
            dve_norm(dve, ch, "l2_moe")
            dve.wait_ge(l2m_prod, l2m_p("gate", J - 1))
            route_centre_both(ch, "l2", 0, E8)
            route_softmax(dve, ch, "l2", None, E8)
            sc = both_score[:, :, 0:E8]
            ch.link(nc.vector.tensor_tensor(sc, both_logit[:, :, 0:E8],
                                            rows_sb[:, 24:32].unsqueeze(1).to_broadcast([P, JT, E8]), ALU.add))
            choose_two(ch, sc, E8, const("first8"))
            combine_two(ch, E8).then_inc(l2m_route, J)
            units = len(e8_units)

            def scale_input(u):
                e, j = e8_units[u]
                dve.wait_ge(l2m_w, u + 1)
                if u >= 2:
                    dve.wait_ge(l2m_front, HC * (u - 1))
                nc.vector.tensor_tensor(m2_x[u % 2], psum[:, 4 + u % 2, :], FA[j][:, :], ALU.mult).then_inc(l2m_x, 1)

            scale_input(0)
            for n in range(units * HC):
                m = hid_rows(n % HC)
                if n % HC == 1 and n // HC + 1 < units:
                    scale_input(n // HC + 1)
                dve.wait_ge(l2m_silu, n + 1)
                if n >= 2:
                    dve.wait_ge(l2m_back, n - 1)
                nc.vector.tensor_tensor(m2_hid[n % 2][0:m, :], psum[0:m, 2 * (n % 2) + 1, :], m2_silu[n % 2][0:m, :],
                                        ALU.mult).then_inc(l2m_hid, 1)
            for j in range(J):
                dve.wait_ge(l2m_back, units * HC)
                nc.vector.scalar_tensor_tensor(XT[j][:, :], psum[:, 6 + j, :], tg_sb[:, 6:7], XT[j][:, :],
                                               ALU.mult, ALU.add).then_inc(x_new, 1)

        def l2_moe_pool(pool):
            pool_norm(pool, "l2_moe")

        INV_SQRT8 = 1.0 / 8.0 ** 0.5
        l3_prod = psem("l3_prod")
        l3_p = Order("kv2", "qk", "row", "v", "q2", "s2", "turn2", "z2", "f1", "f2")
        l3_act = psem("l3_act")
        l3_a = Order("kv2", "qk", "v", "q2", "exp2", "turn2", "f1")
        l3_dve = psem("l3_dve")
        l3_d = Order("pad", "r1", "e2", "w2", "r2", "r3")
        s3_score = psem("s3_score")
        s3_max = psem("s3_max")
        s3_exp = psem("s3_exp")
        s3_norm = psem("s3_norm")
        s3_turn = psem("s3_turn")
        s3_move = psem("s3_move")
        s3_z = psem("s3_z")
        s3_units = [(j, t) for j in range(J) for t in range(NT)]
        used[0] = 0
        v1 = [take(NT * P).rearrange("p (t n) -> p t n", t=NT) for _ in range(J)]
        pad = [take(T) for _ in range(J)]
        s3_e = [take(T) for _ in range(3)]
        s3_p = [take(T) for _ in range(2)]
        s3_m = [take(1) for _ in range(3)]
        s3_sum = [take(1) for _ in range(3)]
        count = [take(1) for _ in range(J)]
        k2 = [take(S2) for _ in range(J)]
        v2 = [take(P, S2) for _ in range(J)]
        e2 = [take(NT * S2).rearrange("p (t s) -> p t s", t=NT) for _ in range(J)]
        p2 = [take(T, S2) for _ in range(J)]
        max2 = [take(NT) for _ in range(J)]

        def l3_attn_pe(pe):
            for j in range(J):
                pe.wait_ge(x_new, x_blk("l2_moe", j))
                pe_norm_in(pe, "l3_in", j, XT[j][:, :])
            for j in range(J):
                nc.tensor.matmul(bank(j, 0)[:, 0:S2], blk("l3_k2"), ctxT[j][:, :], start=True, stop=True)
                nc.tensor.matmul(bank(j, 0)[0:S2, P:2 * P], ctxT[j][:, :], blk("l3_v2"), start=True, stop=True)\
                    .then_inc(l3_prod, 1)
            for j in range(J):
                pe_norm_out(pe, "l3_in", j)
            for j in range(J):
                pe.wait_ge(norm_T, norm("l3_in", j))
                pe.wait_ge(l3_act, l3_a("kv2", j))
                nc.tensor.matmul(bank(j, 0), blk("l3_q1"), FA[j][:, :], start=True, stop=True)
                nc.tensor.matmul(bank(j, 1), blk("l3_k1"), FA[j][:, :], start=True, stop=True).then_inc(l3_prod, 1)
            for j in range(J):
                pe.wait_ge(l3_act, l3_a("qk", j))
                nc.tensor.matmul(bank(j, 2), FB[j][:, 0:1].to_broadcast([P, P]), FC[j][:, :],
                                 start=True, stop=True).then_inc(l3_prod, 1)
            for j in range(J):
                for t in range(NT):
                    last = nc.tensor.matmul(bank(j, 3)[:, t * P:(t + 1) * P], FA[j][:, t * P:(t + 1) * P],
                                            blk("l3_v1"), start=True, stop=True)
                last.then_inc(l3_prod, 1)

            def scores(u):
                j, t = s3_units[u]
                if u >= 2:
                    pe.wait_ge(s3_max, u - 1)
                k = (t + 1) * P
                nc.tensor.matmul(psum[:, u % 2, 0:k], FB[j][:, t * P:k], FC[j][:, 0:k], start=True, stop=True)\
                    .then_inc(s3_score, 1)

            def outputs_of(u):
                j, t = s3_units[u]
                pe.wait_ge(s3_move, u + 1)
                for s in range(t + 1):
                    last = nc.tensor.matmul(psum[:, 4 + j, t * P:(t + 1) * P], v1[j][:, s, :],
                                            s3_p[u % 2][:, s * P:(s + 1) * P], start=(s == 0), stop=(s == t))
                last.then_inc(s3_z, 1)

            pe.wait_ge(l3_dve, l3_d("pad", J - 1))
            scores(0)
            scores(1)
            for u, (j, t) in enumerate(s3_units):
                if u + 2 < len(s3_units):
                    scores(u + 2)
                pe.wait_ge(s3_norm, u + 1)
                if u >= 2:
                    pe.wait_ge(s3_move, u - 1)
                elif u == 1:
                    pe.wait_ge(l3_act, l3_a("v", J - 1))
                for s in range(t + 1):
                    last = nc.tensor.transpose(psum[:, 2 + u % 2, s * P:(s + 1) * P], s3_e[u % 3][:, s * P:(s + 1) * P],
                                               ident)
                last.then_inc(s3_turn, 1)
                if u >= 1:
                    outputs_of(u - 1)
            outputs_of(len(s3_units) - 1)
            for j in range(J):
                pe.wait_ge(l3_dve, l3_d("r1", j))
                if j == 0:
                    pe.wait_ge(s3_move, len(s3_units))
                pe_norm_in(pe, "l3_1", j, FB[j][:, :])
            for j in range(J):
                pe_norm_out(pe, "l3_1", j)
            for j in range(J):
                pe.wait_ge(norm_T, norm("l3_1", j))
                nc.tensor.matmul(bank(j, 0), blk("l3_q2"), FA[j][:, :], start=True, stop=True).then_inc(l3_prod, 1)
            for j in range(J):
                pe.wait_ge(l3_act, l3_a("q2", j))
                nc.tensor.matmul(bank(j, 2)[:, 0:S2], FB[j][:, 0:1].to_broadcast([P, P]), k2[j],
                                 start=True, stop=True)
                for t in range(NT):
                    last = nc.tensor.matmul(bank(j, 3)[:, t * S2:(t + 1) * S2], FB[j][:, t * P:(t + 1) * P], k2[j],
                                            start=True, stop=True)
                last.then_inc(l3_prod, 1)
            for j in range(J):
                pe.wait_ge(l3_dve, l3_d("w2", j))
                for t in range(NT):
                    last = nc.tensor.transpose(bank(j, 0)[0:S2, t * P:(t + 1) * P], e2[j][:, t, :], ident)
                last.then_inc(l3_prod, 1)
            for j in range(J):
                pe.wait_ge(l3_act, l3_a("turn2", j))
                nc.tensor.matmul(bank(j, 1), v2[j], p2[j], start=True, stop=True).then_inc(l3_prod, 1)
            for j in range(J):
                pe.wait_ge(l3_dve, l3_d("r2", j))
                pe_norm_in(pe, "l3_2", j, FB[j][:, :])
            for j in range(J):
                pe_norm_out(pe, "l3_2", j)
            for j in range(J):
                pe.wait_ge(norm_T, norm("l3_2", j))
                nc.tensor.matmul(bank(j, 0), blk("l3_f1"), FA[j][:, :], start=True, stop=True).then_inc(l3_prod, 1)
            for j in range(J):
                pe.wait_ge(l3_act, l3_a("f1", j))
                nc.tensor.matmul(bank(j, 1), blk("l3_f2"), FC[j][:, :], start=True, stop=True).then_inc(l3_prod, 1)
            for j in range(J):
                pe.wait_ge(l3_dve, l3_d("r3", j))
                pe_norm_in(pe, "l3_3", j, FB[j][:, :])
            for j in range(J):
                pe_norm_out(pe, "l3_3", j)

        def l3_attn_act(act):
            for j in range(J):
                act.wait_ge(l3_prod, l3_p("kv2", j))
                nc.scalar.activation(k2[j], bank(j, 0)[:, 0:S2], ACT.Copy)
                nc.scalar.activation(v2[j], bank(j, 0)[0:S2, P:2 * P], ACT.Copy).then_inc(l3_act, 1)
            act_norm(act, "l3_in", FA)
            for j in range(J):
                act.wait_ge(l3_prod, l3_p("qk", j))
                nc.scalar.activation(FB[j][:, :], bank(j, 0), ACT.Copy)
                nc.scalar.activation(FC[j][:, :], bank(j, 1), ACT.Copy).then_inc(l3_act, 1)
            for j in range(J):
                act.wait_ge(l3_prod, l3_p("v", j))
                nc.scalar.activation(v1[j].rearrange("p t n -> p (t n)"), bank(j, 3), ACT.Copy).then_inc(l3_act, 1)

            for u, (j, t) in enumerate(s3_units):
                k = (t + 1) * P
                act.wait_ge(s3_max, u + 1)
                nc.scalar.activation(s3_e[u % 3][:, 0:k], s3_e[u % 3][:, 0:k], ACT.Exp, bias=s3_m[u % 3],
                                     scale=INV_SQRT8, accum_out=s3_sum[u % 3]).then_inc(s3_exp, 1)
                if u >= 1:
                    move3(act, u - 1)
            move3(act, len(s3_units) - 1)
            act_norm(act, "l3_1", FA, "l3_n1g", "l3_n1b")
            for j in range(J):
                act.wait_ge(l3_prod, l3_p("q2", j))
                nc.scalar.activation(FB[j][:, :], bank(j, 0), ACT.Copy).then_inc(l3_act, 1)
            for j in range(J):
                act.wait_ge(l3_dve, l3_d("e2", j))
                nc.scalar.activation(e2[j], e2[j], ACT.Exp, scale=INV_SQRT8).then_inc(l3_act, 1)
            for j in range(J):
                act.wait_ge(l3_prod, l3_p("turn2", j))
                nc.scalar.activation(p2[j], bank(j, 0)[0:S2, :], ACT.Copy).then_inc(l3_act, 1)
            act_norm(act, "l3_2", FA, "l3_n2g", "l3_n2b")
            for j in range(J):
                act.wait_ge(l3_prod, l3_p("f1", j))
                nc.scalar.activation(FC[j][:, :], bank(j, 0), ACT.Relu, bias=col("l3_b1")).then_inc(l3_act, 1)
            act_norm(act, "l3_3", FA, "l3_n3g", "l3_n3b")

        def move3(act, u):
            j, t = s3_units[u]
            act.wait_ge(s3_turn, u + 1)
            if u >= 2:
                act.wait_ge(s3_z, u - 1)
            nc.scalar.activation(s3_p[u % 2][:, 0:(t + 1) * P], psum[:, 2 + u % 2, 0:(t + 1) * P], ACT.Copy)\
                .then_inc(s3_move, 1)

        def l3_attn_dve(dve, ch):
            def key_pad(j, row, n, dst):
                ch.link(nc.vector.tensor_scalar(dst, row, 0.0, None, ALU.not_equal))
                ch.link(nc.vector.tensor_reduce(count[j], dst, AX.X, ALU.add))
                return nc.vector.tensor_scalar(dst, const("keys")[:, 0:n], count[j], LOW, ALU.is_ge, ALU.mult)

            dve_norm(dve, ch, "l3_in")
            for j in range(J):
                dve.wait_ge(l3_prod, l3_p("row", j))
                key_pad(j, bank(j, 2), T, pad[j]).then_inc(l3_dve, 1)
            dve.wait_ge(l3_dve, l3_d("pad", J - 1))

            def masked(u):
                j, t = s3_units[u]
                k = (t + 1) * P
                e = s3_e[u % 3]
                dve.wait_ge(s3_score, u + 1)
                if u >= 3:
                    dve.wait_ge(s3_turn, u - 2)
                ch.link(nc.vector.tensor_tensor(e[:, 0:k], psum[:, u % 2, 0:k], pad[j][:, 0:k], ALU.add))
                ch.link(nc.vector.tensor_tensor(e[:, t * P:k], e[:, t * P:k], const("causal"), ALU.add))
                ch.link(nc.vector.tensor_reduce(s3_m[u % 3], e[:, 0:k], AX.X, ALU.max))
                nc.vector.tensor_scalar(s3_m[u % 3], s3_m[u % 3], -INV_SQRT8, None, ALU.mult).then_inc(s3_max, 1)

            masked(0)
            for u, (j, t) in enumerate(s3_units):
                if u + 1 < len(s3_units):
                    masked(u + 1)
                dve.wait_ge(s3_exp, u + 1)
                ch.link(nc.vector.reciprocal(s3_sum[u % 3], s3_sum[u % 3]))
                k = (t + 1) * P
                nc.vector.tensor_scalar(s3_e[u % 3][:, 0:k], s3_e[u % 3][:, 0:k], s3_sum[u % 3], None, ALU.mult)\
                    .then_inc(s3_norm, 1)
            for j in range(J):
                dve.wait_ge(s3_z, NT * (j + 1))
                nc.vector.tensor_tensor(FB[j][:, :], psum[:, 4 + j, :], FA[j][:, :], ALU.add).then_inc(l3_dve, 1)
            dve_norm(dve, ch, "l3_1")
            for j in range(J):
                wide = [P, NT, S2]
                dve.wait_ge(l3_prod, l3_p("s2", j))
                ch.link(key_pad(j, bank(j, 2)[:, 0:S2], S2, pad[j][:, 0:S2]))
                ch.link(nc.vector.tensor_tensor(e2[j], bank(j, 3)[:, 0:NT * S2].rearrange("p (t s) -> p t s", t=NT),
                                                pad[j][:, 0:S2].unsqueeze(1).to_broadcast(wide), ALU.add))
                ch.link(nc.vector.tensor_reduce(max2[j], e2[j], AX.X, ALU.max))
                nc.vector.tensor_tensor(e2[j], e2[j], max2[j].unsqueeze(2).to_broadcast(wide), ALU.subtract)\
                    .then_inc(l3_dve, 1)
            for j in range(J):
                dve.wait_ge(l3_act, l3_a("exp2", j))
                ch.link(nc.vector.tensor_reduce(max2[j], e2[j], AX.X, ALU.add))
                ch.link(nc.vector.reciprocal(max2[j], max2[j]))
                nc.vector.tensor_tensor(e2[j], e2[j], max2[j].unsqueeze(2).to_broadcast([P, NT, S2]), ALU.mult)\
                    .then_inc(l3_dve, 1)
            for j in range(J):
                dve.wait_ge(l3_prod, l3_p("z2", j))
                nc.vector.tensor_tensor(FB[j][:, :], bank(j, 1), FA[j][:, :], ALU.add).then_inc(l3_dve, 1)
            dve_norm(dve, ch, "l3_2")
            for j in range(J):
                dve.wait_ge(l3_prod, l3_p("f2", j))
                nc.vector.scalar_tensor_tensor(FB[j][:, :], bank(j, 1), col("l3_b2"), FA[j][:, :],
                                               ALU.add, ALU.add).then_inc(l3_dve, 1)
            dve_norm(dve, ch, "l3_3")
            for j in range(J):
                dve.wait_ge(norm_T, norm("l3_3", j))
                nc.vector.scalar_tensor_tensor(XT[j][:, :], FA[j][:, :], tg_sb[:, 3:4], XT[j][:, :],
                                               ALU.mult, ALU.add).then_inc(x_new, 1)

        def l3_attn_pool(pool):
            for name in ("l3_in", "l3_1", "l3_2", "l3_3"):
                pool_norm(pool, name)

        l3f_prod = psem("l3f_prod")
        l3f_p = Order("up", "down")
        l3f_act = psem("l3f_act")
        l3f_a = Order("up", "y")
        used[0] = 0
        hidden3 = [take(4 * T) for _ in range(J)]

        def l3_ffn_pe(pe):
            for j in range(J):
                pe.wait_ge(x_new, x_blk("l3_attn", j))
                pe_norm_in(pe, "l3_ffn", j, XT[j][:, :])
            for j in range(J):
                pe_norm_out(pe, "l3_ffn", j)
            for j in range(J):
                pe.wait_ge(norm_T, norm("l3_ffn", j))
                for c in range(4):
                    last = nc.tensor.matmul(bank(j, c), blk(f"l3_up{c}"), FA[j][:, :], start=True, stop=True)
                last.then_inc(l3f_prod, 1)
            for j in range(J):
                pe.wait_ge(l3f_act, l3f_a("up", j))
                for c in range(4):
                    last = nc.tensor.matmul(bank(j, 0), blk(f"l3_down{c}"), hidden3[j][:, c * T:(c + 1) * T],
                                            start=(c == 0), stop=(c == 3))
                last.then_inc(l3f_prod, 1)

        def l3_ffn_act(act):
            act_norm(act, "l3_ffn", FA)
            for j in range(J):
                act.wait_ge(l3f_prod, l3f_p("up", j))
                for c in range(4):
                    last = nc.scalar.activation(hidden3[j][:, c * T:(c + 1) * T], bank(j, c), ACT.Gelu,
                                                bias=col(f"l3_bfc{c}"))
                last.then_inc(l3f_act, 1)
            for j in range(J):
                act.wait_ge(l3f_prod, l3f_p("down", j))
                nc.scalar.activation(FB[j][:, :], bank(j, 0), ACT.Identity, bias=col("l3_bproj")).then_inc(l3f_act, 1)

        def l3_ffn_dve(dve, ch):
            dve_norm(dve, ch, "l3_ffn")
            for j in range(J):
                dve.wait_ge(l3f_act, l3f_a("y", j))
                nc.vector.scalar_tensor_tensor(FC[j][:, :], FB[j][:, :], tg_sb[:, 7:8], XT[j][:, :],
                                               ALU.mult, ALU.add).then_inc(x_new, 1)

        def l3_ffn_pool(pool):
            pool_norm(pool, "l3_ffn")

        quant_most = sem("quant_most")
        quant_all = sem("quant_all")
        quant_lora = sem("quant_lora")
        quant = sb("quant", [P, 2, 4])
        ROUND = 1.5 * 2.0 ** 23

        def quant_w(n):
            return blk4(("l3_up0", "l3_down0")[n])

        def quant_pe(pe):
            nc.tensor.matmul(psum[:, 0, :], lora_sb[:, 0, 0:P], lora_sb[:, 1, 0:512], start=True, stop=True)
            for c in range(4):
                last = nc.tensor.matmul(psum[:, 1, c * P:(c + 1) * P], lora_sb[:, 0, P + c * P:2 * P + c * P],
                                        lora_sb[:, 1, 512:512 + P], start=True, stop=True)
            last.then_inc(quant_lora, 1)

        def quant_pool(pool):
            pool.wait_ge(quant_most, 2)
            for n in range(2):
                nc.gpsimd.partition_all_reduce(quant[:, n, 1:2], quant[:, n, 0:1], P, bass.bass_isa.ReduceOp.max)\
                    .then_inc(quant_all, 1)

        def quant_most_dve():
            for n in range(2):
                nc.vector.tensor_reduce(quant[:, n, 0:1], quant_w(n), AX.X, ALU.max, apply_absolute_value=True)\
                    .then_inc(quant_most, 1)

        def quant_dve(dve, ch):
            dve.wait_ge(quant_all, 2)
            both = quant[:, :, 1], quant[:, :, 2], quant[:, :, 3]
            ch.link(nc.vector.tensor_scalar(both[1], both[0], 1.0 / 127.0, None, ALU.mult))
            ch.link(nc.vector.reciprocal(both[2], both[1]))
            r = [arena[:, n * 512:(n + 1) * 512] for n in range(2)]
            w = [quant_w(n) for n in range(2)]
            scale = [quant[:, n, 2:3] for n in range(2)]
            inv = [quant[:, n, 3:4] for n in range(2)]

            def on_both(op):
                for n in range(2):
                    ch.tag(op(n))
                ch.settle()

            on_both(lambda n: nc.vector.tensor_scalar(r[n], w[n], inv[n], ROUND, ALU.mult, ALU.add))
            on_both(lambda n: nc.vector.tensor_scalar(r[n], r[n], ROUND, 127.0, ALU.subtract, ALU.min))
            on_both(lambda n: nc.vector.tensor_scalar(r[n], r[n], -128.0, scale[n], ALU.max, ALU.mult))
            on_both(lambda n: nc.vector.tensor_tensor(r[n], r[n], w[n], ALU.subtract))
            on_both(lambda n: nc.vector.tensor_tensor(w[n], w[n], r[n], ALU.add))
            dve.wait_ge(quant_lora, 1)
            on_both(lambda n: nc.vector.scalar_tensor_tensor(w[n], psum[:, n, :], 2.0, w[n], ALU.mult, ALU.add))
        INPUT_DMAS = 5 * J
        L0_LAST, L3_FIRST = BLOCKS.index("l1_q"), BLOCKS.index("l3_up0")
        FIRST_LOADS = [
            (gates_sb[:, :], gates), (picks_sb[:, :], picks), (cols_sb[:, :], cols), (rows_sb[:, :], rows), (consts_sb[:, :], consts),
            (blocks_sb[:, L3_FIRST:, :], blocks[:, L3_FIRST:, :]),
            (lora_sb[:, 0, 0:P], A_fc), (lora_sb[:, 1, 0:512], B_fc),
            (lora_sb[:, 0, P:P + 512], A_proj), (lora_sb[:, 1, 512:512 + P], B_proj),
            (blocks_sb[:, 0:L0_LAST, :], blocks[:, 0:L0_LAST, :])]
        L0_MOE_LOADS = [
            (gate16_sb[:, :], gate16)] + [
            (be2_sb[k * 16:(k + 1) * 16, :], be2) for k in range(3)] + [
            (we1_sb[:, :, :], We1.rearrange("e d i -> d e i")), (we3_sb[:, :, :], We3.rearrange("e d i -> d e i")),
            (we2_sb[:, :, :], We2.rearrange("(p two) i d -> (two i) p d", two=2))]
        LATER_LOADS = [
            (blocks_sb[:, L0_LAST:L3_FIRST, :], blocks[:, L0_LAST:L3_FIRST, :]),
            (l1_gate_sb[:, :], l1_gate), (l2_gate_sb[:, :], l2_gate),
            (l1w1_sb[:, :, :], W1.rearrange("e d f -> d e f"))] + [
            (l1w2_sb[:, e:e + 4, :, :], W2[e:e + 4].rearrange("e (c p) d -> p e c d", p=P)) for e in (0, 4)] + [
            (l2w1_sb[:, :, :], w1.rearrange("e d f -> d e f")), (l2w3_sb[:, :, :], w3.rearrange("e d f -> d e f"))] + [
            (l2w2_sb[0:hid_rows(c), :, c, :], w2[:, c * P:c * P + hid_rows(c), :].rearrange("e p d -> p e d"))
            for c in range(3)]
        ENGINES = 4

        PE_PARTS = [l0_attn_pe, l0_moe_pe, l1_attn_pe, l1_moe_pe, l2_attn_pe, l2_moe_pe, l3_attn_pe, l3_ffn_pe]
        ACT_PARTS = [l0_attn_act, l0_moe_act, l1_attn_act, l1_moe_act, l2_attn_act, l2_moe_act, l3_attn_act, l3_ffn_act]
        DVE_PARTS = [l0_attn_dve, l0_moe_dve, l1_attn_dve, l1_moe_dve, l2_attn_dve, l2_moe_dve, l3_attn_dve, l3_ffn_dve]
        POOL_PARTS = [l0_attn_pool, l0_moe_pool, l1_attn_pool, l1_moe_pool, l2_attn_pool, l2_moe_pool, l3_attn_pool, l3_ffn_pool]

        block = ctx.enter_context(nc.Block())

        def pass_end(eng, i):
            eng.sem_inc(pass_done, 1)
            eng.wait_ge(cleared, i + 1)

        @block.sync
        def _(sp):
            def load(dst, src):
                sp.dma_start(dst, src).then_inc(loaded, 16)

            for dst, src in FIRST_LOADS:
                load(dst, src)

            def load_ctx(b, j):
                sp.dma_start(ctxT[j][:, :], ctx_t[bass.ds(b, 1)].rearrange("o f t -> (o f) t")).then_inc(inputs, 16)
                sp.dma_start(ctx_tok[j][:, :], ctx_k[bass.ds(b, 1)].rearrange("o s f -> (o s) f")).then_inc(inputs, 16)
                sp.dma_start(key_ok[j][:, :], key_mask[bass.ds(b, 1)].rearrange("o s -> s o")).then_inc(inputs, 16)
                sp.dma_start(mask_in[j].rearrange("p (t s) -> p t s", s=S2),
                             attn_mask[bass.ds(b, 1)].rearrange("a o (t p) s -> p (a o t) s", p=P)).then_inc(inputs, 16)

            def load_x(b, j):
                sp.dma_start(XT[j][:, :], x[bass.ds(b, 1)].rearrange("o f t -> (o f) t")).then_inc(inputs, 16)

            def store(b, j):
                sp.wait_ge(x_new, x_blk("l3_ffn", j))
                sp.dma_start(out[bass.ds(b, 1)].rearrange("o f t -> (o f) t"), FC[j][:, :]).then_inc(outputs, 16)

            for j in range(J):
                load_x(j, j)
                load_ctx(j, j)
            with sp.Fori(0, PASSES - 1) as i:
                sp.wait_ge(x_new, x_blk("l3_attn", J - 1))
                for j in range(J):
                    load_ctx((i + 1) * J + j, j)
                for j in range(J):
                    store(i * J + j, j)
                    load_x((i + 1) * J + j, j)
                sp.wait_ge(outputs, 16 * J * (i + 1))
                sp.wait_ge(pass_done, ENGINES * (i + 1))
                for s in per_pass + [chain_d]:
                    sp.sem_clear(s)
                sp.sem_inc(cleared, 1)
            for j in range(J):
                store((PASSES - 1) * J + j, j)
            sp.wait_ge(outputs, 16 * J * PASSES)
            sp.sem_inc(cleared, 1)


        quant_step = sem("quant_step")

        @block.gpsimd
        def _(pool):
            ch = Chain(pool, setup_pool)
            ch.tag(nc.gpsimd.memset(half_sb[:, :], -0.5))
            ch.tag(nc.gpsimd.memset(carry_sb[:, :], 0.0))
            pool.wait_ge(setup_done, 1)
            ch.tag(nc.gpsimd.partition_all_reduce(qk_most[:, :], qk_scale[:, :], P, bass.bass_isa.ReduceOp.absmax))
            pool.wait_ge(setup_pool, ch.n)
            quant_pool(pool)
            with pool.Fori(0, PASSES) as i:
                for part in POOL_PARTS:
                    part(pool)
                pass_end(pool, i)

        @block.tensor
        def _(pe):
            pe.wait_ge(loaded, 16 * len(FIRST_LOADS))
            quant_pe(pe)
            pe.wait_ge(setup_done, 3)
            with pe.Fori(0, PASSES) as i:
                pe.wait_ge(inputs, 16 * INPUT_DMAS * (i + 1))
                for part in PE_PARTS:
                    part(pe)
                pass_end(pe, i)

        @block.scalar
        def _(act):
            act.wait_ge(loaded, 16 * len(FIRST_LOADS))
            nc.scalar.activation(tg_sb[:, :], gates_sb[:, :], ACT.Tanh).then_inc(setup_act, 1)
            for dst, src in L0_MOE_LOADS:
                nc.scalar.dma_start(dst, src).then_inc(loaded_l0_moe, 16)
            for dst, src in LATER_LOADS:
                nc.scalar.dma_start(dst, src).then_inc(loaded_later, 16)
            with act.Fori(0, PASSES) as i:
                for part in ACT_PARTS:
                    part(act)
                pass_end(act, i)

        @block.vector
        def _(dve):
            ch = Chain(dve, chain_d)
            dve.wait_ge(loaded, 16 * len(FIRST_LOADS))
            quant_most_dve()
            nc.vector.tensor_tensor(qk_scale[:, :], col("l2_qs"), col("l2_ks"), ALU.mult).then_inc(setup_done, 1)
            dve.wait_ge(setup_pool, 3)
            nc.vector.tensor_scalar(shift[:, :], qk_most[:, :], -8.0, None, ALU.mult).then_inc(setup_done, 1)
            dve.wait_ge(setup_done, 2)
            qc = Chain(dve, quant_step)
            quant_dve(dve, qc)
            dve.sem_inc(setup_done, 1)
            dve.wait_ge(setup_act, 1)
            with dve.Fori(0, PASSES) as i:
                for part in DVE_PARTS:
                    part(dve, ch)
                pass_end(dve, i)


def _square(a):
    return [a[:, i * P:(i + 1) * P] for i in range(a.shape[1] // P)]


def _stack_blocks(np, i):
    def per_head(w):
        a = np.zeros((P, P), w.dtype)
        for h in range(16):
            a[8 * h:8 * h + 8, 8 * h:8 * h + 8] = w.T
        return a

    qkv, inp = i["L0_xattn_qkv_w"], i["L0_xattn_in_proj_w"]
    out = [qkv[256:384].T, i["L0_xattn_sa_out_w"].T, inp[0:128].T, inp[128:256].T, inp[256:384].T,
           i["L0_xattn_mha_out_w"].T]
    out += _square(i["L0_xattn_lin1_w"].T)
    out += [i["L0_xattn_lin2_w"].T[c * P:(c + 1) * P] for c in range(4)]
    out += [i["L0_ffn_ws1"], i["L0_ffn_ws3"], i["L0_ffn_ws2"]]
    out += [per_head(i["L1_xattn_Wq"]), per_head(i["L1_xattn_Wk"]), per_head(i["L1_xattn_Wv"]), i["L1_xattn_Wo"].T]
    out += _square(i["L2_xattn_Wq"]) + _square(i["L2_xattn_Wkv"])
    out += [i["L2_xattn_Wo"][c * P:(c + 1) * P] for c in range(4)]
    out += [i[f"L3_xattn_{n}"] for n in ("Wq1", "Wk1", "Wv1", "Wq2", "Wk2", "Wv2", "fc1_w", "fc2_w")]
    out += _square(i["L3_ffn_W_fc"].T)
    out += [i["L3_ffn_W_proj"].T[c * P:(c + 1) * P] for c in range(4)]
    assert len(out) == len(BLOCKS)
    return np.ascontiguousarray(np.stack(out, axis=1))


def _stack_cols(np, i):
    qkv_b, in_b = i["L0_xattn_qkv_b"], i["L0_xattn_in_proj_b"]
    rows = [qkv_b[256:384], i["L0_xattn_sa_out_b"], in_b[0:128], in_b[128:256], in_b[256:384],
            i["L0_xattn_mha_out_b"]]
    rows += list(i["L0_xattn_lin1_b"].reshape(4, P)) + [i["L0_xattn_lin2_b"]]
    rows += [i[f"L0_xattn_ln{n}_{p}"] for n in (1, 2, 3) for p in "gb"]
    rows += list(i["L0_ffn_be1"].reshape(8, P)) + list(i["L0_ffn_be3"].reshape(8, P))
    rows += [i["L0_ffn_bs1"], i["L0_ffn_bs3"], i["L0_ffn_bs2"], i["L1_xattn_bo"]]
    rows += list(i["L1_ffn_b1"].reshape(32, P)) + list(i["L1_ffn_b2"])
    rows += [i[f"L2_xattn_{n}"] for n in ("ln_x_w", "ln_x_b", "ln_l_w", "ln_l_b", "ln_o_w", "ln_o_b")]
    rows += [np.concatenate([i[f"L2_xattn_{n}"]] * 2) for n in ("q_scale", "k_scale")]
    rows += [i["L3_xattn_fc1_b"], i["L3_xattn_fc2_b"]]
    rows += [i[f"L3_xattn_ln{n}_{p}"] for n in (1, 2, 3) for p in "gb"]
    rows += list(i["L3_ffn_b_fc"].reshape(4, P)) + [i["L3_ffn_b_proj"]]
    assert len(rows) == len(COLS)
    return np.ascontiguousarray(np.stack(rows, axis=1))


def _constants(np):
    i = np.arange(P)
    c = {"ident": np.eye(P), "upto": i[:, None] <= i[None, :], "ones": np.ones((P, P)),
         "causal": np.where(i[None, :] > i[:, None], LOW, 0.0),
         "heads16": i[:, None] // 16 == np.arange(8)[None, :], "heads8": i[:, None] // 8 == np.arange(16)[None, :],
         "halves": i[:, None] // 64 == np.arange(2)[None, :],
         "first16": np.broadcast_to(16 - np.arange(16), (P, 16)), "first8": np.broadcast_to(8 - np.arange(8), (P, 8)),
         "first4": np.broadcast_to(4 - np.arange(4), (P, 4)), "keys": np.broadcast_to(np.arange(512), (P, 512))}
    packed = np.concatenate([np.asarray(c[n], np.float32) for n in CONSTS], axis=1)
    picks = np.zeros((P, P + 8 + 8 * P))
    picks[:, 0:P] = np.eye(P)
    picks[0:24, P:P + 8] = np.tile(np.eye(8), (3, 1))
    picks[0:48, P + 8:] = np.tile(np.repeat(np.eye(16), 64, axis=1), (3, 1))
    return np.ascontiguousarray(packed), np.where(picks, 0x3F80, 0).astype(np.uint16)


def kernel(**inputs):
    import numpy as np
    import concourse.bacc as bacc
    from concourse.bass_utils import run_bass_kernel_spmd

    i = {k: np.asarray(v) for k, v in inputs.items()}
    consts, picks = _constants(np)
    laid = {
        "x": i["x"].transpose(0, 2, 1),
        "ctx_t": i["ctx_1024"].transpose(0, 2, 1), "ctx_k": i["ctx_1024"],
        "attn_mask": i["mask_Bx1xSxS2_if1"], "key_mask": i["mask_BxS2_bk0"],
        "gates": np.broadcast_to(np.concatenate([i["g_xattn"], i["g_ffn"]]), (P, 8)),
        "blocks": _stack_blocks(np, i), "cols": _stack_cols(np, i),
        "rows": np.broadcast_to(np.concatenate([i["L0_ffn_gate_b"], i["L1_ffn_gate_b"], i["L2_ffn_expert_bias"]]),
                                (P, 32)),
        "consts": consts, "picks": picks,
        "gate16": i["L0_ffn_gate_w"].T, "be2": i["L0_ffn_be2"], "l1_gate": i["L1_ffn_gate_w"].T,
        "l2_gate": i["L2_ffn_gate_w"].T, "We1": i["L0_ffn_We1"], "We2": i["L0_ffn_We2"], "We3": i["L0_ffn_We3"],
        "W1": i["L1_ffn_W1"], "W2": i["L1_ffn_W2"], "w1": i["L2_ffn_w1"], "w2": i["L2_ffn_w2"], "w3": i["L2_ffn_w3"],
        "A_fc": i["L3_ffn_A_fc"], "B_fc": i["L3_ffn_B_fc"].T, "A_proj": i["L3_ffn_A_proj"],
        "B_proj": i["L3_ffn_B_proj"].T,
    }
    nc = bacc.Bacc("TRN2", target_bir_lowering=False, num_devices=1)
    arrays, args = {}, {}
    for name, a in laid.items():
        a = np.ascontiguousarray(a)
        arrays[f"in_{name}_dram"] = a
        args[name] = nc.dram_tensor(f"in_{name}_dram", a.shape, mybir.dt.from_np(a.dtype), kind="ExternalInput").ap()
    out = nc.dram_tensor("out_0_dram", (B, P, T), F32, kind="ExternalOutput").ap()
    flamingo_kernel(nc, **args, out=out)
    r = run_bass_kernel_spmd(nc, [arrays], core_ids=[0])
    return np.ascontiguousarray(np.asarray(r.results[0]["out_0_dram"]).transpose(0, 2, 1))
```
